# Optimizing a Trainium2 kernel written in Bass

```python
import numpy as np
import jax
import jax.numpy as jnp

def _softmax(x, axis=-1):
    return jax.nn.softmax(x, axis=axis)

def _gelu(x):
    return jax.nn.gelu(x, approximate=True)

def _silu(x):
    return jax.nn.silu(x)

def _sigmoid(x):
    return jax.nn.sigmoid(x)

def _layernorm(x, axis=-1, eps=1e-05):
    m = jnp.mean(x, axis=axis, keepdims=True)
    v = jnp.var(x, axis=axis, keepdims=True)
    return (x - m) / jnp.sqrt(v + eps)

def _scatter_add(tgt, idx, src, axis=0):
    return tgt.at[idx].add(src)

def _segment_sum(src, seg, n):
    return jax.ops.segment_sum(src, seg, n)
kernel_name = 'mk_recurrent_d2_jaxref_r4_abdddd'

def setup_inputs(seed: int=0):
    np.random.seed(seed)
    _w = jnp.asarray

    def _L0_attn_setup():
        import jax, jax.numpy as jnp
        import numpy as np
        B, T, H, NUM_LAYERS = (8, 1024, 256, 2)

        def _log_g(x):
            return jnp.where(x >= 0.0, jnp.log(jax.nn.relu(x) + 0.5), -jax.nn.softplus(-x))

        def _heinsen_scan(log_coeffs, log_values):
            a_star = jnp.cumsum(log_coeffs, axis=1)
            return jnp.exp(a_star + jax.lax.cumlogsumexp(log_values - a_star, axis=1))
        key = jax.random.key(seed)
        k0, k1, k2 = jax.random.split(key, 3)
        scale = 1.0 / np.sqrt(H)
        return {'h': jax.random.normal(k0, (B, T, H), dtype=jnp.float32), 'W0': jax.random.normal(k1, (H, 3 * H), dtype=jnp.float32) * scale, 'W1': jax.random.normal(k2, (H, 3 * H), dtype=jnp.float32) * scale}
    _L0_attn_in = _L0_attn_setup()

    def _L0_ffn_setup():
        import jax, jax.numpy as jnp
        import numpy as np
        B, S, D, F, E = (1, 256, 256, 1024, 8)
        EPS = 1e-05

        def _sublayer(xs, g, b, W1e, b1e, W2e, b2e):
            mu = jnp.mean(xs, axis=-1, keepdims=True)
            var = jnp.mean(jnp.square(xs - mu), axis=-1, keepdims=True)
            h = (xs - mu) * jax.lax.rsqrt(var + EPS) * g + b
            return xs + jax.nn.relu(h @ W1e.T + b1e) @ W2e.T + b2e
        key = jax.random.key(seed)
        ks = jax.random.split(key, 4)
        x = jax.random.normal(ks[0], (B, S, D), jnp.float32)
        centroids = jax.random.normal(ks[1], (E, D), jnp.float32) * 0.1
        gamma = jnp.ones((E, D), jnp.float32)
        beta = jnp.zeros((E, D), jnp.float32)
        W1 = jax.random.normal(ks[2], (E, F, D), jnp.float32) * 0.02
        b1 = jnp.zeros((E, F), jnp.float32)
        W2 = jax.random.normal(ks[3], (E, D, F), jnp.float32) * 0.02
        b2 = jnp.zeros((E, D), jnp.float32)
        return {'x': x, 'centroids': centroids, 'gamma': gamma, 'beta': beta, 'W1': W1, 'b1': b1, 'W2': W2, 'b2': b2}
    _L0_ffn_in = _L0_ffn_setup()

    def _L1_attn_setup():
        import jax, jax.numpy as jnp
        import numpy as np
        B, T, D, H, LORA = (4, 256, 256, 16, 64)
        HD = D // H
        BLOCK_ID, N_BLOCKS = (6, 12)

        def _ln(x, w, b, eps=1e-05):
            m = x.mean(-1, keepdims=True)
            v = ((x - m) ** 2).mean(-1, keepdims=True)
            return (x - m) * jax.lax.rsqrt(v + eps) * w + b

        def _lora(z, a, b, l):
            return l + jnp.tanh(z @ a.T) @ b.T

        def _reference_tuple_inner(x, xw, rW, kW, vW, gW, r_la, r_lb, r_ll, k_la, k_lb, k_ll, v_la, v_lb, v_ll, g_la, g_lb, g_ll, d_la, d_lb, d_ll, ln_w, ln_b, oW, init_state, u):
            b, t, d = x.shape
            h = init_state.shape[0]
            hd = d // h
            xx = jnp.concatenate([jnp.zeros_like(x[:, :1]), x[:, :-1]], axis=1)
            dx = xx - x
            lerpx = x + dx * xw
            r = (x + dx * _lora(lerpx, r_la, r_lb, r_ll)) @ rW.T
            k = (x + dx * _lora(lerpx, k_la, k_lb, k_ll)) @ kW.T
            v = (x + dx * _lora(lerpx, v_la, v_lb, v_ll)) @ vW.T
            g = (x + dx * _lora(lerpx, g_la, g_lb, g_ll)) @ gW.T
            w = jnp.exp(-jnp.exp(_lora(x + dx * _lora(lerpx, d_la, d_lb, d_ll), d_la, d_lb, d_ll)))
            split = lambda z: z.reshape(b, t, h, hd).transpose(1, 0, 2, 3)
            rs, ws, ks, vs = (split(r), split(w), split(k), split(v))
            uh = u.reshape(h, hd)
            st0 = jnp.broadcast_to(init_state, (b, h, hd, hd))

            def step(st, inp):
                rt, wt, kt, vt = inp
                kv = jnp.einsum('bhi,bhj->bhij', kt, vt)
                y = jnp.einsum('bhi,bhij->bhj', rt, st + uh[None, :, :, None] * kv)
                return (wt[..., None] * st + kv, y)
            st1, ys = jax.lax.scan(step, st0, (rs, ws, ks, vs))
            o = jax.nn.silu(g.reshape(b, t, h, hd)) * _ln(ys.transpose(1, 0, 2, 3), ln_w, ln_b)
            return (o.reshape(b, t, d) @ oW.T, st1)
        key = jax.random.key(seed)
        ks = iter(jax.random.split(key, 64))
        rn = lambda shape, s: jax.random.normal(next(ks), shape, jnp.float32) * s
        inp = {}
        inp['x'] = rn((B, T, D), 1.0)
        r1 = 1.0 - BLOCK_ID / N_BLOCKS
        i = np.arange(D)
        inp['xw'] = jnp.asarray(1.0 - (i / D) ** r1, jnp.float32)
        for nm in ('rW', 'kW', 'vW', 'gW'):
            inp[nm] = rn((D, D), 0.02)
        for p in ('r', 'k', 'v', 'g', 'd'):
            inp[p + '_la'] = rn((LORA, D), 0.001)
            inp[p + '_lb'] = rn((D, LORA), 0.001)
            inp[p + '_ll'] = rn((D,), 1.0)
        inp['ln_w'] = jnp.full((HD,), ((1 + BLOCK_ID) / N_BLOCKS) ** 0.7, jnp.float32)
        inp['ln_b'] = jnp.zeros((HD,), jnp.float32)
        inp['oW'] = rn((D, D), 0.02)
        inp['init_state'] = rn((H, HD, HD), 1.0)
        r0 = BLOCK_ID / (N_BLOCKS - 1)
        ih = i % HD
        inp['u'] = jnp.asarray(r0 * (1 - ih / (D - 1)) + np.remainder(0.1 * (ih + 1), 3.0), jnp.float32)
        return inp
    _L1_attn_in = _L1_attn_setup()

    def _L1_ffn_setup():
        import jax, jax.numpy as jnp
        import numpy as np
        B, T, C = (2, 512, 256)
        H, D = (16, 64)
        CR = 8
        R = C // CR
        ROPE = D // 2
        NOPE = D - ROPE
        E, K, I, S = (8, 2, 128, 1)
        THETA = 100000.0
        EPS = 1e-05

        def _rmsnorm(x, w):
            rms = jnp.sqrt(jnp.mean(x * x, axis=-1, keepdims=True) + EPS)
            return w * (x / rms)

        def _rope(xh):
            d = xh.shape[-1]
            t = jnp.arange(xh.shape[2], dtype=jnp.float32)
            freqs = 1.0 / THETA ** (jnp.arange(0, d, 2, dtype=jnp.float32) / d)
            ang = jnp.outer(t, freqs)
            cos, sin = (jnp.cos(ang), jnp.sin(ang))
            xr = xh.reshape(xh.shape[:-1] + (d // 2, 2))
            x0, x1 = (xr[..., 0], xr[..., 1])
            rot = jnp.stack([x0 * cos - x1 * sin, x0 * sin + x1 * cos], axis=-1)
            return rot.reshape(xh.shape)

        def _attention(x, Wq, Wkva, Wkvb, Wo):
            b, t, _ = x.shape
            q = (x @ Wq).reshape(b, t, H, D).transpose(0, 2, 1, 3)
            ckv = x @ Wkva
            kv_latent, k_rope = (ckv[:, :, :R], ckv[:, :, R:])
            kv = (kv_latent @ Wkvb).reshape(b, t, H, NOPE).transpose(0, 2, 1, 3)
            k_rope = jnp.broadcast_to(k_rope[:, None, :, :], (b, H, t, ROPE))
            q_nope, q_rope = (q[..., :NOPE], q[..., NOPE:])
            q = jnp.concatenate([q_nope, _rope(q_rope)], axis=-1)
            k = jnp.concatenate([kv, _rope(k_rope)], axis=-1)
            v = jnp.concatenate([kv, jnp.zeros_like(k_rope)], axis=-1)
            att = jnp.einsum('bhqd,bhkd->bhqk', q, k) / jnp.sqrt(jnp.float32(D))
            mask = jnp.tril(jnp.ones((t, t), dtype=bool))
            att = jnp.where(mask, att, jnp.float32(-jnp.inf))
            att = jax.nn.softmax(att, axis=-1)
            y = jnp.einsum('bhqk,bhkd->bhqd', att, v)
            y = y.transpose(0, 2, 1, 3).reshape(b, t, H * D)
            return y @ Wo

        def _experts(x_flat, Wg, Wu, Wd):
            g = jax.nn.silu(jnp.einsum('nc,eci->nei', x_flat, Wg))
            u = jnp.einsum('nc,eci->nei', x_flat, Wu)
            return jnp.einsum('nei,eic->nec', g * u, Wd)

        def _moe(x, Wgate, expert_bias, Wg, Wu, Wd, sWg, sWu, sWd):
            b, t, c = x.shape
            xf = x.reshape(-1, c)
            shared = jnp.mean(_experts(xf, sWg, sWu, sWd), axis=1)
            logits = xf @ Wgate + expert_bias
            probs = jax.nn.softmax(logits, axis=-1)
            topk_p, topk_i = jax.lax.top_k(probs, K)
            topk_p = topk_p / jnp.sum(topk_p, axis=-1, keepdims=True)
            comb = jnp.sum(jax.nn.one_hot(topk_i, E, dtype=xf.dtype) * topk_p[..., None], axis=1)
            routed = jnp.einsum('ne,nec->nc', comb, _experts(xf, Wg, Wu, Wd))
            return (shared + routed).reshape(b, t, c)
        key = jax.random.key(seed)
        ks = jax.random.split(key, 16)
        w = lambda k, shp: jax.random.normal(k, shp, dtype=jnp.float32) * 0.02
        return {'x': jax.random.normal(ks[0], (B, T, C), dtype=jnp.float32), 'w_ln1': jnp.ones((C,), jnp.float32), 'Wq': w(ks[1], (C, H * D)), 'Wkva': w(ks[2], (C, R + ROPE)), 'Wkvb': w(ks[3], (R, H * NOPE)), 'Wo': w(ks[4], (H * D, C)), 'w_ln2': jnp.ones((C,), jnp.float32), 'Wgate': w(ks[5], (C, E)), 'expert_bias': jnp.zeros((E,), jnp.float32), 'Wg': w(ks[6], (E, C, I)), 'Wu': w(ks[7], (E, C, I)), 'Wd': w(ks[8], (E, I, C)), 'sWg': w(ks[9], (S, C, I)), 'sWu': w(ks[10], (S, C, I)), 'sWd': w(ks[11], (S, I, C))}
    _L1_ffn_in = _L1_ffn_setup()
    _d = {'L0_attn_h': _L0_attn_in['h'], 'L0_attn_W0': _L0_attn_in['W0'], 'L0_attn_W1': _L0_attn_in['W1'], 'L0_ffn_centroids': _L0_ffn_in['centroids'], 'L0_ffn_gamma': _L0_ffn_in['gamma'], 'L0_ffn_beta': _L0_ffn_in['beta'], 'L0_ffn_W1': _L0_ffn_in['W1'], 'L0_ffn_b1': _L0_ffn_in['b1'], 'L0_ffn_W2': _L0_ffn_in['W2'], 'L0_ffn_b2': _L0_ffn_in['b2'], 'L1_attn_xw': _L1_attn_in['xw'], 'L1_attn_rW': _L1_attn_in['rW'], 'L1_attn_kW': _L1_attn_in['kW'], 'L1_attn_vW': _L1_attn_in['vW'], 'L1_attn_gW': _L1_attn_in['gW'], 'L1_attn_r_la': _L1_attn_in['r_la'], 'L1_attn_r_lb': _L1_attn_in['r_lb'], 'L1_attn_r_ll': _L1_attn_in['r_ll'], 'L1_attn_k_la': _L1_attn_in['k_la'], 'L1_attn_k_lb': _L1_attn_in['k_lb'], 'L1_attn_k_ll': _L1_attn_in['k_ll'], 'L1_attn_v_la': _L1_attn_in['v_la'], 'L1_attn_v_lb': _L1_attn_in['v_lb'], 'L1_attn_v_ll': _L1_attn_in['v_ll'], 'L1_attn_g_la': _L1_attn_in['g_la'], 'L1_attn_g_lb': _L1_attn_in['g_lb'], 'L1_attn_g_ll': _L1_attn_in['g_ll'], 'L1_attn_d_la': _L1_attn_in['d_la'], 'L1_attn_d_lb': _L1_attn_in['d_lb'], 'L1_attn_d_ll': _L1_attn_in['d_ll'], 'L1_attn_ln_w': _L1_attn_in['ln_w'], 'L1_attn_ln_b': _L1_attn_in['ln_b'], 'L1_attn_oW': _L1_attn_in['oW'], 'L1_attn_init_state': _L1_attn_in['init_state'], 'L1_attn_u': _L1_attn_in['u'], 'L1_ffn_w_ln1': _L1_ffn_in['w_ln1'], 'L1_ffn_Wq': _L1_ffn_in['Wq'], 'L1_ffn_Wkva': _L1_ffn_in['Wkva'], 'L1_ffn_Wkvb': _L1_ffn_in['Wkvb'], 'L1_ffn_Wo': _L1_ffn_in['Wo'], 'L1_ffn_w_ln2': _L1_ffn_in['w_ln2'], 'L1_ffn_Wgate': _L1_ffn_in['Wgate'], 'L1_ffn_expert_bias': _L1_ffn_in['expert_bias'], 'L1_ffn_Wg': _L1_ffn_in['Wg'], 'L1_ffn_Wu': _L1_ffn_in['Wu'], 'L1_ffn_Wd': _L1_ffn_in['Wd'], 'L1_ffn_sWg': _L1_ffn_in['sWg'], 'L1_ffn_sWu': _L1_ffn_in['sWu'], 'L1_ffn_sWd': _L1_ffn_in['sWd']}
    _x0 = _d['L0_attn_h']
    _d['L0_attn_h'] = jax.random.normal(jax.random.fold_in(jax.random.key(seed), 1), (8, 512, 256), dtype=_x0.dtype)
    del _x0
    return _d

def reference(L0_attn_h, L0_attn_W0, L0_attn_W1, L0_ffn_centroids, L0_ffn_gamma, L0_ffn_beta, L0_ffn_W1, L0_ffn_b1, L0_ffn_W2, L0_ffn_b2, L1_attn_xw, L1_attn_rW, L1_attn_kW, L1_attn_vW, L1_attn_gW, L1_attn_r_la, L1_attn_r_lb, L1_attn_r_ll, L1_attn_k_la, L1_attn_k_lb, L1_attn_k_ll, L1_attn_v_la, L1_attn_v_lb, L1_attn_v_ll, L1_attn_g_la, L1_attn_g_lb, L1_attn_g_ll, L1_attn_d_la, L1_attn_d_lb, L1_attn_d_ll, L1_attn_ln_w, L1_attn_ln_b, L1_attn_oW, L1_attn_init_state, L1_attn_u, L1_ffn_w_ln1, L1_ffn_Wq, L1_ffn_Wkva, L1_ffn_Wkvb, L1_ffn_Wo, L1_ffn_w_ln2, L1_ffn_Wgate, L1_ffn_expert_bias, L1_ffn_Wg, L1_ffn_Wu, L1_ffn_Wd, L1_ffn_sWg, L1_ffn_sWu, L1_ffn_sWd):

    def _L0_attn_ref(h, W0, W1):
        import jax, jax.numpy as jnp
        import numpy as np
        B, T, H, NUM_LAYERS = (8, 1024, 256, 2)

        def _log_g(x):
            return jnp.where(x >= 0.0, jnp.log(jax.nn.relu(x) + 0.5), -jax.nn.softplus(-x))

        def _heinsen_scan(log_coeffs, log_values):
            a_star = jnp.cumsum(log_coeffs, axis=1)
            return jnp.exp(a_star + jax.lax.cumlogsumexp(log_values - a_star, axis=1))
        for W in (W0, W1):
            z = jnp.einsum('bth,hk->btk', h, W)
            hidden, gate, proj = jnp.split(z, 3, axis=-1)
            log_coeffs = -jax.nn.softplus(gate)
            log_values = -jax.nn.softplus(-gate) + _log_g(hidden)
            out = _heinsen_scan(log_coeffs, log_values)
            g = jax.nn.sigmoid(proj)
            h = g * out + (1.0 - g) * h
        return h

    def _L0_ffn_ref(x, centroids, gamma, beta, W1, b1, W2, b2):
        import jax, jax.numpy as jnp
        import numpy as np
        B, S, D, F, E = (1, 256, 256, 1024, 8)
        EPS = 1e-05

        def _sublayer(xs, g, b, W1e, b1e, W2e, b2e):
            mu = jnp.mean(xs, axis=-1, keepdims=True)
            var = jnp.mean(jnp.square(xs - mu), axis=-1, keepdims=True)
            h = (xs - mu) * jax.lax.rsqrt(var + EPS) * g + b
            return xs + jax.nn.relu(h @ W1e.T + b1e) @ W2e.T + b2e
        feats = x.reshape(-1, x.shape[-1])
        scores = jax.lax.stop_gradient(feats @ centroids.T)
        expert = jnp.argmax(scores, axis=1)
        onehot = jax.nn.one_hot(expert, E, dtype=feats.dtype)
        alpha = jax.nn.sigmoid(jnp.sum(feats * centroids[expert], axis=-1, keepdims=True))
        ys = jax.vmap(_sublayer, in_axes=(None, 0, 0, 0, 0, 0, 0))(feats, gamma, beta, W1, b1, W2, b2)
        y = jnp.einsum('te,etd->td', onehot, ys)
        out = alpha * y + (1.0 - alpha) * feats
        return out.reshape(x.shape)

    def _L1_attn_ref(x, xw, rW, kW, vW, gW, r_la, r_lb, r_ll, k_la, k_lb, k_ll, v_la, v_lb, v_ll, g_la, g_lb, g_ll, d_la, d_lb, d_ll, ln_w, ln_b, oW, init_state, u):
        import jax, jax.numpy as jnp
        import numpy as np
        B, T, D, H, LORA = (4, 256, 256, 16, 64)
        HD = D // H
        BLOCK_ID, N_BLOCKS = (6, 12)

        def _ln(x, w, b, eps=1e-05):
            m = x.mean(-1, keepdims=True)
            v = ((x - m) ** 2).mean(-1, keepdims=True)
            return (x - m) * jax.lax.rsqrt(v + eps) * w + b

        def _lora(z, a, b, l):
            return l + jnp.tanh(z @ a.T) @ b.T

        def _reference_tuple_inner(x, xw, rW, kW, vW, gW, r_la, r_lb, r_ll, k_la, k_lb, k_ll, v_la, v_lb, v_ll, g_la, g_lb, g_ll, d_la, d_lb, d_ll, ln_w, ln_b, oW, init_state, u):
            b, t, d = x.shape
            h = init_state.shape[0]
            hd = d // h
            xx = jnp.concatenate([jnp.zeros_like(x[:, :1]), x[:, :-1]], axis=1)
            dx = xx - x
            lerpx = x + dx * xw
            r = (x + dx * _lora(lerpx, r_la, r_lb, r_ll)) @ rW.T
            k = (x + dx * _lora(lerpx, k_la, k_lb, k_ll)) @ kW.T
            v = (x + dx * _lora(lerpx, v_la, v_lb, v_ll)) @ vW.T
            g = (x + dx * _lora(lerpx, g_la, g_lb, g_ll)) @ gW.T
            w = jnp.exp(-jnp.exp(_lora(x + dx * _lora(lerpx, d_la, d_lb, d_ll), d_la, d_lb, d_ll)))
            split = lambda z: z.reshape(b, t, h, hd).transpose(1, 0, 2, 3)
            rs, ws, ks, vs = (split(r), split(w), split(k), split(v))
            uh = u.reshape(h, hd)
            st0 = jnp.broadcast_to(init_state, (b, h, hd, hd))

            def step(st, inp):
                rt, wt, kt, vt = inp
                kv = jnp.einsum('bhi,bhj->bhij', kt, vt)
                y = jnp.einsum('bhi,bhij->bhj', rt, st + uh[None, :, :, None] * kv)
                return (wt[..., None] * st + kv, y)
            st1, ys = jax.lax.scan(step, st0, (rs, ws, ks, vs))
            o = jax.nn.silu(g.reshape(b, t, h, hd)) * _ln(ys.transpose(1, 0, 2, 3), ln_w, ln_b)
            return (o.reshape(b, t, d) @ oW.T, st1)
        return _reference_tuple_inner(x, xw, rW, kW, vW, gW, r_la, r_lb, r_ll, k_la, k_lb, k_ll, v_la, v_lb, v_ll, g_la, g_lb, g_ll, d_la, d_lb, d_ll, ln_w, ln_b, oW, init_state, u)[0]

    def _L1_ffn_ref(x, w_ln1, Wq, Wkva, Wkvb, Wo, w_ln2, Wgate, expert_bias, Wg, Wu, Wd, sWg, sWu, sWd):
        import jax, jax.numpy as jnp
        import numpy as np
        B, T, C = (2, 512, 256)
        H, D = (16, 64)
        CR = 8
        R = C // CR
        ROPE = D // 2
        NOPE = D - ROPE
        E, K, I, S = (8, 2, 128, 1)
        THETA = 100000.0
        EPS = 1e-05

        def _rmsnorm(x, w):
            rms = jnp.sqrt(jnp.mean(x * x, axis=-1, keepdims=True) + EPS)
            return w * (x / rms)

        def _rope(xh):
            d = xh.shape[-1]
            t = jnp.arange(xh.shape[2], dtype=jnp.float32)
            freqs = 1.0 / THETA ** (jnp.arange(0, d, 2, dtype=jnp.float32) / d)
            ang = jnp.outer(t, freqs)
            cos, sin = (jnp.cos(ang), jnp.sin(ang))
            xr = xh.reshape(xh.shape[:-1] + (d // 2, 2))
            x0, x1 = (xr[..., 0], xr[..., 1])
            rot = jnp.stack([x0 * cos - x1 * sin, x0 * sin + x1 * cos], axis=-1)
            return rot.reshape(xh.shape)

        def _attention(x, Wq, Wkva, Wkvb, Wo):
            b, t, _ = x.shape
            q = (x @ Wq).reshape(b, t, H, D).transpose(0, 2, 1, 3)
            ckv = x @ Wkva
            kv_latent, k_rope = (ckv[:, :, :R], ckv[:, :, R:])
            kv = (kv_latent @ Wkvb).reshape(b, t, H, NOPE).transpose(0, 2, 1, 3)
            k_rope = jnp.broadcast_to(k_rope[:, None, :, :], (b, H, t, ROPE))
            q_nope, q_rope = (q[..., :NOPE], q[..., NOPE:])
            q = jnp.concatenate([q_nope, _rope(q_rope)], axis=-1)
            k = jnp.concatenate([kv, _rope(k_rope)], axis=-1)
            v = jnp.concatenate([kv, jnp.zeros_like(k_rope)], axis=-1)
            att = jnp.einsum('bhqd,bhkd->bhqk', q, k) / jnp.sqrt(jnp.float32(D))
            mask = jnp.tril(jnp.ones((t, t), dtype=bool))
            att = jnp.where(mask, att, jnp.float32(-jnp.inf))
            att = jax.nn.softmax(att, axis=-1)
            y = jnp.einsum('bhqk,bhkd->bhqd', att, v)
            y = y.transpose(0, 2, 1, 3).reshape(b, t, H * D)
            return y @ Wo

        def _experts(x_flat, Wg, Wu, Wd):
            g = jax.nn.silu(jnp.einsum('nc,eci->nei', x_flat, Wg))
            u = jnp.einsum('nc,eci->nei', x_flat, Wu)
            return jnp.einsum('nei,eic->nec', g * u, Wd)

        def _moe(x, Wgate, expert_bias, Wg, Wu, Wd, sWg, sWu, sWd):
            b, t, c = x.shape
            xf = x.reshape(-1, c)
            shared = jnp.mean(_experts(xf, sWg, sWu, sWd), axis=1)
            logits = xf @ Wgate + expert_bias
            probs = jax.nn.softmax(logits, axis=-1)
            topk_p, topk_i = jax.lax.top_k(probs, K)
            topk_p = topk_p / jnp.sum(topk_p, axis=-1, keepdims=True)
            comb = jnp.sum(jax.nn.one_hot(topk_i, E, dtype=xf.dtype) * topk_p[..., None], axis=1)
            routed = jnp.einsum('ne,nec->nc', comb, _experts(xf, Wg, Wu, Wd))
            return (shared + routed).reshape(b, t, c)
        x = x + _attention(_rmsnorm(x, w_ln1), Wq, Wkva, Wkvb, Wo)
        residual = x
        xn = _rmsnorm(x, w_ln2)
        x_out = _moe(xn, Wgate, expert_bias, Wg, Wu, Wd, sWg, sWu, sWd)
        return residual + x_out
    x = L0_attn_h
    xn = _layernorm(x, axis=-1)
    s = _L0_attn_ref(xn, L0_attn_W0, L0_attn_W1)
    g = _silu(_L0_ffn_ref(xn, L0_ffn_centroids, L0_ffn_gamma, L0_ffn_beta, L0_ffn_W1, L0_ffn_b1, L0_ffn_W2, L0_ffn_b2))
    x = x + s * g
    xn = _layernorm(x, axis=-1)
    s = _L1_attn_ref(xn, L1_attn_xw, L1_attn_rW, L1_attn_kW, L1_attn_vW, L1_attn_gW, L1_attn_r_la, L1_attn_r_lb, L1_attn_r_ll, L1_attn_k_la, L1_attn_k_lb, L1_attn_k_ll, L1_attn_v_la, L1_attn_v_lb, L1_attn_v_ll, L1_attn_g_la, L1_attn_g_lb, L1_attn_g_ll, L1_attn_d_la, L1_attn_d_lb, L1_attn_d_ll, L1_attn_ln_w, L1_attn_ln_b, L1_attn_oW, L1_attn_init_state, L1_attn_u)
    g = _silu(_L1_ffn_ref(xn, L1_ffn_w_ln1, L1_ffn_Wq, L1_ffn_Wkva, L1_ffn_Wkvb, L1_ffn_Wo, L1_ffn_w_ln2, L1_ffn_Wgate, L1_ffn_expert_bias, L1_ffn_Wg, L1_ffn_Wu, L1_ffn_Wd, L1_ffn_sWg, L1_ffn_sWu, L1_ffn_sWd))
    x = x + s * g
    return x

_drawn_inputs = setup_inputs


def setup_inputs(seed=0):
    import zlib

    import numpy as np

    out = dict(_drawn_inputs(seed))
    spreads = {'L0_ffn_gamma': (1.0, 0.6),
     'L0_ffn_beta': (0.0, 0.8),
     'L0_ffn_b1': (0.0, 0.577),
     'L0_ffn_b2': (0.0, 0.1),
     'L1_attn_ln_w': (0.6857119798660278, 0.6),
     'L1_attn_ln_b': (0.0, 0.8),
     'L1_ffn_w_ln1': (1.0, 0.6),
     'L1_ffn_w_ln2': (1.0, 0.6),
     'L1_ffn_expert_bias': (0.0, 0.8)}
    factors = {'L1_attn_xw': 8.0,
     'L1_attn_r_la': 22.25,
     'L1_attn_r_lb': 22.126,
     'L1_attn_k_la': 31.887,
     'L1_attn_k_lb': 32.272,
     'L1_attn_v_la': 40.297,
     'L1_attn_v_lb': 39.919,
     'L1_attn_g_la': 24.33,
     'L1_attn_g_lb': 24.247,
     'L1_attn_d_la': 200.0,
     'L1_attn_d_lb': 200.0,
     'L1_attn_d_ll': 4.069,
     'L1_attn_init_state': 8.0,
     'L1_attn_u': 5.262,
     'L1_ffn_Wq': 8.0,
     'L1_ffn_Wkva': 8.0,
     'L1_ffn_Wkvb': 8.0,
     'L1_ffn_Wo': 8.0,
     'L1_ffn_Wgate': 8.0,
     'L1_ffn_Wg': 8.0,
     'L1_ffn_Wu': 8.0,
     'L1_ffn_Wd': 8.0,
     'L1_ffn_sWg': 8.0,
     'L1_ffn_sWu': 8.0,
     'L1_ffn_sWd': 8.0}
    for name, (base, spread) in spreads.items():
        noise = np.random.default_rng([zlib.crc32(name.encode()), seed]).standard_normal(out[name].shape)
        drawn = base * np.exp(spread * noise) if base else spread * noise
        out[name] = jnp.asarray(drawn.astype(out[name].dtype))
    for name, factor in factors.items():
        out[name] = (out[name] * factor).astype(out[name].dtype)
    return out
```

```python
from contextlib import ExitStack

import concourse.bass as bass
import numpy as np
from concourse import mybir

F32 = mybir.dt.float32
BF16 = mybir.dt.bfloat16
I32 = mybir.dt.int32
U32 = mybir.dt.uint32
ALU = mybir.AluOpType
ACT = mybir.ActivationFunctionType
X = mybir.AxisListType.X

P = 128
B, T, D = 8, 512, 256
NT = T // P
KD = D // P
TILES = B * NT
E, F = 8, 1024
FC = F // P
ROW = D + 1
SLOTS = TILES + E - 1
EPS = 1e-5
HD = 16
HG = P // HD
NH, ND, RD = 16, 32, 32
LORA = 64
ME, MI = 8, 128

CONST = {}
_at = 0
for _name, _n in (("ident", P), ("before", P), ("ones", P), ("iota", E), ("slot", SLOTS),
                  ("sel", HD * P), ("red", HD // 4 * 32), ("spread", P), ("mean", P), ("mask", P),
                  ("cos", T), ("sin", T)):
    if _name == "sel":
        NCONST_A = _at
    CONST[_name] = (_at, _n)
    _at += _n
NCONST = _at


def rho(h, j):
    return 32 * (j % 4) + HG * (j // 4) + h


def constants():
    c = np.zeros((P, NCONST), np.float32)

    def put(name, a):
        at, n = CONST[name]
        c[:, at:at + n] = a

    p = np.arange(P)
    put("ident", np.eye(P))
    put("before", p[:, None] < p[None, :])
    put("ones", 1.0)
    put("iota", np.arange(E)[None, :])
    put("slot", np.arange(SLOTS)[None, :] * P)
    sel = np.zeros((P, HD, P), np.float32)
    red = np.zeros((P, HD // 4, 32), np.float32)
    spread = np.zeros((P, P), np.float32)
    mean = np.zeros((P, P), np.float32)
    for h in range(HG):
        for j in range(HD):
            sel[rho(h, j), j, h * HD:(h + 1) * HD] = 1.0
            spread[h * HD:(h + 1) * HD, rho(h, j)] = 1.0
            for i in range(HD):
                mean[rho(h, j), rho(h, i)] = 1.0 / HD
        for g in range(HD // 4):
            red[h * HD:(h + 1) * HD, g, HG * g + h] = 1.0
    put("sel", sel.reshape(P, -1))
    put("red", red.reshape(P, -1))
    put("spread", spread)
    put("mean", mean)
    put("mask", np.where(p[None, :] > p[:, None], -1e30, 0.0))
    freqs = np.float32(1.0) / np.float32(100000.0) ** (np.arange(0, RD, 2, dtype=np.float32) / np.float32(RD))
    ang = np.outer(np.arange(T, dtype=np.float32), freqs)
    cos, sin = np.ones((P, T), np.float32), np.zeros((P, T), np.float32)
    for base in (ND, ND + 64):
        for r in range(RD):
            cos[base + r] = np.cos(ang[:, r // 2])
            sin[base + r] = np.sin(ang[:, r // 2]) * (1.0 if r % 2 else -1.0)
    put("cos", cos)
    put("sin", sin)
    return c


class Arena:

    def __init__(self, tensor, at=0):
        self.tensor, self.at = tensor, at

    def take(self, *shape):
        n = 1
        for s in shape:
            n *= s
        view = self.tensor[:, self.at:self.at + n]
        self.at += n
        assert self.at <= self.tensor.shape[1], self.at
        if len(shape) == 2:
            return view.rearrange("p (a b) -> p a b", a=shape[0])
        if len(shape) == 3:
            return view.rearrange("p (a b c) -> p a b c", a=shape[0], b=shape[1])
        return view


class Steps:

    def __init__(self, base):
        self.base, self.n = base, 0

    def next(self):
        self.n += 1
        return self.base + self.n


def phase_a(nc, io, dram, mem, const, bank, w1s, w2s, pos_all, tile_expert, ffn_loaded):
    with ExitStack() as ctx:
        def sem(name):
            return ctx.enter_context(nc.semaphore("a_" + name))

        x_sb = mem.take(NT, D)
        xn = x_sb
        xn_all = mem.take(TILES, ROW)
        zeros = mem.take(ROW)
        stats = mem.take(NT, 6)
        mv = mem.take(NT, 2)
        var_eps = mem.take(NT)
        rstd = mem.take(NT)
        neg_half = mem.take(NT)
        h0 = mem.take(KD, T)
        h1 = mem.take(KD, T)
        h2 = h0
        gru_w = [mem.take(KD, 3 * D) for _ in range(2)]
        cent = mem.take(KD, E)
        sig_hidden, sig_gate = mem.take(T), mem.take(T)
        sig = [[sig_hidden, sig_gate, mem.take(T), mem.take(T)] for _ in range(2)]
        scanned = [mem.take(T) for _ in range(2)]
        s_tok = h1.rearrange("p k t -> p (k t)").rearrange("p (i d) -> p i d", i=NT)
        scores = mem.take(TILES, E)
        top = mem.take(TILES)

        def work(tile, n, at=0):
            return tile[:, at:at + n]

        cand = work(sig_hidden, TILES * E).rearrange("p (t e) -> p t e", e=E)
        first = work(sig_hidden, TILES, TILES * E)
        onehot = work(sig_gate, TILES * E).rearrange("p (t e) -> p t e", e=E)
        incl = work(sig[0][2], TILES * E).rearrange("p (t e) -> p t e", e=E)
        excl = work(sig[0][3], TILES * E).rearrange("p (t e) -> p t e", e=E)
        pad_i = work(sig[1][2], E).bitcast(I32)
        padded = work(sig[1][2], E, 16)
        ends = work(sig[1][2], E, 32)
        starts = work(sig[1][2], E, 48)
        posf = work(sig[1][2], TILES, 64)
        slot_e = work(sig[1][2], SLOTS, 128)
        slot_ge = work(sig[1][3], SLOTS * E).rearrange("p (t e) -> p t e", e=E)

        const_in = sem("const_in")
        weights_in = sem("weights_in")
        x_in = sem("x_in")
        zeroed = sem("zeroed")
        zeros_set = sem("zeros_set")
        xn_done = sem("xn_done")
        dve_step = sem("dve_step")
        rstd_done = sem("rstd_done")
        xn_kept = sem("xn_kept")
        xn_turned = sem("xn_turned")
        h0_left = sem("h0_left")
        h0_right = sem("h0_right")
        score_mm = sem("score_mm")
        scores_read = sem("scores_read")
        gru_mm = sem("gru_mm")
        gru_sig = sem("gru_sig")
        gru_read = sem("gru_read")
        gru_step = sem("gru_step")
        gru_scan = sem("gru_scan")
        blend_step = sem("blend_step")
        h_ready = sem("h_ready")
        s_turned = sem("s_turned")
        s_out = sem("s_out")
        s_stored = sem("s_stored")
        chain = sem("chain")
        route_mm = sem("route_mm")
        pos_done = sem("pos_done")
        alpha_done = sem("alpha_done")
        top_done = sem("top_done")
        scattered = sem("scattered")

        NPER = 2 * NT + 1
        block = ctx.enter_context(nc.Block())
        h_rows = io["L0_attn_h"].rearrange("b t d -> (b t) d")

        @block.sync
        def _(sp):
            sp.dma_start(const, io["const"][:, 0:NCONST_A]).then_inc(const_in, 16)
            sp.dma_start(x_sb, h_rows[0:T, :].rearrange("(i p) d -> p i d", p=P)).then_inc(x_in, 16)
            for layer in range(2):
                sp.dma_start(gru_w[layer], io[f"L0_attn_W{layer}"].rearrange("(k p) n -> p k n", p=P)).then_inc(weights_in, 16)
            sp.dma_start(cent, io["centT"].rearrange("(k p) n -> p k n", p=P)).then_inc(weights_in, 16)
            sp.wait_ge(zeros_set, 1)

            def expert_weights(e):
                sp.dma_start(w1s[:, bass.ds(e * KD * F, KD * F)].rearrange("p (k f) -> p k f", k=KD),
                             io["W1T"][bass.ds(e * D, D), :].rearrange("(k p) f -> p k f", p=P)).then_inc(ffn_loaded, 16)
                sp.dma_start(w2s[:, bass.ds(e * FC * D, FC * D)].rearrange("p (k f) -> p k f", k=FC),
                             io["W2T"][bass.ds(e * F, F), :].rearrange("(k p) f -> p k f", p=P)).then_inc(ffn_loaded, 16)
                for z in range(5):
                    sp.dma_start(dram["sorted"][bass.ds((5 * e + z) * P, P), :], zeros).then_inc(zeroed, 16)

            with sp.Fori(0, B - 1) as b:
                sp.wait_ge(xn_kept, b + 2)
                sp.wait_ge(xn_turned, 2 * b + 2)
                sp.dma_start(x_sb, h_rows[bass.ds(b * T + T, T), :].rearrange("(i p) d -> p i d", p=P)).then_inc(x_in, 16)
                expert_weights(b)
            expert_weights(B - 1)

        @block.tensor
        def _(pe):
            pe.wait_ge(const_in, 16)
            pe.wait_ge(weights_in, 48)
            ident = const[:, 0:P]

            def gru_unit(b, u):
                layer, m, s = u // 2, u % 2, 3 * (u % 2)
                src = h0 if layer == 0 else h1
                pe.wait_ge(gru_sig, 16 * b + 4 * u + 4)
                pe.wait_ge(gru_read, 4 * b + u + 1)
                for q in range(3):
                    for k in range(KD):
                        last = nc.tensor.matmul(bank[s + q][:, :], gru_w[layer][:, k, q * D + m * P:q * D + (m + 1) * P],
                                                src[:, k, :], start=(k == 0), stop=(k == KD - 1))
                last.then_inc(gru_mm, 1)

            with pe.Fori(0, B) as b:
                pe.wait_ge(xn_done, NT * b + NT)
                pe.wait_ge(s_out, 2 * b + 2)
                for k in range(KD):
                    for i in range(NT):
                        last = nc.tensor.transpose(bank[6 + k][:, i * P:(i + 1) * P], xn[:, i, k * P:(k + 1) * P], ident)
                    last.then_inc(xn_turned, 1)
                pe.wait_ge(h0_left, b + 1)
                pe.wait_ge(h0_right, b + 1)
                for i in range(NT):
                    for k in range(KD):
                        last = nc.tensor.matmul(bank[6][:, i * E:(i + 1) * E], h0[:, k, i * P:(i + 1) * P], cent[:, k, :],
                                                start=(k == 0), stop=(k == KD - 1))
                last.then_inc(score_mm, 1)
                gru_unit(b, 0)
                gru_unit(b, 1)
                pe.wait_ge(h_ready, 4 * b + 2 + 2)
                gru_unit(b, 2)
                gru_unit(b, 3)
                pe.wait_ge(h_ready, 4 * b + 4 + 2)
                pe.wait_ge(scores_read, b + 1)
                for half in range(2):
                    for i in (2 * half, 2 * half + 1):
                        for m in range(KD):
                            last = nc.tensor.transpose(bank[6 + half][:, (i % 2) * D + m * P:(i % 2) * D + (m + 1) * P],
                                                       h2[:, m, i * P:(i + 1) * P], ident)
                    last.then_inc(s_turned, 1)
            pe.wait_ge(chain, 4)
            at = CONST["before"][0]
            oh = onehot.rearrange("p t e -> p (t e)")
            nc.tensor.matmul(bank[0][:, 0:TILES * E], const[:, at:at + P], oh, start=True, stop=True)
            at = CONST["ones"][0]
            nc.tensor.matmul(bank[1][:, 0:TILES * E], const[:, at:at + P], oh, start=True, stop=True).then_inc(route_mm, 1)

        @block.scalar
        def _(act):
            act.sem_inc(gru_sig, 8)
            act.sem_inc(s_out, 2)
            act.sem_inc(s_stored, 16)
            with act.Fori(0, B) as b:
                act.wait_ge(xn_turned, 2 * b + 2)
                nc.scalar.activation(h0[:, 1, :], bank[7][:, :], ACT.Copy).then_inc(h0_right, 1)
                for u in range(4):
                    s = 3 * (u % 2)
                    act.wait_ge(gru_mm, 4 * b + u + 1)
                    act.wait_ge(gru_scan, 4 * b + u + 2)
                    act.wait_ge(h_ready, 4 * b + u + 1)
                    tiles = sig[u % 2]
                    nc.scalar.activation(tiles[0], bank[s][:, :], ACT.Sigmoid).then_inc(gru_sig, 1)
                    nc.scalar.activation(tiles[1], bank[s + 1][:, :], ACT.Sigmoid).then_inc(gru_sig, 1)
                    nc.scalar.activation(tiles[2], bank[s + 1][:, :], ACT.Sigmoid, scale=-1.0).then_inc(gru_sig, 1)
                    nc.scalar.activation(tiles[3], bank[s + 2][:, :], ACT.Sigmoid).then_inc(gru_sig, 1)
                for half in range(2):
                    act.wait_ge(s_turned, 2 * b + half + 1)
                    nc.scalar.activation(s_tok[:, 2 * half:2 * half + 2, :], bank[6 + half][:, :].rearrange("p (i d) -> p i d", i=2),
                                         ACT.Copy).then_inc(s_out, 1)
                act.wait_ge(s_out, 2 * b + 4)
                act.dma_start(dram["s"][bass.ds(b * T, T), :].rearrange("(i p) d -> p i d", p=P), s_tok).then_inc(s_stored, 16)
            act.wait_ge(top_done, 1)
            nc.scalar.activation(xn_all[:, :, D], top, ACT.Sigmoid).then_inc(alpha_done, 1)
            act.wait_ge(s_stored, 16 * B + 16)

        @block.vector
        def _(v):
            v.memset(zeros, 0.0).then_inc(zeros_set, 1)
            v.sem_inc(gru_read, 2)
            v.sem_inc(gru_scan, 2)
            with v.Fori(0, B) as b:
                step = Steps(NPER * b)
                v.wait_ge(x_in, 16 * b + 16)
                for i in range(NT):
                    nc.vector.bn_stats(stats[:, i, :], x_sb[:, i, :]).then_inc(dve_step, 1)
                for i in range(NT):
                    got = step.next()
                v.wait_ge(dve_step, got)
                nc.vector.memset(var_eps, EPS)
                for i in range(NT):
                    nc.vector.bn_aggr(mv[:, i, :], stats[:, i, :]).then_inc(dve_step, 1)
                for i in range(NT):
                    got = step.next()
                v.wait_ge(dve_step, got)
                nc.vector.tensor_scalar_add(var_eps, mv[:, :, 1], EPS).then_inc(dve_step, 1)
                v.wait_ge(rstd_done, b + 1)
                for i in range(NT):
                    nc.vector.tensor_scalar(xn[:, i, :], x_sb[:, i, :], mv[:, i, 0:1], rstd[:, i:i + 1],
                                            ALU.subtract, ALU.mult).then_inc(xn_done, 1)
                v.wait_ge(xn_turned, 2 * b + 1)
                nc.vector.tensor_copy(h0[:, 0, :], bank[6][:, :]).then_inc(h0_left, 1)
                v.wait_ge(score_mm, b + 1)
                nc.vector.tensor_copy(scores.rearrange("p t e -> p (t e)")[:, bass.ds(b * NT * E, NT * E)],
                                      bank[6][:, 0:NT * E]).then_inc(scores_read, 1)
                for u in range(4):
                    tiles = sig[u % 2]
                    hidden = bank[3 * (u % 2)]
                    at = 16 * b + 4 * u + 8
                    link = Steps(8 * b + 2 * u)
                    v.wait_ge(gru_sig, at + 1)
                    nc.vector.tensor_scalar_min(tiles[0], tiles[0], 0.5).then_inc(gru_step, 1)
                    v.wait_ge(gru_step, link.next())
                    nc.vector.scalar_tensor_tensor(tiles[0], hidden[:, :], 0.0, tiles[0], ALU.max, ALU.add).then_inc(gru_read, 1)
                    v.wait_ge(gru_read, 4 * b + u + 1 + 2)
                    v.wait_ge(gru_sig, at + 2)
                    nc.vector.tensor_tensor(tiles[1], tiles[0], tiles[1], ALU.mult).then_inc(gru_step, 1)
                    v.wait_ge(gru_step, link.next())
                    v.wait_ge(gru_sig, at + 3)
                    v.wait_ge(h_ready, 4 * b + u + 1)
                    nc.vector.tensor_tensor_scan(scanned[u % 2], tiles[2], tiles[1], 0.0, ALU.mult, ALU.add).then_inc(gru_scan, 1)
            link = Steps(0)
            v.wait_ge(scores_read, B)
            nc.vector.tensor_reduce(top, scores, X, ALU.max).then_inc(top_done, 1)
            v.wait_ge(top_done, 1)
            nc.vector.tensor_tensor(cand, scores, top.rearrange("p (t o) -> p t o", o=1).broadcast_to([P, TILES, E]), ALU.is_ge).then_inc(chain, 1)
            v.wait_ge(chain, link.next())
            iota = const[:, CONST["iota"][0]:CONST["iota"][0] + E].rearrange("p (o e) -> p o e", o=1).broadcast_to([P, TILES, E])
            nc.vector.scalar_tensor_tensor(cand, cand, -float(E), iota, ALU.mult, ALU.add).then_inc(chain, 1)
            v.wait_ge(chain, link.next())
            nc.vector.tensor_reduce(first, cand, X, ALU.min).then_inc(chain, 1)
            v.wait_ge(chain, link.next())
            nc.vector.tensor_tensor(onehot, cand, first.rearrange("p (t o) -> p t o", o=1).broadcast_to([P, TILES, E]), ALU.is_equal).then_inc(chain, 1)
            v.wait_ge(chain, link.next())
            v.wait_ge(route_mm, 1)
            ranks = bank[0][:, 0:TILES * E].rearrange("p (t e) -> p t e", e=E)
            counts = bank[1][:, 0:TILES * E].rearrange("p (t e) -> p t e", e=E)
            one = const[:, CONST["ones"][0]:CONST["ones"][0] + TILES]
            for e in range(E):
                last = nc.vector.tensor_tensor_scan(incl[:, :, e], one, counts[:, :, e], 0.0, ALU.mult, ALU.add)
            last.then_inc(chain, 1)
            v.wait_ge(chain, link.next())
            nc.vector.tensor_tensor(excl, incl, counts, ALU.subtract).then_inc(chain, 1)
            nc.vector.tensor_scalar_add(pad_i, incl[:, TILES - 1, :], float(P - 1)).then_inc(chain, 1)
            link.next()
            v.wait_ge(chain, link.next())
            nc.vector.tensor_single_scalar(pad_i, pad_i, 7, ALU.arith_shift_right).then_inc(chain, 1)
            v.wait_ge(chain, link.next())
            nc.vector.tensor_scalar_mul(padded, pad_i, float(P)).then_inc(chain, 1)
            v.wait_ge(chain, link.next())
            nc.vector.tensor_tensor_scan(ends, one[:, 0:E], padded, 0.0, ALU.mult, ALU.add).then_inc(chain, 1)
            v.wait_ge(chain, link.next())
            nc.vector.tensor_tensor(starts, ends, padded, ALU.subtract).then_inc(chain, 1)
            nc.vector.tensor_tensor(excl, excl, ranks, ALU.add).then_inc(chain, 1)
            link.next()
            v.wait_ge(chain, link.next())
            nc.vector.tensor_tensor(excl, excl, starts.rearrange("p (o e) -> p o e", o=1).broadcast_to([P, TILES, E]), ALU.add).then_inc(chain, 1)
            v.wait_ge(chain, link.next())
            nc.vector.tensor_tensor(excl, excl, onehot, ALU.mult).then_inc(chain, 1)
            v.wait_ge(chain, link.next())
            nc.vector.tensor_reduce(posf, excl, X, ALU.add).then_inc(chain, 1)
            v.wait_ge(chain, link.next())
            nc.vector.tensor_copy(pos_all[:, 0:TILES], posf).then_inc(pos_done, 1)
            nc.vector.memset(pos_all[:, TILES:TILES + NT], 0)
            slot = const[:, CONST["slot"][0]:CONST["slot"][0] + SLOTS].rearrange("p (t o) -> p t o", o=1).broadcast_to([P, SLOTS, E])
            nc.vector.tensor_tensor(slot_ge, slot, ends.rearrange("p (o e) -> p o e", o=1).broadcast_to([P, SLOTS, E]), ALU.is_ge).then_inc(chain, 1)
            v.wait_ge(chain, link.next())
            nc.vector.tensor_reduce(slot_e, slot_ge, X, ALU.add).then_inc(chain, 1)
            v.wait_ge(chain, link.next())
            nc.vector.tensor_scalar_min(tile_expert, slot_e, float(E - 1)).then_inc(chain, 1)
            v.wait_ge(chain, link.next())

        @block.gpsimd
        def _(g):
            g.memset(neg_half, -0.5).then_inc(xn_kept, 1)
            g.sem_inc(h_ready, 2)
            g.wait_ge(xn_kept, 1)
            with g.Fori(0, B) as b:
                g.wait_ge(dve_step, NPER * b + NPER)
                nc.gpsimd.tensor_tensor(rstd, var_eps, neg_half, ALU.pow).then_inc(rstd_done, 1)
                g.wait_ge(xn_done, NT * b + NT)
                nc.gpsimd.tensor_copy(xn_all[:, bass.ds(b * NT, NT), 0:D], xn).then_inc(xn_kept, 1)
                for u in range(4):
                    src, dst = (h0, h1) if u < 2 else (h1, h2)
                    m = u % 2
                    link = Steps(8 * b + 2 * u)
                    g.wait_ge(gru_scan, 4 * b + u + 1 + 2)
                    blend = scanned[m]
                    nc.gpsimd.tensor_tensor(blend, scanned[m], src[:, m, :], ALU.subtract).then_inc(blend_step, 1)
                    g.wait_ge(blend_step, link.next())
                    g.wait_ge(gru_sig, 16 * b + 4 * u + 4 + 8)
                    nc.gpsimd.tensor_tensor(blend, blend, sig[m][3], ALU.mult).then_inc(blend_step, 1)
                    g.wait_ge(blend_step, link.next())
                    if u == 0:
                        g.wait_ge(s_stored, 16 * b + 16)
                    nc.gpsimd.tensor_tensor(dst[:, m, :], blend, src[:, m, :], ALU.add).then_inc(h_ready, 1)
            g.wait_ge(zeroed, 16 * 5 * B)
            g.wait_ge(pos_done, 1)
            g.wait_ge(alpha_done, 1)
            for t in range(TILES):
                g.indirect_dma_start(out=dram["sorted"][:, :], out_offset=bass.IndirectOffsetOnAxis(ap=pos_all[:, t:t + 1], axis=0),
                                     in_=xn_all[:, t, :], in_offset=None).then_inc(scattered, 16)
            g.wait_ge(scattered, 16 * TILES)


def phase_b(nc, io, dram, mem, const, bank, w1s, w2s, tile_expert, ffn_loaded):
    with ExitStack() as ctx:
        def sem(name):
            return ctx.enter_context(nc.semaphore("b_" + name))

        xs = [mem.take(ROW) for _ in range(2)]
        n_tok = mem.take(D)
        stats, mv = mem.take(6), mem.take(2)
        var_eps, rstd, neg_half = mem.take(1), mem.take(1), mem.take(1)
        nT = mem.take(KD, P)
        z_sb = mem.take(F)
        hT = mem.take(FC, P)
        f_sb = [mem.take(D) for _ in range(2)]
        g_sb = [mem.take(D) for _ in range(2)]
        gamma, beta = mem.take(E * KD), mem.take(E * KD)
        b1 = mem.take(E * FC)
        b2 = mem.take(E * D)
        turn_bank, z_bank, zT_bank, out_bank = bank[0], bank[1:3], bank[3:5], bank[5:7]

        small_in = sem("small_in")
        xs_in = [sem(f"xs_in{u}") for u in range(2)]
        var_done = sem("var_done")
        stat_step = sem("stat_step")
        rstd_done = sem("rstd_done")
        n_done = sem("n_done")
        n_turned = sem("n_turned")
        nT_done = sem("nT_done")
        z_mm = sem("z_mm")
        z_left = sem("z_left")
        z_right = sem("z_right")
        z_turned = sem("z_turned")
        h_left = sem("h_left")
        h_right = sem("h_right")
        out_mm = sem("out_mm")
        f_done = sem("f_done")
        g_done = sem("g_done")
        g_stored = [sem(f"g_stored{u}") for u in range(2)]

        PAIRS = (SLOTS - 1) // 2
        assert SLOTS == 2 * PAIRS + 1
        block = ctx.enter_context(nc.Block())

        def expert_of(engine, k):
            return engine.value_load(tile_expert[0:1, bass.ds(k, 1)], min_val=0, max_val=E - 1)

        @block.sync
        def _(sp):
            for dst, name in ((gamma, "gammaT"), (beta, "betaT"), (b1, "b1T")):
                sp.dma_start(dst, io[name][:, :]).then_inc(small_in, 16)
            sp.dma_start(b2[0:1, :], io["b2row"][:, :]).then_inc(small_in, 16)
            for k in range(2):
                sp.dma_start(xs[k], dram["sorted"][k * P:(k + 1) * P, :]).then_inc(xs_in[k], 16)

            def store(k, u):
                sp.wait_ge(g_done, k + 1 + 2)
                sp.dma_start(dram["g"][bass.ds(k * P, P), :], g_sb[u]).then_inc(g_stored[u], 16)

            with sp.Fori(0, PAIRS) as j:
                for u in range(2):
                    k = 2 * j + u
                    store(k, u)
                    sp.dma_start(xs[u], dram["sorted"][bass.ds((k + 2) * P, P), :]).then_inc(xs_in[u], 16)
            store(SLOTS - 1, 0)
            sp.wait_ge(xs_in[1], 16 * (PAIRS + 1))
            sp.wait_ge(g_stored[0], 16 * (PAIRS + 1) + 16)
            sp.wait_ge(g_stored[1], 16 * PAIRS + 16)

        @block.tensor
        def _(pe):
            ident = const[:, 0:P]
            ones_row = const[0:1, CONST["ones"][0]:CONST["ones"][0] + P]

            def front(k):
                e = expert_of(pe, k)
                pe.wait_ge(n_done, k + 1)
                for c in range(KD):
                    last = nc.tensor.transpose(turn_bank[:, c * P:(c + 1) * P], n_tok[:, c * P:(c + 1) * P], ident)
                last.then_inc(n_turned, 1)
                pe.wait_ge(nT_done, k + 1)
                for half in range(2):
                    for c in range(KD):
                        last = nc.tensor.matmul(z_bank[half][:, :], nT[:, c, :],
                                                w1s[:, bass.ds(e * (KD * F) + (c * F + half * 512), 512)],
                                                start=(c == 0), stop=(c == KD - 1))
                last.then_inc(z_mm, 1)

            def turn_z(k):
                for half in range(2):
                    pe.wait_ge(z_left if half == 0 else z_right, k + 1)
                    for c in range(4):
                        last = nc.tensor.transpose(zT_bank[half][:, c * P:(c + 1) * P],
                                                   z_sb[:, half * 512 + c * P:half * 512 + (c + 1) * P], ident)
                    last.then_inc(z_turned, 1)

            def back(k, u):
                e = expert_of(pe, k)
                pe.wait_ge(f_done, k + 1)
                nc.tensor.matmul(out_bank[u][:, 0:D], ones_row, b2[0:1, bass.ds(e * D, D)], start=True, stop=False)
                pe.wait_ge(h_left, k + 1)
                pe.wait_ge(h_right, k + 1)
                for c in range(FC):
                    last = nc.tensor.matmul(out_bank[u][:, 0:D], hT[:, c, :],
                                            w2s[:, bass.ds(e * (FC * D) + c * D, D)], start=False, stop=(c == FC - 1))
                last.then_inc(out_mm, 1)

            pe.wait_ge(ffn_loaded, 16 * 2 * E)
            pe.wait_ge(small_in, 64)
            front(0)
            with pe.Fori(0, PAIRS) as j:
                for u in range(2):
                    k = 2 * j + u
                    turn_z(k)
                    front(k + 1)
                    back(k, u)
            turn_z(SLOTS - 1)
            back(SLOTS - 1, 0)

        @block.scalar
        def _(act):
            act.sem_inc(g_done, 2)
            for u in range(2):
                act.sem_inc(g_stored[u], 16)

            def z_out(k):
                act.wait_ge(z_mm, k + 1)
                nc.scalar.activation(z_sb[:, 0:512], z_bank[0][:, :], ACT.Copy).then_inc(z_left, 1)

            def relu(k):
                e = expert_of(act, k)
                act.wait_ge(z_turned, 2 * k + 1)
                for c in range(4):
                    last = nc.scalar.activation(hT[:, c, :], zT_bank[0][:, c * P:(c + 1) * P], ACT.Relu,
                                                bias=b1[:, bass.ds(e * FC + c, 1)])
                last.then_inc(h_left, 1)

            def silu(k, j, u):
                act.wait_ge(g_stored[u], 16 * j + 16)
                act.wait_ge(f_done, k + 1 + 2)
                nc.scalar.activation(g_sb[u], f_sb[u], ACT.Silu).then_inc(g_done, 1)

            act.wait_ge(small_in, 64)
            z_out(0)
            with act.Fori(0, PAIRS) as j:
                for u in range(2):
                    k = 2 * j + u
                    relu(k)
                    z_out(k + 1)
                    silu(k, j, u)
            relu(SLOTS - 1)
            silu(SLOTS - 1, PAIRS, 0)

        @block.vector
        def _(v):
            v.sem_inc(f_done, 2)
            v.wait_ge(small_in, 64)

            def norm(k, loads, u):
                step = Steps(2 * k)
                e = expert_of(v, k)
                v.wait_ge(xs_in[u], 16 * loads)
                nc.vector.bn_stats(stats, xs[u][:, 0:D]).then_inc(stat_step, 1)
                v.wait_ge(stat_step, step.next())
                nc.vector.memset(var_eps, EPS)
                nc.vector.bn_aggr(mv, stats).then_inc(stat_step, 1)
                v.wait_ge(stat_step, step.next())
                nc.vector.tensor_scalar_add(var_eps, mv[:, 1:2], EPS).then_inc(var_done, 1)
                v.wait_ge(rstd_done, k + 1)
                nc.vector.tensor_scalar(n_tok, xs[u][:, 0:D], mv[:, 0:1], rstd, ALU.subtract, ALU.mult).then_inc(n_done, 1)
                v.wait_ge(n_turned, k + 1)
                for c in range(KD):
                    last = nc.vector.tensor_scalar(nT[:, c, :], turn_bank[:, c * P:(c + 1) * P], gamma[:, bass.ds(e * KD + c, 1)],
                                                   beta[:, bass.ds(e * KD + c, 1)], ALU.mult, ALU.add)
                last.then_inc(nT_done, 1)

            def z_out(k):
                v.wait_ge(z_mm, k + 1)
                nc.vector.tensor_copy(z_sb[:, 512:1024], z_bank[1][:, :]).then_inc(z_right, 1)

            def relu(k):
                e = expert_of(v, k)
                v.wait_ge(z_turned, 2 * k + 2)
                for c in range(4):
                    last = nc.vector.tensor_scalar(hT[:, 4 + c, :], zT_bank[1][:, c * P:(c + 1) * P],
                                                   b1[:, bass.ds(e * FC + (4 + c), 1)], 0.0, ALU.add, ALU.max)
                last.then_inc(h_right, 1)

            def finish(k, u):
                v.wait_ge(out_mm, k + 1)
                v.wait_ge(g_done, k + 1)
                nc.vector.scalar_tensor_tensor(f_sb[u], out_bank[u][:, 0:D], xs[u][:, D:D + 1], xs[u][:, 0:D],
                                               ALU.mult, ALU.add).then_inc(f_done, 1)

            norm(0, 1, 0)
            z_out(0)
            with v.Fori(0, PAIRS) as j:
                for u in range(2):
                    k = 2 * j + u
                    norm(k + 1, j + 1 + u, 1 - u)
                    relu(k)
                    z_out(k + 1)
                    finish(k, u)
            relu(SLOTS - 1)
            finish(SLOTS - 1, 0)

        @block.gpsimd
        def _(g):
            g.memset(neg_half, -0.5).then_inc(n_set := sem("neg_set"), 1)
            g.wait_ge(n_set, 1)
            with g.Fori(0, SLOTS) as k:
                g.wait_ge(var_done, k + 1)
                nc.gpsimd.tensor_tensor(rstd, var_eps, neg_half, ALU.pow).then_inc(rstd_done, 1)


PAIR = {"r": (0, 0), "k": (0, 64), "v": (1, 0), "g": (1, 64), "d": (2, 0)}
MIX_ORDER = "drkvg"
HEADS_PER_TILE = 2
HGROUP = 4
STEPS = NH * NT
UNITS = KD * HD
LAG = 3
PROBS = 3
PRODS = 6


class Outputs:

    def __init__(self, table, nbank):
        self.at = {name: n for n, (name, _) in enumerate(table)}
        self.reader = {name: who for name, who in table}
        self.n = len(table)
        self.names = [name for name, _ in table]
        self.order = {who: [x for x, w in table if w == who] for who in "avh"}
        self.nbank = nbank

    def bank(self, name):
        return self.at[name] % self.nbank

    def before(self, name):
        n = self.at[name] - self.nbank
        return self.names[n] if n >= 0 else None

    def made(self, b, name):
        return self.n * b + (self.at[name] + 1)

    def read(self, b, name):
        mine = self.order[self.reader[name]]
        return len(mine) * b + (mine.index(name) + 2)


PRE = ([("t0", "v"), ("t1", "a"), ("la_rk", "a"), ("la_vg", "a"), ("la_d", "a"),
        ("lb_d0", "v"), ("lb_d1", "v"), ("lb_r0", "v"), ("lb_r1", "v"), ("la_dd", "a"), ("lb_k0", "v"), ("lb_k1", "v"),
        ("pr_r0", "a"), ("pr_r1", "a"), ("lb_v0", "v"), ("lb_v1", "v"), ("pr_k0", "a"), ("pr_k1", "a"),
        ("lb_g0", "v"), ("lb_g1", "v"), ("pr_v0", "a"), ("pr_v1", "a"), ("lb_w0", "a"), ("lb_w1", "a"),
        ("pr_g0", "a"), ("pr_g1", "a"), ("xb0", "v"), ("xb1", "a"), ("ckv", "v")]
       + [(f"q{i}", "v") for i in range(NH // HEADS_PER_TILE)] + [("sp0", "v"), ("sp1", "v")]
       + [(f"k{i}", "a") for i in range(NH // HEADS_PER_TILE)] + [(f"v{i}", "a") for i in range(NT)])
def _experts():
    for e in range(ME + 2):
        if e <= ME:
            yield from ((f"g{e}", "a"), (f"u{e}", "h"))
        if e:
            yield from ((f"d{e - 1}a", "v"), (f"d{e - 1}b", "v"))


POST = ([("mean0", "v"), ("mean1", "v"), ("wo0", "v"), ("wo1", "v"), ("var0", "v"), ("var1", "v"),
         ("xc0", "v"), ("xc1", "a"), ("gate", "v")] + list(_experts()) + [("o0", "v"), ("o1", "v")])


def phase_c(nc, io, dram, mem, const, bank, pos_all, out):
    with ExitStack() as ctx:
        def sem(name):
            return ctx.enter_context(nc.semaphore("c_" + name))

        pre, post = Outputs(PRE, 8), Outputs(POST, 8)
        tail = mem.take(NCONST - NCONST_A)

        def table(name):
            at = CONST[name][0] - NCONST_A
            return tail[:, at:at + CONST[name][1]]

        sel, red = table("sel").rearrange("p (j c) -> p j c", j=HD), table("red").rearrange("p (g c) -> p g c", c=32)
        spread, mean_m, mask, cos, sin = (table(x) for x in ("spread", "mean", "mask", "cos", "sin"))
        rkvg_w = {x: mem.take(KD, D) for x in "rkvg"}
        o_w = mem.take(KD, D)
        la_w = mem.take(KD, 5 * LORA)
        lb_w = mem.take(3, D)
        vecs = mem.take(io["vecs"].shape[1])
        VEC = {}
        at = 0
        for name, n in (("ll_r", KD), ("ll_k", KD), ("ll_v", KD), ("ll_g", KD), ("ll_d", KD), ("xw", KD), ("u", KD),
                        ("init", KD * HD), ("ln_w", 1), ("ln_b", 1), ("w_ln1", KD), ("w_ln2", KD)):
            VEC[name] = vecs[:, at:at + n]
            at += n
        q_w = mem.take(KD, NH * 64)
        kva_w = mem.take(KD, ND + RD)
        kbuild = mem.take(NH // HEADS_PER_TILE, P)
        kvb_w = mem.take(NH * ND)
        wo_w = mem.take(NH // HGROUP, D)
        gate_w = mem.take(KD, ME)
        gate_b = mem.take(ME)
        eg_w = [mem.take(KD, MI) for _ in range(ME + 1)]
        eu_w = [mem.take(KD, MI) for _ in range(ME + 1)]
        ed_w = [mem.take(D) for _ in range(ME + 1)]
        mask_b = mem.take(P // 2).bitcast(BF16)
        ident_b = mem.take(P // 2).bitcast(BF16)
        x2, xn = mem.take(NT, D), mem.take(NT, D)
        proj = {x: mem.take(KD, T) for x in "rkvgw"}
        bonus = mem.take(KD, T)
        prods_at = mem.at
        prods = [mem.take(T) for _ in range(PRODS)]
        kv = mem.take(T)
        state_at = mem.at
        state = [mem.take(T + 1) for _ in range(2)]
        probs_at = mem.at
        probs = [mem.take(T) for _ in range(PROBS)]
        qT, kT = mem.take(NH // 2, T), mem.take(NH // 2, T)
        v_tok = mem.take(NT, NH * ND)
        turned_at = mem.at
        turned = [mem.take(NT, T) for _ in range(HGROUP)]
        neg_max, row_sum, row_inv = mem.take(STEPS), mem.take(STEPS), mem.take(STEPS)
        stats, mv = mem.take(NT, 6), mem.take(NT, 2)
        var_eps, rstd, ssq, rms = mem.take(NT), mem.take(NT), mem.take(NT), mem.take(NT)
        neg_half = mem.take(NT)
        idx = mem.take(NT).bitcast(U32)
        waste = mem.take(NT)
        logits = mem.take(NT, ME)
        route = [mem.take(NT, ME) for _ in range(4)]
        routs = [mem.take(NT) for _ in range(6)]
        early = Arena(mem.tensor, turned_at)
        x_in, s_in, g_in = early.take(NT, D), early.take(NT, D), early.take(NT, D)
        xnT, dxT, lerp = early.take(KD, T), early.take(KD, T), early.take(KD, T)
        mix = [early.take(KD, T) for _ in range(2)]
        early = Arena(mem.tensor, probs_at)
        th = [early.take(T) for _ in range(3)]
        silu_g = [th[0], th[1]]
        hid = [th[2], kv]
        early = Arena(mem.tensor, prods_at)
        xb = early.take(NT, D)
        xbT = early.take(KD, T)
        acc_at = early.at
        shuf = [early.take(T) for _ in range(2)]
        acc = Arena(mem.tensor, acc_at).take(NT, D)
        ckvT = Arena(mem.tensor, state_at).take(T)
        yT = [qT[:, 2 * i, :] for i in range(NH // HGROUP)]
        y = proj["r"]
        sq, inv = proj["v"], proj["k"]

        weights_in, ready_b = sem("weights_in"), sem("ready_b")
        kb_step = sem("kb_step")
        x_loaded, g_loaded, idx_set = sem("x_loaded"), sem("g_loaded"), sem("idx_set")
        stored = sem("stored")
        made = sem("made")
        made2 = sem("made2")
        a_read, v_read = sem("a_read"), sem("v_read")
        a_read2, v_read2 = sem("a_read2"), sem("v_read2")
        x2_step = sem("x2_step")
        var_done, rstd_done = sem("var_done"), sem("rstd_done")
        xn_done, ssq_done, ms_done, rms_done, xb_done = (sem(x) for x in ("xn_done", "ssq_done", "ms_done", "rms_done", "xb_done"))
        dx_step, lerp_done = sem("dx_step"), sem("lerp_done")
        mixed = sem("mixed")
        w_step = sem("w_step")
        turned_q = sem("turned_q")
        rope_step, rope_mul, init_set, pool_set = sem("rope_step"), sem("rope_mul"), sem("init_set"), sem("pool_set")
        ruk_done = sem("ruk_done")
        bonus_done = sem("bonus_done")
        (s_mm, s_max, s_exp, s_inv, s_norm, s_turn, s_keep, vrep, kv_done, scan_done, prod_done, red_mm, y_read, pv_mm,
         y_out) = (sem(x) for x in ("score_mm", "max", "exp", "rowinv", "norm", "turn", "keep", "vrep", "kv", "scan", "prod",
                                    "red", "y_read", "pv_mm", "y_out"))
        sq_done, inv_done, ln_step, o_done = (sem(x) for x in ("sq", "inv", "ln_step", "o_done"))
        gsilu = sem("gsilu")
        ssq2_done, ms2_done, rms2_done, xc_done = (sem(x) for x in ("ssq2", "ms2", "rms2", "xc"))
        top_step, comb_in, comb_out, comb_done = sem("top_step"), sem("comb_in"), sem("comb_out"), sem("comb_done")
        hid_done = sem("hid")
        f_done, out_ready = sem("f_done"), sem("out_ready")

        block = ctx.enter_context(nc.Block())
        NW = 17 + 3 * (ME + 1)

        @block.sync
        def _(sp):
            def load(dst, src):
                sp.dma_start(dst, src).then_inc(weights_in, 16)

            load(tail, io["const"][:, NCONST_A:NCONST])
            load(vecs, io["vecs"][:, :])
            load(la_w, io["laT"].rearrange("(k p) n -> p k n", p=P))
            load(lb_w, io["lbT"].rearrange("(g p) n -> p g n", p=P))
            for x in "rkvg":
                load(rkvg_w[x], io[x + "WT"].rearrange("(k p) n -> p k n", p=P))
            load(q_w, io["L1_ffn_Wq"].rearrange("(k p) n -> p k n", p=P))
            load(kva_w, io["L1_ffn_Wkva"].rearrange("(k p) n -> p k n", p=P))
            load(kvb_w[0:ND, :], io["L1_ffn_Wkvb"][:, :])
            sp.wait_ge(kb_step, 1)
            for h in range(HEADS_PER_TILE):
                load(kbuild[0:ND, :, 64 * h:64 * h + ND],
                     io["L1_ffn_Wkvb"].rearrange("p (t h n) -> p t h n", h=2, n=ND)[:, :, h, :])
            load(o_w, io["oWT"].rearrange("(k p) n -> p k n", p=P))
            load(wo_w, io["Wo"].rearrange("(g p) n -> p g n", p=P))
            load(gate_w, io["L1_ffn_Wgate"].rearrange("(k p) n -> p k n", p=P))
            load(gate_b, io["gate_b"][:, :].broadcast_to([P, ME]))
            for e in range(ME + 1):
                wg, wu, wd = ((io["L1_ffn_" + x][e] if e < ME else io["L1_ffn_s" + x][0]) for x in ("Wg", "Wu", "Wd"))
                load(eg_w[e], wg.rearrange("(k p) n -> p k n", p=P))
                load(eu_w[e], wu.rearrange("(k p) n -> p k n", p=P))
                load(ed_w[e], wd)
            x_rows = io["L0_attn_h"].rearrange("b t d -> (b t) d")
            out_rows = out.rearrange("b t d -> (b t) d")

            def load_sequence(b):
                sp.dma_start(x_in, x_rows[bass.ds(b * T, T), :].rearrange("(i p) d -> p i d", p=P)).then_inc(x_loaded, 16)
                sp.dma_start(s_in, dram["s"][bass.ds(b * T, T), :].rearrange("(i p) d -> p i d", p=P)).then_inc(x_loaded, 16)

            def store_sequence(b):
                sp.wait_ge(out_ready, b + 1)
                sp.dma_start(out_rows[bass.ds(b * T, T), :].rearrange("(i p) d -> p i d", p=P), x2).then_inc(stored, 16)

            load_sequence(0)
            with sp.Fori(0, B - 1) as b:
                sp.wait_ge(pv_mm, 4 * b + 4 + 4)
                load_sequence(b + 1)
                store_sequence(b)
            store_sequence(B - 1)
            sp.wait_ge(stored, 16 * B + 16)

        @block.tensor
        def _(pe):
            ident = const[:, 0:P]

            def begin(b, name, table, sems):
                old = table.before(name)
                if old is not None:
                    pe.wait_ge(sems[table.reader[old]], table.read(b, old))

            pre_read, post_read = {"a": a_read, "v": v_read}, {"a": a_read2, "v": v_read2, "h": hid_done}

            def product(b, name, pairs, width=T, rows=P):
                begin(b, name, pre, pre_read)
                dst = bank[pre.bank(name)]
                for n, (w, x) in enumerate(pairs):
                    last = nc.tensor.matmul(dst[0:rows, 0:width], w, x, start=(n == 0), stop=(n == len(pairs) - 1))
                last.then_inc(made, 1)

            def turn(dst, src, name, b, table, sems, signal):
                begin(b, name, table, sems)
                for i in range(NT):
                    last = nc.tensor.transpose(dst[:, i * P:(i + 1) * P], src(i), ident)
                last.then_inc(signal, 1)

            def lora_b(b, x, name, th_tile):
                g, r0 = PAIR[x]
                for m in range(KD):
                    product(b, f"lb_{name}{m}", [(lb_w[r0:r0 + LORA, g, m * P:(m + 1) * P], th_tile[r0:r0 + LORA, :])])

            def project(b, x):
                src = mix[MIX_ORDER.index(x) % 2]
                pe.wait_ge(mixed, 10 * b + 2 * MIX_ORDER.index(x) + 2)
                for m in range(KD):
                    product(b, f"pr_{x}{m}", [(rkvg_w[x][:, k, m * P:(m + 1) * P], src[:, k, :]) for k in range(KD)])

            def scores(b, s):
                h, qt = s // NT, s % NT
                dst, rows, n = bank[3 + s % 2], 64 * (h % 2), (qt + 1) * P
                if s >= 2:
                    pe.wait_ge(s_exp, STEPS * b + (s - 1))
                nc.tensor.matmul(dst[:, 0:n], qT[rows:rows + 64, h // 2, qt * P:(qt + 1) * P], kT[rows:rows + 64, h // 2, 0:n],
                                 start=True, stop=False)
                nc.tensor.matmul(dst[:, qt * P:n], ident_b, mask_b, start=False, stop=True).then_inc(s_mm, 1)

            def turn_probs(b, s):
                qt = s % NT
                pe.wait_ge(s_norm, STEPS * b + (s + 1))
                if s >= 2:
                    pe.wait_ge(s_keep, STEPS * b + (s - 1))
                for kt in range(qt + 1):
                    last = nc.tensor.transpose(bank[5 + s % 2][:, kt * P:(kt + 1) * P], probs[s % PROBS][:, kt * P:(kt + 1) * P], ident)
                last.then_inc(s_turn, 1)

            def replicate_v(b, n):
                if n >= 2:
                    pe.wait_ge(kv_done, UNITS * b + (n - 1))
                nc.tensor.matmul(bank[n % 2][:, :], sel[:, n % HD, :], proj["v"][:, n // HD, :], start=True, stop=True).then_inc(vrep, 1)

            def reduce_state(b, g):
                pe.wait_ge(prod_done, UNITS * b + (4 * g + 4))
                if g == 4:
                    pe.wait_ge(y_read, 2 * b + 1)
                for q in range(4):
                    last = nc.tensor.matmul(bank[2][32 * q:32 * q + 32, :], red[:, g % 4, :], prods[(4 * g + q) % PRODS],
                                            start=(g % 4 == 0), stop=(g % 4 == 3))
                last.then_inc(red_mm, 1)

            def weigh_values(b, g):
                pe.wait_ge(s_keep, STEPS * b + 4 * NT * (g + 1))
                if g:
                    pe.wait_ge(y_out, 4 * b + g)
                for kt in range(NT):
                    for i in range(HGROUP):
                        h = HGROUP * g + i
                        last = nc.tensor.matmul(bank[7][32 * i:32 * i + 32, kt * P:T], v_tok[:, kt, h * ND:(h + 1) * ND],
                                                turned[i][:, kt, kt * P:T], start=(kt == 0), stop=(kt == NT - 1))
                last.then_inc(pv_mm, 1)

            pe.wait_ge(weights_in, 16 * NW)
            pe.wait_ge(ready_b, 4)
            pe.sem_inc(pv_mm, NH // HGROUP)
            with pe.Fori(0, B) as b:
                pe.wait_ge(a_read2, len(post.order["a"]) * b + 1)
                pe.wait_ge(v_read2, len(post.order["v"]) * b + 1)
                pe.wait_ge(xn_done, b + 1)
                for k in range(KD):
                    turn(bank[pre.bank(f"t{k}")], lambda i: xn[:, i, k * P:(k + 1) * P], f"t{k}", b, pre, pre_read, made)
                pe.wait_ge(lerp_done, b + 1)
                for name, at, n in (("rk", 0, 2), ("vg", 2, 2), ("d", 4, 1)):
                    product(b, "la_" + name, [(la_w[:, k, at * LORA:(at + n) * LORA], lerp[:, k, :]) for k in range(KD)],
                            rows=n * LORA)
                pe.wait_ge(a_read, pre.read(b, "la_d"))
                lora_b(b, "d", "d", th[2])
                lora_b(b, "r", "r", th[0])
                pe.wait_ge(mixed, 10 * b + 2)
                product(b, "la_dd", [(la_w[:, k, 4 * LORA:5 * LORA], mix[0][:, k, :]) for k in range(KD)], rows=LORA)
                lora_b(b, "k", "k", th[0])
                project(b, "r")
                lora_b(b, "v", "v", th[1])
                project(b, "k")
                lora_b(b, "g", "g", th[1])
                project(b, "v")
                pe.wait_ge(a_read, pre.read(b, "la_dd"))
                lora_b(b, "d", "w", th[2])
                project(b, "g")
                pe.wait_ge(xb_done, b + 1)
                for k in range(KD):
                    turn(bank[pre.bank(f"xb{k}")], lambda i: xb[:, i, k * P:(k + 1) * P], f"xb{k}", b, pre, pre_read, made)
                pe.wait_ge(v_read, pre.read(b, "xb0"))
                pe.wait_ge(a_read, pre.read(b, "xb1"))
                product(b, "ckv", [(kva_w[:, k, :], xbT[:, k, :]) for k in range(KD)], rows=ND + RD)
                for i in range(NH // 2):
                    product(b, f"q{i}", [(q_w[:, k, i * P:(i + 1) * P], xbT[:, k, :]) for k in range(KD)])
                pe.wait_ge(ruk_done, 2 * b + 2)
                for m in range(KD):
                    product(b, f"sp{m}", [(spread, bonus[:, m, :])])
                pe.wait_ge(turned_q, 9 * b + 1)
                for i in range(NH // 2):
                    product(b, f"k{i}", [(kbuild[0:64, i, :], ckvT[0:64, :])])
                for i in range(NT):
                    product(b, f"v{i}", [(ckvT[0:ND, i * P:(i + 1) * P], kvb_w[0:ND, :])])
                pe.wait_ge(a_read, pre.read(b, f"v{NT - 1}"))
                pe.wait_ge(v_read, pre.read(b, "sp1"))
                pe.wait_ge(turned_q, 9 * b + 9)
                for s in range(STEPS + LAG + 2):
                    if s < STEPS:
                        scores(b, s)
                        if s % 2 == 0:
                            replicate_v(b, s // 2)
                    if s >= 16 + LAG and (s - LAG) % 16 == 0:
                        weigh_values(b, (s - LAG) // 16 - 1)
                    if LAG <= s < STEPS + LAG:
                        turn_probs(b, s - LAG)
                    if s >= 10 and (s - 10) % 8 == 0 and (s - 10) // 8 < 8:
                        reduce_state(b, (s - 10) // 8)
                def result(name, pairs, dst):
                    begin(b, name, post, post_read)
                    for n, (o, w, x, first, last_one) in enumerate(pairs):
                        last = nc.tensor.matmul(dst[o], w, x, start=first, stop=last_one)
                    last.then_inc(made2, 1)

                pe.wait_ge(y_out, 4 * b + 4)
                pe.wait_ge(y_read, 2 * b + 2)
                full = slice(None), slice(0, T)
                for m in range(KD):
                    result(f"mean{m}", [(full, mean_m, y[:, m, :], True, True)], bank[post.bank(f"mean{m}")])

                def by_tokens(name, tiles, lhs, rhs, n):
                    result(name, [((slice(None), slice((i % 2) * D, (i % 2 + 1) * D)), lhs(i, c), rhs(c), c == 0, c == n - 1)
                                  for i in tiles for c in range(n)], bank[post.bank(name)])

                for half in range(2):
                    by_tokens(f"wo{half}", (2 * half, 2 * half + 1), lambda i, c: yT[c][:, i * P:(i + 1) * P],
                              lambda c: wo_w[:, c, :], NH // HGROUP)
                pe.wait_ge(sq_done, 2 * b + 2)
                for m in range(KD):
                    result(f"var{m}", [(full, mean_m, sq[:, m, :], True, True)], bank[post.bank(f"var{m}")])
                pe.wait_ge(xc_done, b + 1)
                for k in range(KD):
                    turn(bank[post.bank(f"xc{k}")], lambda i: xb[:, i, k * P:(k + 1) * P], f"xc{k}", b, post, post_read, made2)
                pe.wait_ge(v_read2, post.read(b, "xc0"))
                pe.wait_ge(a_read2, post.read(b, "xc1"))
                result("gate", [((slice(None), slice(i * ME, (i + 1) * ME)), xbT[:, k, i * P:(i + 1) * P], gate_w[:, k, :],
                                 k == 0, k == KD - 1) for i in range(NT) for k in range(KD)], bank[post.bank("gate")])

                def up(e):
                    for x, w in (("g", eg_w[e]), ("u", eu_w[e])):
                        result(f"{x}{e}", [(full, w[:, k, :], xbT[:, k, :], k == 0, k == KD - 1) for k in range(KD)],
                               bank[post.bank(f"{x}{e}")])

                def down(e):
                    pe.wait_ge(hid_done, post.read(b, f"u{e}"))
                    for half, name in enumerate("ab"):
                        by_tokens(f"d{e}{name}", (2 * half, 2 * half + 1), lambda i, c: hid[e % 2][:, i * P:(i + 1) * P],
                                  lambda c: ed_w[e], 1)

                for e in range(ME + 2):
                    if e <= ME:
                        up(e)
                    if e:
                        down(e - 1)
                pe.wait_ge(o_done, 2 * b + 2)
                for half in range(2):
                    by_tokens(f"o{half}", (2 * half, 2 * half + 1), lambda i, c: y[:, c, i * P:(i + 1) * P],
                              lambda c: o_w[:, c, :], KD)

        @block.scalar
        def _(act):
            act.sem_inc(a_read, 1)
            act.sem_inc(a_read2, 1)
            act.sem_inc(stored, 16)
            act.wait_ge(weights_in, 16 * NW)
            with act.Fori(0, B) as b:
                def take(name, dst, func, **kw):
                    act.wait_ge(made, pre.made(b, name))
                    rows = dst.shape[0]
                    return nc.scalar.activation(dst, bank[pre.bank(name)][0:rows, :], func, **kw)

                act.wait_ge(xn_done, b + 1)
                for i in range(NT):
                    last = nc.scalar.activation(xb[:, i, :], xn[:, i, :], ACT.Square, accum_out=ssq[:, i:i + 1])
                last.then_inc(ssq_done, 1)
                take("t1", xnT[:, 1, :], ACT.Copy).then_inc(a_read, 1)
                for n, name in enumerate(("rk", "vg")):
                    take("la_" + name, th[n], ACT.Tanh).then_inc(a_read, 1)
                take("la_d", th[2][0:LORA, :], ACT.Tanh).then_inc(a_read, 1)
                act.wait_ge(made, pre.made(b, "lb_d1"))
                take("la_dd", th[2][0:LORA, :], ACT.Tanh).then_inc(a_read, 1)
                for x in "rkv":
                    for m in range(KD):
                        take(f"pr_{x}{m}", proj[x][:, m, :], ACT.Copy).then_inc(a_read, 1)
                    if x == "v":
                        for m in range(KD):
                            take(f"lb_w{m}", proj["w"][:, m, :], ACT.Exp, bias=VEC["ll_d"][:, m:m + 1]).then_inc(a_read, 1)
                            act.wait_ge(a_read, pre.read(b, f"lb_w{m}"))
                            nc.scalar.activation(proj["w"][:, m, :], proj["w"][:, m, :], ACT.Exp, scale=-1.0).then_inc(w_step, 1)
                for m in range(KD):
                    take(f"pr_g{m}", proj["g"][:, m, :], ACT.Copy).then_inc(a_read, 1)
                take("xb1", xbT[:, 1, :], ACT.Copy, scale=VEC["w_ln1"][:, 1:2]).then_inc(a_read, 1)
                for i in range(NH // 2):
                    take(f"k{i}", kT[:, i, :], ACT.Copy, scale=0.125).then_inc(a_read, 1)
                for i in range(NT):
                    take(f"v{i}", v_tok[:, i, :], ACT.Copy).then_inc(a_read, 1)

                def exp(s):
                    n = (s % NT + 1) * P
                    act.wait_ge(s_max, STEPS * b + (s + 1))
                    if s >= PROBS:
                        act.wait_ge(s_turn, STEPS * b + (s - PROBS + 1))
                    nc.scalar.activation(probs[s % PROBS][:, 0:n], bank[3 + s % 2][:, 0:n], ACT.Exp, bias=neg_max[:, s:s + 1],
                                         accum_out=row_sum[:, s:s + 1]).then_inc(s_exp, 1)

                def keep(s):
                    h, qt = s // NT, s % NT
                    act.wait_ge(s_turn, STEPS * b + (s + 1))
                    if h >= HGROUP and s % (HGROUP * NT) == 0:
                        act.wait_ge(pv_mm, 4 * b + h // HGROUP + 4)
                    nc.scalar.activation(turned[h % HGROUP][:, 0:qt + 1, qt * P:(qt + 1) * P],
                                         bank[5 + s % 2][:, 0:(qt + 1) * P].rearrange("p (k c) -> p k c", c=P),
                                         ACT.Copy).then_inc(s_keep, 1)

                for s in range(STEPS + LAG + 2):
                    if s >= 16 + LAG + 1 and (s - LAG - 1) % 16 == 0:
                        g = (s - LAG - 1) // 16 - 1
                        act.wait_ge(pv_mm, 4 * b + g + 5)
                        nc.scalar.activation(yT[g], bank[7][:, :], ACT.Copy).then_inc(y_out, 1)
                    if LAG < s <= STEPS + LAG:
                        keep(s - LAG - 1)
                    if s < STEPS:
                        exp(s)

                def take2(name, dst, func, **kw):
                    act.wait_ge(made2, post.made(b, name))
                    return nc.scalar.activation(dst, bank[post.bank(name)][:, :], func, **kw)

                for m in range(KD):
                    act.wait_ge(v_read2, post.read(b, f"var{m}"))
                    nc.scalar.activation(inv[:, m, :], inv[:, m, :], ACT.Sqrt).then_inc(inv_done, 1)
                for m in range(KD):
                    nc.scalar.activation(proj["g"][:, m, :], proj["g"][:, m, :], ACT.Silu).then_inc(gsilu, 1)
                act.wait_ge(v_read2, post.read(b, "wo1"))
                for i in range(NT):
                    last = nc.scalar.activation(xb[:, i, :], xn[:, i, :], ACT.Square, accum_out=ssq[:, i:i + 1])
                last.then_inc(ssq2_done, 1)
                take2("xc1", xbT[:, 1, :], ACT.Copy, scale=VEC["w_ln2"][:, 1:2]).then_inc(a_read2, 1)
                act.wait_ge(comb_in, 2 * b + 2)
                nc.scalar.activation(routs[4], routs[4], ACT.Tanh, scale=0.5).then_inc(comb_out, 1)
                take2("g0", silu_g[0], ACT.Silu).then_inc(a_read2, 1)
                take2("g1", silu_g[1], ACT.Silu).then_inc(a_read2, 1)
                for e in range(2, ME + 1):
                    act.wait_ge(hid_done, post.read(b, f"u{e - 2}"))
                    take2(f"g{e}", silu_g[e % 2], ACT.Silu).then_inc(a_read2, 1)
                act.wait_ge(v_read2, post.read(b, f"d{ME}b"))
                nc.scalar.activation(acc, acc, ACT.Silu).then_inc(f_done, 1)

        @block.vector
        def _(v):
            v.memset(kbuild[0:64, :, :], 0.0).then_inc(kb_step, 1)
            v.wait_ge(kb_step, 1)
            for h in range(HEADS_PER_TILE):
                v.tensor_copy(kbuild[ND:64, :, 64 * h + ND:64 * h + 64],
                              const[ND:64, ND:64].rearrange("p (o n) -> p o n", o=1).broadcast_to([RD, NH // 2, RD])).then_inc(ready_b, 1)
            v.sem_inc(v_read, 1)
            v.sem_inc(v_read2, 1)
            v.sem_inc(hid_done, 1)
            v.wait_ge(weights_in, 16 * NW)
            v.tensor_copy(mask_b, mask).then_inc(ready_b, 1)
            v.tensor_copy(ident_b, const[:, 0:P]).then_inc(ready_b, 1)
            with v.Fori(0, B) as b:
                step = Steps(4 * b)
                v.wait_ge(x_loaded, 32 * b + 32)
                v.wait_ge(g_loaded, 64 * b + 64)
                nc.vector.tensor_tensor(s_in, s_in, g_in, ALU.mult).then_inc(x2_step, 1)
                v.wait_ge(stored, 16 * b + 16)
                v.wait_ge(x2_step, step.next())
                nc.vector.tensor_tensor(x2, x_in, s_in, ALU.add).then_inc(x2_step, 1)
                v.wait_ge(x2_step, step.next())
                for i in range(NT):
                    last = nc.vector.bn_stats(stats[:, i, :], x2[:, i, :])
                last.then_inc(x2_step, 1)
                v.wait_ge(x2_step, step.next())
                nc.vector.memset(var_eps, EPS)
                for i in range(NT):
                    last = nc.vector.bn_aggr(mv[:, i, :], stats[:, i, :])
                last.then_inc(x2_step, 1)
                v.wait_ge(x2_step, step.next())
                nc.vector.tensor_scalar_add(var_eps, mv[:, :, 1], EPS).then_inc(var_done, 1)
                v.wait_ge(rstd_done, b + 1)
                for i in range(NT):
                    last = nc.vector.tensor_scalar(xn[:, i, :], x2[:, i, :], mv[:, i, 0:1], rstd[:, i:i + 1], ALU.subtract, ALU.mult)
                last.then_inc(xn_done, 1)
                v.wait_ge(made, pre.made(b, "t0"))
                nc.vector.tensor_copy(xnT[:, 0, :], bank[pre.bank("t0")][:, :]).then_inc(v_read, 1)
                v.wait_ge(v_read, pre.read(b, "t0"))
                v.wait_ge(a_read, pre.read(b, "t1"))
                nc.vector.tensor_scalar_mul(dxT[:, :, 0:1], xnT[:, :, 0:1], -1.0).then_inc(dx_step, 1)
                nc.vector.tensor_tensor(dxT[:, :, 1:T], xnT[:, :, 0:T - 1], xnT[:, :, 1:T], ALU.subtract).then_inc(dx_step, 1)
                v.wait_ge(dx_step, 2 * b + 2)
                for k in range(KD):
                    last = nc.vector.scalar_tensor_tensor(lerp[:, k, :], dxT[:, k, :], VEC["xw"][:, k:k + 1], xnT[:, k, :],
                                                          ALU.mult, ALU.add)
                last.then_inc(lerp_done, 1)
                v.wait_ge(ssq_done, b + 1)
                nc.vector.tensor_scalar(ssq, ssq, 1.0 / D, EPS, ALU.mult, ALU.add).then_inc(ms_done, 1)
                v.wait_ge(rms_done, b + 1)
                for i in range(NT):
                    last = nc.vector.tensor_scalar_mul(xb[:, i, :], xn[:, i, :], rms[:, i:i + 1])
                last.then_inc(xb_done, 1)
                for n, x in enumerate(MIX_ORDER):
                    if x == "k":
                        v.wait_ge(made, pre.made(b, "la_dd"))
                    elif n >= 2:
                        v.wait_ge(made, pre.made(b, f"pr_{MIX_ORDER[n - 2]}1"))
                    for m in range(KD):
                        name = f"lb_{x}{m}"
                        v.wait_ge(made, pre.made(b, name))
                        nc.vector.scalar_tensor_tensor(mix[n % 2][:, m, :], bank[pre.bank(name)][:, :], VEC["ll_" + x][:, m:m + 1],
                                                       dxT[:, m, :], ALU.add, ALU.mult).then_inc(v_read, 1)
                v.wait_ge(made, pre.made(b, "xb0"))
                nc.vector.tensor_scalar_mul(xbT[:, 0, :], bank[pre.bank("xb0")][:, :], VEC["w_ln1"][:, 0:1]).then_inc(v_read, 1)
                swap = [i ^ 1 for i in range(32)]
                for n in range(1 + NH // 2):
                    name, rows = ("ckv", 64) if n == 0 else (f"q{n - 1}", P)
                    dst = ckvT if n == 0 else qT[:, n - 1, :]
                    src = bank[pre.bank(name)]
                    v.wait_ge(made, pre.made(b, name))
                    if n >= 2:
                        v.wait_ge(turned_q, 9 * b + (n - 1))
                    nc.vector.tensor_tensor(dst[0:rows, :], src[0:rows, :], cos[0:rows, :], ALU.mult).then_inc(rope_step, 1)
                    nc.vector.stream_shuffle(shuf[n % 2][0:rows, :], src[0:rows, :], swap).then_inc(v_read, 1)
                v.wait_ge(a_read, pre.read(b, "pr_k1"))
                for m in range(KD):
                    nc.vector.scalar_tensor_tensor(bonus[:, m, :], proj["r"][:, m, :], VEC["u"][:, m:m + 1], proj["k"][:, m, :],
                                                   ALU.mult, ALU.mult).then_inc(ruk_done, 1)
                for m in range(KD):
                    v.wait_ge(made, pre.made(b, f"sp{m}"))
                    v.wait_ge(a_read, pre.read(b, f"pr_v{m}"))
                    nc.vector.tensor_tensor(bonus[:, m, :], bank[pre.bank(f"sp{m}")][:, :], proj["v"][:, m, :], ALU.mult).then_inc(v_read, 1)
                v.wait_ge(w_step, 2 * b + 2)

                def highest(s):
                    n = (s % NT + 1) * P
                    v.wait_ge(s_mm, STEPS * b + (s + 1))
                    nc.vector.tensor_reduce(neg_max[:, s:s + 1], bank[3 + s % 2][:, 0:n], X, ALU.max, negate=True).then_inc(s_max, 1)

                def invert(s):
                    v.wait_ge(s_exp, STEPS * b + (s + 1))
                    nc.vector.reciprocal(row_inv[:, s:s + 1], row_sum[:, s:s + 1]).then_inc(s_inv, 1)

                def outer(n):
                    v.wait_ge(vrep, UNITS * b + (n + 1))
                    if n:
                        v.wait_ge(scan_done, UNITS * b + n)
                    nc.vector.tensor_tensor(kv, bank[n % 2][:, :], proj["k"][:, n // HD, :], ALU.mult).then_inc(kv_done, 1)

                def scan(n):
                    m, j = n // HD, n % HD
                    v.wait_ge(kv_done, UNITS * b + (n + 1))
                    if n >= 2:
                        v.wait_ge(prod_done, UNITS * b + (n - 1))
                    nc.vector.tensor_tensor_scan(state[n % 2][:, 1:T + 1], proj["w"][:, m, :], kv,
                                                 VEC["init"][:, m * HD + j:m * HD + j + 1], ALU.mult, ALU.add).then_inc(scan_done, 1)

                def read_out(m):
                    v.wait_ge(red_mm, 8 * b + (4 * m + 4))
                    nc.vector.tensor_tensor(y[:, m, :], bank[2][:, :], bonus[:, m, :], ALU.add).then_inc(y_read, 1)

                for s in range(STEPS + LAG + 2):
                    if s < STEPS:
                        highest(s)
                    if 1 <= s <= STEPS:
                        invert(s - 1)
                    if s < STEPS:
                        outer(s // 2) if s % 2 == 0 else scan(s // 2)
                    if s in (35, 67):
                        read_out((s - 35) // 32)

                for m in range(KD):
                    v.wait_ge(made2, post.made(b, f"mean{m}"))
                    nc.vector.tensor_tensor(y[:, m, :], y[:, m, :], bank[post.bank(f"mean{m}")][:, :], ALU.subtract).then_inc(v_read2, 1)
                for half in range(2):
                    v.wait_ge(made2, post.made(b, f"wo{half}"))
                    nc.vector.tensor_tensor(xn[:, 2 * half:2 * half + 2, :], xn[:, 2 * half:2 * half + 2, :],
                                            bank[post.bank(f"wo{half}")][:, :].rearrange("p (i d) -> p i d", i=2), ALU.add).then_inc(v_read2, 1)
                for m in range(KD):
                    v.wait_ge(made2, post.made(b, f"var{m}"))
                    nc.vector.tensor_scalar_add(inv[:, m, :], bank[post.bank(f"var{m}")][:, :], EPS).then_inc(v_read2, 1)
                v.wait_ge(ssq2_done, b + 1)
                nc.vector.tensor_scalar(ssq, ssq, 1.0 / D, EPS, ALU.mult, ALU.add).then_inc(ms2_done, 1)
                v.wait_ge(rms2_done, b + 1)
                for i in range(NT):
                    last = nc.vector.tensor_scalar_mul(xb[:, i, :], xn[:, i, :], rms[:, i:i + 1])
                last.then_inc(xc_done, 1)
                v.wait_ge(made2, post.made(b, "xc0"))
                nc.vector.tensor_scalar_mul(xbT[:, 0, :], bank[post.bank("xc0")][:, :], VEC["w_ln2"][:, 0:1]).then_inc(v_read2, 1)
                iota = const[:, CONST["iota"][0]:CONST["iota"][0] + ME].rearrange("p (o e) -> p o e", o=1).broadcast_to([P, NT, ME])

                def wide(t):
                    return t.rearrange("p (t o) -> p t o", o=1).broadcast_to([P, NT, ME])

                v.wait_ge(made2, post.made(b, "gate"))
                bias = gate_b.rearrange("p (o e) -> p o e", o=1).broadcast_to([P, NT, ME])
                nc.vector.tensor_tensor(logits, bank[post.bank("gate")][:, 0:NT * ME].rearrange("p (t e) -> p t e", e=ME), bias,
                                        ALU.add).then_inc(v_read2, 1)
                v.wait_ge(v_read2, post.read(b, "gate"))
                tstep = Steps(10 * b)
                best, where = (routs[0], routs[1]), (routs[2], routs[3])
                for n in range(2):
                    hot = route[n]
                    nc.vector.tensor_reduce(best[n], logits, X, ALU.max).then_inc(top_step, 1)
                    v.wait_ge(top_step, tstep.next())
                    nc.vector.tensor_tensor(hot, logits, wide(best[n]), ALU.is_ge).then_inc(top_step, 1)
                    v.wait_ge(top_step, tstep.next())
                    nc.vector.scalar_tensor_tensor(hot, hot, -float(ME), iota, ALU.mult, ALU.add).then_inc(top_step, 1)
                    v.wait_ge(top_step, tstep.next())
                    nc.vector.tensor_reduce(where[n], hot, X, ALU.min).then_inc(top_step, 1)
                    v.wait_ge(top_step, tstep.next())
                    nc.vector.tensor_tensor(hot, hot, wide(where[n]), ALU.is_equal).then_inc(top_step, 1)
                    v.wait_ge(top_step, tstep.next())
                    if n == 0:
                        nc.vector.scalar_tensor_tensor(logits, hot, -3.0e38, logits, ALU.mult, ALU.add).then_inc(comb_in, 1)
                        v.wait_ge(comb_in, 2 * b + 1)
                nc.vector.tensor_tensor(routs[4], best[0], best[1], ALU.subtract).then_inc(comb_in, 1)
                v.wait_ge(comb_out, b + 1)
                nc.vector.tensor_scalar(routs[5], routs[4], -0.5, 0.5, ALU.mult, ALU.add).then_inc(comb_done, 1)
                nc.vector.tensor_scalar(routs[4], routs[4], 0.5, 0.5, ALU.mult, ALU.add).then_inc(comb_done, 1)
                v.wait_ge(comb_done, 5 * b + 2)
                nc.vector.tensor_tensor(route[0], route[0], wide(routs[4]), ALU.mult).then_inc(comb_done, 1)
                nc.vector.tensor_tensor(route[1], route[1], wide(routs[5]), ALU.mult).then_inc(comb_done, 1)
                v.wait_ge(comb_done, 5 * b + 4)
                nc.vector.tensor_tensor(route[2], route[0], route[1], ALU.add).then_inc(comb_done, 1)
                v.wait_ge(comb_done, 5 * b + 5)

                def hidden(e):
                    v.wait_ge(a_read2, post.read(b, f"g{e}"))
                    v.wait_ge(made2, post.made(b, f"u{e}"))
                    nc.vector.tensor_tensor(hid[e % 2], silu_g[e % 2], bank[post.bank(f"u{e}")][:, :], ALU.mult).then_inc(hid_done, 1)

                hidden(0)
                for e in range(ME + 1):
                    if e < ME:
                        hidden(e + 1)
                    for half, name in enumerate("ab"):
                        v.wait_ge(made2, post.made(b, f"d{e}{name}"))
                        if e:
                            v.wait_ge(v_read2, post.read(b, f"d{e - 1}{name}"))
                        for i in (2 * half, 2 * half + 1):
                            src = bank[post.bank(f"d{e}{name}")][:, (i % 2) * D:(i % 2 + 1) * D]
                            weight = route[2][:, i, e:e + 1] if e < ME else 1.0
                            base = xn[:, i, :] if e == 0 else acc[:, i, :]
                            last = nc.vector.scalar_tensor_tensor(acc[:, i, :], src, weight, base, ALU.mult, ALU.add)
                        last.then_inc(v_read2, 1)
                for m in range(KD):
                    v.wait_ge(inv_done, 2 * b + m + 1)
                    lstep = Steps(6 * b + 3 * m)
                    nc.vector.reciprocal(inv[:, m, :], inv[:, m, :]).then_inc(ln_step, 1)
                    v.wait_ge(ln_step, lstep.next())
                    nc.vector.tensor_tensor(y[:, m, :], y[:, m, :], inv[:, m, :], ALU.mult).then_inc(ln_step, 1)
                    v.wait_ge(ln_step, lstep.next())
                    nc.vector.tensor_scalar(y[:, m, :], y[:, m, :], VEC["ln_w"], VEC["ln_b"], ALU.mult, ALU.add).then_inc(ln_step, 1)
                    v.wait_ge(ln_step, lstep.next())
                    v.wait_ge(gsilu, 2 * b + m + 1)
                    nc.vector.tensor_tensor(y[:, m, :], y[:, m, :], proj["g"][:, m, :], ALU.mult).then_inc(o_done, 1)
                v.wait_ge(f_done, b + 1)
                for half in range(2):
                    v.wait_ge(made2, post.made(b, f"o{half}"))
                    nc.vector.tensor_tensor(acc[:, 2 * half:2 * half + 2, :], acc[:, 2 * half:2 * half + 2, :],
                                            bank[post.bank(f"o{half}")][:, :].rearrange("p (i d) -> p i d", i=2), ALU.mult).then_inc(v_read2, 1)
                v.wait_ge(v_read2, post.read(b, "o1"))
                nc.vector.tensor_tensor(x2, x2, acc, ALU.add).then_inc(out_ready, 1)

        @block.gpsimd
        def _(g):
            g.memset(neg_half, -0.5).then_inc(pool_set, 1)
            g.wait_ge(pool_set, 1)
            g.wait_ge(weights_in, 16 * NW)

            def gather(b):
                nc.gpsimd.tensor_copy(idx, pos_all[:, bass.ds(b * NT, NT)]).then_inc(idx_set, 1)
                g.wait_ge(idx_set, b + 1)
                nc.gpsimd.tensor_tensor(waste, neg_half, neg_half, ALU.mult)
                for i in range(NT):
                    g.indirect_dma_start(out=g_in[:, i, :], out_offset=None, in_=dram["g"][:, :],
                                         in_offset=bass.IndirectOffsetOnAxis(ap=idx[:, i:i + 1], axis=0)).then_inc(g_loaded, 16)

            gather(0)
            with g.Fori(0, B) as b:
                g.wait_ge(var_done, b + 1)
                nc.gpsimd.tensor_tensor(rstd, var_eps, neg_half, ALU.pow).then_inc(rstd_done, 1)
                g.wait_ge(ms_done, b + 1)
                nc.gpsimd.tensor_tensor(rms, ssq, neg_half, ALU.pow).then_inc(rms_done, 1)
                for n, x in enumerate(MIX_ORDER):
                    for m in range(KD):
                        g.wait_ge(v_read, pre.read(b, f"lb_{x}{m}"))
                        nc.gpsimd.tensor_tensor(mix[n % 2][:, m, :], mix[n % 2][:, m, :], xnT[:, m, :], ALU.add).then_inc(mixed, 1)
                for n in range(1 + NH // 2):
                    name, rows = ("ckv", 64) if n == 0 else (f"q{n - 1}", P)
                    dst = ckvT if n == 0 else qT[:, n - 1, :]
                    g.wait_ge(v_read, pre.read(b, name))
                    nc.gpsimd.tensor_tensor(shuf[n % 2][0:rows, :], shuf[n % 2][0:rows, :], sin[0:rows, :], ALU.mult).then_inc(rope_mul, 1)
                    g.wait_ge(rope_mul, 9 * b + (n + 1))
                    nc.gpsimd.tensor_tensor(dst[0:rows, :], dst[0:rows, :], shuf[n % 2][0:rows, :], ALU.add).then_inc(turned_q, 1)

                def norm(s):
                    n = (s % NT + 1) * P
                    g.wait_ge(s_inv, STEPS * b + (s + 1))
                    nc.gpsimd.tensor_tensor(probs[s % PROBS][:, 0:n], probs[s % PROBS][:, 0:n],
                                            row_inv[:, s:s + 1].broadcast_to([P, n]), ALU.mult).then_inc(s_norm, 1)

                def product(n):
                    m, j = n // HD, n % HD
                    nc.gpsimd.tensor_copy(state[n % 2][:, 0:1], VEC["init"][:, m * HD + j:m * HD + j + 1]).then_inc(init_set, 1)
                    g.wait_ge(init_set, UNITS * b + (n + 1))
                    g.wait_ge(scan_done, UNITS * b + (n + 1))
                    if n >= PRODS:
                        g.wait_ge(red_mm, 8 * b + (n - PRODS) // 4 + 1)
                    nc.gpsimd.tensor_tensor(prods[n % PRODS], state[n % 2][:, 0:T], proj["r"][:, m, :], ALU.mult).then_inc(prod_done, 1)

                for s in range(1, STEPS + 2):
                    if s <= STEPS:
                        norm(s - 1)
                    if s >= 2 and s % 2 == 0:
                        product(s // 2 - 1)
                g.wait_ge(pv_mm, 4 * b + 4 + 4)
                gather(b + 1)
                for m in range(KD):
                    g.wait_ge(v_read2, post.read(b, f"mean{m}"))
                    nc.gpsimd.tensor_tensor(sq[:, m, :], y[:, m, :], y[:, m, :], ALU.mult).then_inc(sq_done, 1)
                g.wait_ge(ms2_done, b + 1)
                nc.gpsimd.tensor_tensor(rms, ssq, neg_half, ALU.pow).then_inc(rms2_done, 1)
            g.wait_ge(g_loaded, 64 * (B + 1))


IN_NAMES = ["L0_attn_h", "L0_attn_W0", "L0_attn_W1", "centT", "W1T", "W2T", "const",
            "gammaT", "betaT", "b1T", "b2row", "vecs", "laT", "lbT", "rWT", "kWT", "vWT", "gWT", "oWT", "Wo", "gate_b",
            "L1_ffn_Wq", "L1_ffn_Wkva", "L1_ffn_Wkvb", "L1_ffn_Wgate", "L1_ffn_Wg", "L1_ffn_Wu", "L1_ffn_Wd",
            "L1_ffn_sWg", "L1_ffn_sWu", "L1_ffn_sWd"]


def build(nc, io, out):
    with ExitStack() as ctx:
        def scratch(name, shape):
            return nc.dram_tensor(name, shape, F32, kind="Internal").ap()

        dram = {"sorted": scratch("sorted_rows", ((SLOTS + 1) * P, ROW)),
                "g": scratch("gate_rows", (SLOTS * P, D)),
                "s": scratch("s_rows", (B * T, D))}
        arena = ctx.enter_context(nc.sbuf_tensor("arena", [P, 53200], F32))
        bank = [ctx.enter_context(nc.psum_tensor(f"bank{i}", [P, 512], F32)) for i in range(8)]
        ffn_loaded = ctx.enter_context(nc.semaphore("ffn_loaded"))
        mem = Arena(arena)
        const = mem.take(NCONST_A)
        pos_all = mem.take(TILES + NT).bitcast(U32)
        after_pos = mem.at
        tile_expert = mem.take(SLOTS).bitcast(I32)
        w1s = mem.take(E * KD * F)
        w2s = mem.take(E * FC * D)
        phase_a(nc, io, dram, Arena(arena, mem.at), const, bank, w1s, w2s, pos_all, tile_expert, ffn_loaded)
        phase_b(nc, io, dram, Arena(arena, mem.at), const, bank, w1s, w2s, tile_expert, ffn_loaded)
        phase_c(nc, io, dram, Arena(arena, after_pos), const, bank, pos_all, out)


def kernel(**inputs):
    import concourse.bacc as bacc
    from concourse.bass_utils import run_bass_kernel_spmd

    a = {k: np.asarray(x) for k, x in inputs.items()}
    a["centT"] = a["L0_ffn_centroids"].T
    a["W1T"] = a["L0_ffn_W1"].transpose(0, 2, 1).reshape(E * D, F)
    a["W2T"] = a["L0_ffn_W2"].transpose(0, 2, 1).reshape(E * F, D)
    for name, key in (("gammaT", "L0_ffn_gamma"), ("betaT", "L0_ffn_beta"), ("b1T", "L0_ffn_b1")):
        a[name] = a[key].reshape(-1, P).T
    a["b2row"] = a["L0_ffn_b2"].reshape(1, -1)
    order = np.zeros(P, np.int64)
    for h in range(HG):
        for j in range(HD):
            order[rho(h, j)] = h * HD + j
    both = np.concatenate([order, P + order])
    for x in "rkvg":
        w = a[f"L1_attn_{x}W"].T
        a[x + "WT"] = w[:, both] if x in "vg" else w
    a["oWT"] = a["L1_attn_oW"].T[both]
    a["laT"] = np.concatenate([a[f"L1_attn_{x}_la"].T for x in "rkvgd"], axis=1)
    a["lbT"] = np.concatenate([a[f"L1_attn_{x}_lb"].T for x in "rkvgd"] + [np.zeros((LORA, D), np.float32)])

    def columns(x):
        return x.reshape(KD, P, -1).transpose(1, 0, 2).reshape(P, -1)

    a["vecs"] = np.concatenate(
        [columns(a[f"L1_attn_{x}_ll"]) for x in "rkvgd"] + [columns(a["L1_attn_xw"]), columns(a["L1_attn_u"]),
         columns(a["L1_attn_init_state"].reshape(D, HD)), a["L1_attn_ln_w"][order % HD][:, None],
         a["L1_attn_ln_b"][order % HD][:, None], columns(a["L1_ffn_w_ln1"]), columns(a["L1_ffn_w_ln2"])], axis=1)
    a["Wo"] = a["L1_ffn_Wo"].reshape(NH, 64, D)[:, :ND].reshape(NH * ND, D)
    a["gate_b"] = a["L1_ffn_expert_bias"].reshape(1, ME)
    a["const"] = constants()
    nc = bacc.Bacc("TRN2", target_bir_lowering=False, num_devices=1)
    arrays, io = {}, {}
    for name in IN_NAMES:
        arrays["in_" + name] = np.ascontiguousarray(a[name])
        io[name] = nc.dram_tensor("in_" + name, arrays["in_" + name].shape, F32, kind="ExternalInput").ap()
    out = nc.dram_tensor("out_0", (B, T, D), F32, kind="ExternalOutput").ap()
    build(nc, io, out)
    r = run_bass_kernel_spmd(nc, [arrays], core_ids=[0])
    return r.results[0]["out_0"]
```

```python
from contextlib import ExitStack

import concourse.bass as bass
import numpy as np
from concourse import mybir

F32 = mybir.dt.float32
BF16 = mybir.dt.bfloat16
I32 = mybir.dt.int32
U32 = mybir.dt.uint32
ALU = mybir.AluOpType
ACT = mybir.ActivationFunctionType
X = mybir.AxisListType.X

P = 128
B, T, D = 8, 512, 256
NT = T // P
KD = D // P
TILES = B * NT
E, F = 8, 1024
FC = F // P
ROW = D + 1
SLOTS = TILES + E - 1
EPS = 1e-5
ROUTE_STEPS = 17
HD = 16
RING = 4
HG = P // HD
NH, ND, RD = 16, 32, 32
LORA = 64
ME, MI = 8, 128

CONST = {}
_at = 0
for _name, _n in (("ident", P), ("before", P), ("ones", P), ("iota", E), ("slot", SLOTS),
                  ("sel", HD * P), ("red", HD // 4 * 32), ("spread", P), ("mean", P), ("mask", P),
                  ("cos", T), ("sin", T)):
    if _name == "sel":
        NCONST_A = _at
    CONST[_name] = (_at, _n)
    _at += _n
NCONST = _at


def rho(h, j):
    return 32 * (j % 4) + HG * (j // 4) + h


def constants():
    c = np.zeros((P, NCONST), np.float32)

    def put(name, a):
        at, n = CONST[name]
        c[:, at:at + n] = a

    p = np.arange(P)
    put("ident", np.eye(P))
    put("before", p[:, None] < p[None, :])
    put("ones", 1.0)
    put("iota", np.arange(E)[None, :])
    put("slot", np.arange(SLOTS)[None, :] * P)
    sel = np.zeros((P, HD, P), np.float32)
    red = np.zeros((P, HD // 4, 32), np.float32)
    spread = np.zeros((P, P), np.float32)
    mean = np.zeros((P, P), np.float32)
    for h in range(HG):
        for j in range(HD):
            sel[rho(h, j), j, h * HD:(h + 1) * HD] = 1.0
            spread[h * HD:(h + 1) * HD, rho(h, j)] = 1.0
            for i in range(HD):
                mean[rho(h, j), rho(h, i)] = 1.0 / HD
        for g in range(HD // 4):
            red[h * HD:(h + 1) * HD, g, HG * g + h] = 1.0
    put("sel", sel.reshape(P, -1))
    put("red", red.reshape(P, -1))
    put("spread", spread)
    put("mean", mean)
    put("mask", np.where(p[None, :] > p[:, None], -1e30, 0.0))
    freqs = np.float32(1.0) / np.float32(100000.0) ** (np.arange(0, RD, 2, dtype=np.float32) / np.float32(RD))
    ang = np.outer(np.arange(T, dtype=np.float32), freqs)
    cos, sin = np.ones((P, T), np.float32), np.zeros((P, T), np.float32)
    for base in (ND, ND + 64):
        for r in range(RD):
            cos[base + r] = np.cos(ang[:, r // 2])
            sin[base + r] = np.sin(ang[:, r // 2]) * (1.0 if r % 2 else -1.0)
    put("cos", cos)
    put("sin", sin)
    return c


class Arena:

    def __init__(self, tensor, at=0):
        self.tensor, self.at = tensor, at

    def take(self, *shape):
        n = 1
        for s in shape:
            n *= s
        view = self.tensor[:, self.at:self.at + n]
        self.at += n
        assert self.at <= self.tensor.shape[1], self.at
        if len(shape) == 2:
            return view.rearrange("p (a b) -> p a b", a=shape[0])
        if len(shape) == 3:
            return view.rearrange("p (a b c) -> p a b c", a=shape[0], b=shape[1])
        return view


class Steps:

    def __init__(self, base):
        self.base, self.n = base, 0

    def next(self):
        self.n += 1
        return self.base + self.n


def phase_a(nc, io, dram, mem, spare, const, bank, w1s, w2s, pos_all, tile_expert, ffn_loaded):
    with ExitStack() as ctx:
        def sem(name):
            return ctx.enter_context(nc.semaphore("a_" + name))

        x_sb = mem.take(NT, D)
        xn = x_sb
        xn_all = mem.take(TILES, ROW)
        zeros = mem.take(ROW)
        stats = mem.take(NT, 6)
        mv = mem.take(NT, 2)
        var_eps = mem.take(NT)
        rstd = mem.take(NT)
        neg_half = mem.take(NT)
        h0 = mem.take(KD, T)
        h1 = mem.take(KD, T)
        h2 = spare.take(KD, T)
        gru_w = [mem.take(KD, 3 * D) for _ in range(2)]
        cent = mem.take(KD, E)
        sig_hidden, sig_gate = mem.take(T), mem.take(T)
        sig = [[sig_hidden, sig_gate, mem.take(T), mem.take(T), spare.take(T)] for _ in range(2)]
        scanned = mem.take(T)
        s_tok = mem.take(NT, D)
        scores = mem.take(TILES, E)
        top = mem.take(TILES)
        cand, onehot, incl, excl = (spare.take(TILES, E) for _ in range(4))
        slot_ge = spare.take(SLOTS, E)
        first, posf = spare.take(TILES), spare.take(TILES)
        pad_i = spare.take(E).bitcast(I32)
        padded, ends, starts = spare.take(E), spare.take(E), spare.take(E)
        slot_e = spare.take(SLOTS)

        const_in = sem("const_in")
        weights_in = sem("weights_in")
        x_in = sem("x_in")
        zeroed = sem("zeroed")
        zeros_set = sem("zeros_set")
        half_set = sem("half_set")
        xn_done = sem("xn_done")
        dve_step = sem("dve_step")
        rstd_done = sem("rstd_done")
        xn_kept = sem("xn_kept")
        xn_turned = sem("xn_turned")
        h0_left = sem("h0_left")
        h0_right = sem("h0_right")
        score_mm = sem("score_mm")
        scores_read = sem("scores_read")
        gru_mm = sem("gru_mm")
        gru_sig = sem("gru_sig")
        gru_read = sem("gru_read")
        gru_step = sem("gru_step")
        gru_scan = sem("gru_scan")
        kept_h = sem("kept_h")
        h_ready = sem("h_ready")
        s_turned = sem("s_turned")
        s_out = sem("s_out")
        s_stored = sem("s_stored")
        chain = sem("chain")
        route_mm = sem("route_mm")
        route_read = sem("route_read")
        pos_done = sem("pos_done")
        alpha_done = sem("alpha_done")
        top_done = sem("top_done")
        scattered = sem("scattered")

        NPER = 2 * NT + 1
        block = ctx.enter_context(nc.Block())
        h_rows = io["L0_attn_h"].rearrange("b t d -> (b t) d")

        @block.sync
        def _(sp):
            sp.dma_start(x_sb, h_rows[0:T, :].rearrange("(i p) d -> p i d", p=P)).then_inc(x_in, 16)
            sp.dma_start(const, io["const"][:, 0:NCONST_A]).then_inc(const_in, 16)
            for layer in range(2):
                sp.dma_start(gru_w[layer], io[f"L0_attn_W{layer}"].rearrange("(k p) n -> p k n", p=P)).then_inc(weights_in, 16)
            sp.dma_start(cent, io["centT"].rearrange("(k p) n -> p k n", p=P)).then_inc(weights_in, 16)
            sp.wait_ge(zeros_set, 1)

            def expert_weights(e):
                sp.dma_start(w1s[:, bass.ds(e * KD * F, KD * F)].rearrange("p (k f) -> p k f", k=KD),
                             io["W1T"][bass.ds(e * D, D), :].rearrange("(k p) f -> p k f", p=P)).then_inc(ffn_loaded, 16)
                sp.dma_start(w2s[:, bass.ds((E - 1) * FC * D - e * (FC * D), FC * D)].rearrange("p (k f) -> p k f", k=FC),
                             io["W2T"][bass.ds(e * F, F), :].rearrange("(k p) f -> p k f", p=P)).then_inc(ffn_loaded, 16)

            with sp.Fori(0, B - 1) as b:
                sp.wait_ge(xn_kept, b + 1)
                sp.wait_ge(xn_turned, 2 * b + 2)
                sp.dma_start(x_sb, h_rows[bass.ds(b * T + T, T), :].rearrange("(i p) d -> p i d", p=P)).then_inc(x_in, 16)
                expert_weights(b)
                for z in range(6):
                    sp.dma_start(dram["sorted"][bass.ds((6 * b + z) * P, P), :], zeros).then_inc(zeroed, 16)
            sp.wait_ge(h_ready, 4 * B + 2)
            sp.wait_ge(s_turned, 2 * B)
            sp.wait_ge(chain, ROUTE_STEPS)
            sp.wait_ge(pos_done, 1)
            expert_weights(B - 1)

        def sequences(engine, body):
            body(0)
            with engine.Fori(1, B - 1) as b:
                body(b)
            body(B - 1)

        def is_(b, n):
            return isinstance(b, int) and b == n

        @block.tensor
        def _(pe):
            ident = const[:, 0:P]

            def turn_in(b):
                pe.wait_ge(xn_done, NT * b + NT)
                for k in range(KD):
                    for i in range(NT):
                        last = nc.tensor.transpose(bank[6 + k][:, i * P:(i + 1) * P], xn[:, i, k * P:(k + 1) * P], ident)
                    last.then_inc(xn_turned, 1)
                pe.wait_ge(h0_left, b + 1)
                pe.wait_ge(h0_right, b + 1)
                for i in range(NT):
                    for k in range(KD):
                        last = nc.tensor.matmul(bank[6][:, i * E:(i + 1) * E], h0[:, k, i * P:(i + 1) * P], cent[:, k, :],
                                                start=(k == 0), stop=(k == KD - 1))
                last.then_inc(score_mm, 1)

            def banks_free(b, u):
                pe.wait_ge(gru_sig, 20 * b + 5 * u + 5)
                pe.wait_ge(gru_read, 4 * b + u + 1)

            def gru_half(b, u, k):
                layer, m, s = u // 2, u % 2, 3 * (u % 2)
                src = h0 if layer == 0 else h1
                for q in range(3):
                    last = nc.tensor.matmul(bank[s + q][:, :], gru_w[layer][:, k, q * D + m * P:q * D + (m + 1) * P],
                                            src[:, k, :], start=(k == 0), stop=(k == KD - 1))
                if k == KD - 1:
                    last.then_inc(gru_mm, 1)

            def turn_out(b):
                pe.wait_ge(h_ready, 4 * b + 4 + 2)
                pe.wait_ge(scores_read, b + 1)
                for half in range(2):
                    for i in (2 * half, 2 * half + 1):
                        for m in range(KD):
                            last = nc.tensor.transpose(bank[6 + half][:, (i % 2) * D + m * P:(i % 2) * D + (m + 1) * P],
                                                       h2[:, m, i * P:(i + 1) * P], ident)
                    last.then_inc(s_turned, 1)

            def ranks():
                pe.wait_ge(chain, 4)
                oh = onehot.rearrange("p t e -> p (t e)")
                for n, name in enumerate(("before", "ones")):
                    at = CONST[name][0]
                    last = nc.tensor.matmul(bank[6 + n][:, 0:TILES * E], const[:, at:at + P], oh, start=True, stop=True)
                last.then_inc(route_mm, 1)

            def sequence(b):
                banks_free(b, 0)
                gru_half(b, 0, 0)
                gru_half(b, 0, 1)
                if is_(b, B - 1):
                    ranks()
                banks_free(b, 1)
                gru_half(b, 1, 0)
                gru_half(b, 1, 1)
                if not is_(b, 0):
                    if is_(b, B - 1):
                        pe.wait_ge(route_read, 1)
                    else:
                        pe.wait_ge(scores_read, b + 1)
                    turn_out(b - 1)
                for k in range(KD):
                    pe.wait_ge(h_ready, 4 * b + k + 1 + 2)
                    for u in (2, 3):
                        if k == 0:
                            banks_free(b, u)
                        gru_half(b, u, k)
                if not is_(b, B - 1):
                    pe.wait_ge(s_out, 2 * b + 2)
                    turn_in(b + 1)

            pe.wait_ge(const_in, 16)
            pe.wait_ge(weights_in, 48)
            turn_in(0)
            sequences(pe, sequence)
            pe.wait_ge(s_out, 2 * B)
            turn_out(B - 1)

        @block.scalar
        def _(act):
            act.sem_inc(gru_sig, 10)
            act.sem_inc(s_out, 2)
            act.sem_inc(s_stored, 16)

            def right(b):
                act.wait_ge(xn_turned, 2 * b + 2)
                if not is_(b, 0):
                    act.wait_ge(kept_h, 4 * b - 2)
                nc.scalar.activation(h0[:, 1, :], bank[7][:, :], ACT.Copy).then_inc(h0_right, 1)

            def unit(b, u):
                s = 3 * (u % 2)
                act.wait_ge(gru_mm, 4 * b + u + 1)
                act.wait_ge(gru_scan, 4 * b + u + 2)
                act.wait_ge(h_ready, 4 * b + u + 1)
                for n, (q, scale) in enumerate(((0, 1.0), (1, 1.0), (1, -1.0), (2, 1.0), (2, -1.0))):
                    nc.scalar.activation(sig[u % 2][n], bank[s + q][:, :], ACT.Sigmoid, scale=scale).then_inc(gru_sig, 1)

            def store(b):
                act.wait_ge(s_stored, 16 * b + 16)
                for half in range(2):
                    act.wait_ge(s_turned, 2 * b + half + 1)
                    nc.scalar.activation(s_tok[:, 2 * half:2 * half + 2, :],
                                         bank[6 + half][:, :].rearrange("p (i d) -> p i d", i=2), ACT.Copy).then_inc(s_out, 1)
                act.wait_ge(s_out, 2 * b + 4)
                act.dma_start(dram["s"][bass.ds(b * T, T), :].rearrange("(i p) d -> p i d", p=P), s_tok).then_inc(s_stored, 16)

            def sequence(b):
                if is_(b, B - 1):
                    act.wait_ge(top_done, 1)
                    nc.scalar.activation(xn_all[:, :, D], top, ACT.Sigmoid).then_inc(alpha_done, 1)
                unit(b, 0)
                unit(b, 1)
                if not is_(b, 0):
                    store(b - 1)
                unit(b, 2)
                if not is_(b, B - 1):
                    right(b + 1)
                unit(b, 3)

            right(0)
            sequences(act, sequence)
            store(B - 1)
            act.wait_ge(s_stored, 16 * B + 16)

        @block.vector
        def _(v):
            v.memset(zeros, 0.0).then_inc(zeros_set, 1)
            v.sem_inc(gru_read, 2)
            v.sem_inc(gru_scan, 2)
            v.sem_inc(h_ready, 2)

            def norm(b):
                step = Steps(NPER * b)
                v.wait_ge(x_in, 16 * b + 16)
                for i in range(NT):
                    nc.vector.bn_stats(stats[:, i, :], x_sb[:, i, :]).then_inc(dve_step, 1)
                for i in range(NT):
                    got = step.next()
                v.wait_ge(dve_step, got)
                nc.vector.memset(var_eps, EPS)
                for i in range(NT):
                    nc.vector.bn_aggr(mv[:, i, :], stats[:, i, :]).then_inc(dve_step, 1)
                for i in range(NT):
                    got = step.next()
                v.wait_ge(dve_step, got)
                nc.vector.tensor_scalar_add(var_eps, mv[:, :, 1], EPS).then_inc(dve_step, 1)
                v.wait_ge(rstd_done, b + 1)
                for i in range(NT):
                    nc.vector.tensor_scalar(xn[:, i, :], x_sb[:, i, :], mv[:, i, 0:1], rstd[:, i:i + 1],
                                            ALU.subtract, ALU.mult).then_inc(xn_done, 1)

            def left(b):
                v.wait_ge(xn_turned, 2 * b + 1)
                if not is_(b, 0):
                    v.wait_ge(kept_h, 4 * b - 2)
                nc.vector.tensor_copy(h0[:, 0, :], bank[6][:, :]).then_inc(h0_left, 1)

            def read_scores(b):
                v.wait_ge(score_mm, b + 1)
                nc.vector.tensor_copy(scores.rearrange("p t e -> p (t e)")[:, bass.ds(b * NT * E, NT * E)],
                                      bank[6][:, 0:NT * E]).then_inc(scores_read, 1)

            def unit(b, u):
                hidden = bank[3 * (u % 2)]
                s_hid, s_gate, s_rest, s_proj, kept = sig[u % 2]
                at, n = 20 * b + 5 * u + 10, 4 * b + u
                link = Steps(12 * b + 3 * u)
                v.wait_ge(gru_sig, at + 1)
                nc.vector.tensor_scalar_min(s_hid, s_hid, 0.5).then_inc(gru_step, 1)
                v.wait_ge(gru_step, link.next())
                nc.vector.scalar_tensor_tensor(s_hid, hidden[:, :], 0.0, s_hid, ALU.max, ALU.add).then_inc(gru_read, 1)
                v.wait_ge(gru_read, n + 1 + 2)
                v.wait_ge(gru_sig, at + 2)
                nc.vector.tensor_tensor(s_gate, s_hid, s_gate, ALU.mult).then_inc(gru_step, 1)
                v.wait_ge(gru_step, link.next())
                v.wait_ge(gru_sig, at + 3)
                v.wait_ge(h_ready, n + 2)
                nc.vector.tensor_tensor_scan(scanned, s_rest, s_gate, 0.0, ALU.mult, ALU.add).then_inc(gru_scan, 1)
                v.wait_ge(gru_scan, n + 1 + 2)
                v.wait_ge(gru_sig, at + 4)
                nc.vector.tensor_tensor(scanned, scanned, s_proj, ALU.mult).then_inc(gru_step, 1)
                v.wait_ge(gru_step, link.next())
                v.wait_ge(kept_h, n + 1)
                dst = h1 if u < 2 else h2
                nc.vector.tensor_tensor(dst[:, u % 2, :], scanned, kept, ALU.add).then_inc(h_ready, 1)

            link = Steps(0)

            def hottest():
                v.wait_ge(scores_read, B)
                nc.vector.tensor_reduce(top, scores, X, ALU.max).then_inc(top_done, 1)
                v.wait_ge(top_done, 1)
                nc.vector.tensor_tensor(cand, scores, top.rearrange("p (t o) -> p t o", o=1).broadcast_to([P, TILES, E]),
                                        ALU.is_ge).then_inc(chain, 1)
                v.wait_ge(chain, link.next())
                iota = const[:, CONST["iota"][0]:CONST["iota"][0] + E].rearrange("p (o e) -> p o e", o=1).broadcast_to([P, TILES, E])
                nc.vector.scalar_tensor_tensor(cand, cand, -float(E), iota, ALU.mult, ALU.add).then_inc(chain, 1)
                v.wait_ge(chain, link.next())
                nc.vector.tensor_reduce(first, cand, X, ALU.min).then_inc(chain, 1)
                v.wait_ge(chain, link.next())
                nc.vector.tensor_tensor(onehot, cand, first.rearrange("p (t o) -> p t o", o=1).broadcast_to([P, TILES, E]),
                                        ALU.is_equal).then_inc(chain, 1)
                link.next()

            def positions():
                v.wait_ge(route_mm, 1)
                rank = bank[6][:, 0:TILES * E].rearrange("p (t e) -> p t e", e=E)
                counts = bank[7][:, 0:TILES * E].rearrange("p (t e) -> p t e", e=E)
                one = const[:, CONST["ones"][0]:CONST["ones"][0] + TILES]
                for e in range(E):
                    last = nc.vector.tensor_tensor_scan(incl[:, :, e], one, counts[:, :, e], 0.0, ALU.mult, ALU.add)
                last.then_inc(chain, 1)
                v.wait_ge(chain, link.next())
                nc.vector.tensor_tensor(excl, incl, counts, ALU.subtract).then_inc(chain, 1)
                nc.vector.tensor_scalar_add(pad_i, incl[:, TILES - 1, :], float(P - 1)).then_inc(chain, 1)
                link.next()
                v.wait_ge(chain, link.next())
                nc.vector.tensor_tensor(excl, excl, rank, ALU.add).then_inc(route_read, 1)
                nc.vector.tensor_single_scalar(pad_i, pad_i, 7, ALU.arith_shift_right).then_inc(chain, 1)
                v.wait_ge(chain, link.next())
                nc.vector.tensor_scalar_mul(padded, pad_i, float(P)).then_inc(chain, 1)
                v.wait_ge(chain, link.next())
                nc.vector.tensor_tensor_scan(ends, one[:, 0:E], padded, 0.0, ALU.mult, ALU.add).then_inc(chain, 1)
                v.wait_ge(chain, link.next())
                nc.vector.tensor_tensor(starts, ends, padded, ALU.subtract).then_inc(chain, 1)
                v.wait_ge(chain, link.next())
                v.wait_ge(route_read, 1)
                nc.vector.tensor_tensor(excl, excl, starts.rearrange("p (o e) -> p o e", o=1).broadcast_to([P, TILES, E]),
                                        ALU.add).then_inc(chain, 1)
                v.wait_ge(chain, link.next())
                nc.vector.tensor_tensor(excl, excl, onehot, ALU.mult).then_inc(chain, 1)
                v.wait_ge(chain, link.next())
                nc.vector.tensor_reduce(posf, excl, X, ALU.add).then_inc(chain, 1)
                v.wait_ge(chain, link.next())
                nc.vector.memset(pos_all[:, TILES:TILES + NT], 0)
                nc.vector.tensor_copy(pos_all[:, 0:TILES], posf).then_inc(pos_done, 1)
                slot = const[:, CONST["slot"][0]:CONST["slot"][0] + SLOTS].rearrange("p (t o) -> p t o", o=1).broadcast_to([P, SLOTS, E])
                nc.vector.tensor_tensor(slot_ge, slot, ends.rearrange("p (o e) -> p o e", o=1).broadcast_to([P, SLOTS, E]),
                                        ALU.is_ge).then_inc(chain, 1)
                v.wait_ge(chain, link.next())
                nc.vector.tensor_reduce(slot_e, slot_ge, X, ALU.add).then_inc(chain, 1)
                v.wait_ge(chain, link.next())
                nc.vector.tensor_scalar_min(tile_expert, slot_e, float(E - 1)).then_inc(chain, 1)
                v.wait_ge(chain, link.next())
                assert link.n == ROUTE_STEPS

            def sequence(b):
                if is_(b, B - 1):
                    hottest()
                unit(b, 0)
                if is_(b, B - 1):
                    positions()
                unit(b, 1)
                if not is_(b, B - 1):
                    norm(b + 1)
                unit(b, 2)
                if not is_(b, B - 1):
                    left(b + 1)
                unit(b, 3)
                if not is_(b, B - 1):
                    read_scores(b + 1)

            norm(0)
            left(0)
            read_scores(0)
            sequences(v, sequence)

        @block.gpsimd
        def _(g):
            g.memset(neg_half, -0.5).then_inc(half_set, 1)
            g.wait_ge(half_set, 1)

            def norm(b):
                g.wait_ge(dve_step, NPER * b + NPER)
                nc.gpsimd.tensor_tensor(rstd, var_eps, neg_half, ALU.pow).then_inc(rstd_done, 1)
                g.wait_ge(xn_done, NT * b + NT)
                nc.gpsimd.tensor_copy(xn_all[:, bass.ds(b * NT, NT), 0:D], xn).then_inc(xn_kept, 1)

            def unit(b, u):
                src = h0 if u < 2 else h1
                if u >= 2:
                    g.wait_ge(h_ready, 4 * b + u - 1 + 2)
                else:
                    g.wait_ge(h0_left if u == 0 else h0_right, b + 1)
                g.wait_ge(gru_sig, 20 * b + 5 * u + 5 + 10)
                nc.gpsimd.tensor_tensor(sig[u % 2][4], sig[u % 2][4], src[:, u % 2, :], ALU.mult).then_inc(kept_h, 1)

            def scatter(t0, t1):
                for t in range(t0, t1):
                    g.indirect_dma_start(out=dram["sorted"][:, :],
                                         out_offset=bass.IndirectOffsetOnAxis(ap=pos_all[:, t:t + 1], axis=0),
                                         in_=xn_all[:, t, :], in_offset=None).then_inc(scattered, 16)

            def sequence(b):
                unit(b, 0)
                unit(b, 1)
                if is_(b, B - 1):
                    g.wait_ge(zeroed, 16 * 6 * (B - 1))
                    g.wait_ge(alpha_done, 1)
                    g.wait_ge(pos_done, 1)
                    scatter(0, 8)
                else:
                    norm(b + 1)
                unit(b, 2)
                unit(b, 3)

            norm(0)
            sequences(g, sequence)
            scatter(8, TILES)
            g.wait_ge(scattered, 16 * TILES)


def phase_b(nc, io, dram, mem, const, bank, w1s, w2s, tile_expert, ffn_loaded):
    with ExitStack() as ctx:
        def sem(name):
            return ctx.enter_context(nc.semaphore("b_" + name))

        xs = [mem.take(ROW) for _ in range(RING)]
        n_tok = mem.take(D)
        stats, mv = mem.take(6), mem.take(2)
        var_eps, rstd, neg_half = mem.take(1), mem.take(1), mem.take(1)
        nT = [mem.take(KD, P) for _ in range(2)]
        z_sb = mem.take(F)
        hT = mem.take(FC, P)
        f_sb = [mem.take(D) for _ in range(2)]
        g_sb = [mem.take(D) for _ in range(RING)]
        gamma, beta = mem.take(E * KD), mem.take(E * KD)
        b1 = mem.take(E * FC)
        b2 = mem.take(E * D)
        turn_bank, z_bank, zT_bank, out_bank = bank[0], bank[1:3], bank[3:5], bank[5:7]

        small_in = sem("small_in")
        xs_in = [sem(f"xs_in{u}") for u in range(RING)]
        var_done = sem("var_done")
        stat_step = sem("stat_step")
        rstd_done = sem("rstd_done")
        n_done = sem("n_done")
        n_turned = sem("n_turned")
        nT_done = sem("nT_done")
        z_mm = sem("z_mm")
        z_left = sem("z_left")
        z_right = sem("z_right")
        z_turned = sem("z_turned")
        h_left = sem("h_left")
        h_right = sem("h_right")
        out_mm = sem("out_mm")
        f_done = sem("f_done")
        g_done = sem("g_done")
        g_stored = [sem(f"g_stored{u}") for u in range(RING)]

        ROUNDS = (SLOTS - 2) // RING
        REST = SLOTS - RING * ROUNDS
        assert 2 <= REST < RING
        block = ctx.enter_context(nc.Block())

        def tiles(engine, tile):
            with engine.Fori(0, ROUNDS) as j:
                for u in range(RING):
                    tile(RING * j + u, u)
            for u in range(REST):
                tile(RING * ROUNDS + u, u, min(2, REST - 1 - u))

        def expert_of(engine, k):
            return engine.value_load(tile_expert[0:1, bass.ds(k, 1)], min_val=0, max_val=E - 1)

        @block.sync
        def _(sp):
            for dst, name in ((gamma, "gammaT"), (beta, "betaT"), (b1, "b1T")):
                sp.dma_start(dst, io[name][:, :]).then_inc(small_in, 16)
            sp.dma_start(b2[0:1, :], io["b2row"][:, :]).then_inc(small_in, 16)
            for k in range(RING):
                sp.dma_start(xs[k], dram["sorted"][k * P:(k + 1) * P, :]).then_inc(xs_in[k], 16)

            def store(k, u):
                sp.wait_ge(g_done, k + 1 + 2)
                sp.dma_start(dram["g"][bass.ds(k * P, P), :], g_sb[u]).then_inc(g_stored[u], 16)

            with sp.Fori(0, ROUNDS) as j:
                for u in range(RING):
                    k = RING * j + u
                    store(k, u)
                    sp.dma_start(xs[u], dram["sorted"][bass.ds((k + RING) * P, P), :]).then_inc(xs_in[u], 16)
            for u in range(REST):
                store(RING * ROUNDS + u, u)
            for u in range(RING):
                sp.wait_ge(xs_in[u], 16 * (ROUNDS + 1))
                sp.wait_ge(g_stored[u], 16 * (ROUNDS + (u < REST)) + 16)

        @block.tensor
        def _(pe):
            ident = const[:, 0:P]
            ones_row = const[0:1, CONST["ones"][0]:CONST["ones"][0] + P]

            def turn_norm(k):
                pe.wait_ge(n_done, k + 1)
                if not (isinstance(k, int) and k == 0):
                    pe.wait_ge(nT_done, k)
                for c in range(KD):
                    last = nc.tensor.transpose(turn_bank[:, c * P:(c + 1) * P], n_tok[:, c * P:(c + 1) * P], ident)
                last.then_inc(n_turned, 1)

            def expand(k, u):
                e = expert_of(pe, k)
                pe.wait_ge(nT_done, k + 1)
                for half in range(2):
                    for c in range(KD):
                        last = nc.tensor.matmul(z_bank[half][:, :], nT[u % 2][:, c, :],
                                                w1s[:, bass.ds(e * (KD * F) + (c * F + half * 512), 512)],
                                                start=(c == 0), stop=(c == KD - 1))
                last.then_inc(z_mm, 1)

            def turn_z(k):
                for half in range(2):
                    pe.wait_ge(z_left if half == 0 else z_right, k + 1)
                    for c in range(4):
                        last = nc.tensor.transpose(zT_bank[half][:, c * P:(c + 1) * P],
                                                   z_sb[:, half * 512 + c * P:half * 512 + (c + 1) * P], ident)
                    last.then_inc(z_turned, 1)

            def back(k, u):
                e = expert_of(pe, k)
                pe.wait_ge(f_done, k + 1)
                nc.tensor.matmul(out_bank[u % 2][:, 0:D], ones_row, b2[0:1, bass.ds(e * D, D)], start=True, stop=False)
                pe.wait_ge(h_left, k + 1)
                pe.wait_ge(h_right, k + 1)
                for c in range(FC):
                    last = nc.tensor.matmul(out_bank[u % 2][:, 0:D], hT[:, c, :],
                                            w2s[:, bass.ds((E - 1) * FC * D + c * D - e * (FC * D), D)], start=False, stop=(c == FC - 1))
                last.then_inc(out_mm, 1)

            pe.wait_ge(ffn_loaded, 16 * 2 * E)
            pe.wait_ge(small_in, 64)
            turn_norm(0)
            expand(0, 0)
            turn_norm(1)

            def tile(k, u, ahead=2):
                turn_z(k)
                if ahead >= 1:
                    expand(k + 1, u + 1)
                if ahead >= 2:
                    turn_norm(k + 2)
                back(k, u)

            tiles(pe, tile)

        @block.scalar
        def _(act):
            act.sem_inc(g_done, 2)
            for u in range(RING):
                act.sem_inc(g_stored[u], 16)

            def z_out(k):
                act.wait_ge(z_mm, k + 1)
                nc.scalar.activation(z_sb[:, 0:512], z_bank[0][:, :], ACT.Copy).then_inc(z_left, 1)

            def relu(k):
                e = expert_of(act, k)
                act.wait_ge(z_turned, 2 * k + 1)
                for c in range(4):
                    last = nc.scalar.activation(hT[:, c, :], zT_bank[0][:, c * P:(c + 1) * P], ACT.Relu,
                                                bias=b1[:, bass.ds(e * FC + c, 1)])
                last.then_inc(h_left, 1)

            def silu(k, u):
                act.wait_ge(g_stored[u], 4 * k - (4 * u - 16))
                act.wait_ge(f_done, k + 1 + 2)
                nc.scalar.activation(g_sb[u], f_sb[u % 2], ACT.Silu).then_inc(g_done, 1)

            act.wait_ge(small_in, 64)
            z_out(0)

            def tile(k, u, ahead=2):
                relu(k)
                if ahead >= 1:
                    z_out(k + 1)
                silu(k, u)

            tiles(act, tile)

        @block.vector
        def _(v):
            v.sem_inc(f_done, 2)
            v.wait_ge(small_in, 64)

            def norm(k, u):
                step = Steps(2 * k)
                v.wait_ge(xs_in[u % RING], 4 * k - (4 * (u % RING) - 16))
                nc.vector.bn_stats(stats, xs[u % RING][:, 0:D]).then_inc(stat_step, 1)
                v.wait_ge(stat_step, step.next())
                nc.vector.memset(var_eps, EPS)
                nc.vector.bn_aggr(mv, stats).then_inc(stat_step, 1)
                v.wait_ge(stat_step, step.next())
                nc.vector.tensor_scalar_add(var_eps, mv[:, 1:2], EPS).then_inc(var_done, 1)
                v.wait_ge(rstd_done, k + 1)
                nc.vector.tensor_scalar(n_tok, xs[u % RING][:, 0:D], mv[:, 0:1], rstd, ALU.subtract, ALU.mult).then_inc(n_done, 1)

            def scale_norm(k, u):
                e = expert_of(v, k)
                v.wait_ge(n_turned, k + 1)
                for c in range(KD):
                    last = nc.vector.tensor_scalar(nT[u % 2][:, c, :], turn_bank[:, c * P:(c + 1) * P], gamma[:, bass.ds(e * KD + c, 1)],
                                                   beta[:, bass.ds(e * KD + c, 1)], ALU.mult, ALU.add)
                last.then_inc(nT_done, 1)

            def z_out(k):
                v.wait_ge(z_mm, k + 1)
                nc.vector.tensor_copy(z_sb[:, 512:1024], z_bank[1][:, :]).then_inc(z_right, 1)

            def relu(k):
                e = expert_of(v, k)
                v.wait_ge(z_turned, 2 * k + 2)
                for c in range(4):
                    last = nc.vector.tensor_scalar(hT[:, 4 + c, :], zT_bank[1][:, c * P:(c + 1) * P],
                                                   b1[:, bass.ds(e * FC + (4 + c), 1)], 0.0, ALU.add, ALU.max)
                last.then_inc(h_right, 1)

            def finish(k, u):
                v.wait_ge(out_mm, k + 1)
                v.wait_ge(g_done, k + 1)
                nc.vector.scalar_tensor_tensor(f_sb[u % 2], out_bank[u % 2][:, 0:D], xs[u][:, D:D + 1], xs[u][:, 0:D],
                                               ALU.mult, ALU.add).then_inc(f_done, 1)

            norm(0, 0)
            scale_norm(0, 0)
            norm(1, 1)
            z_out(0)
            scale_norm(1, 1)

            def tile(k, u, ahead=2):
                relu(k)
                if ahead >= 2:
                    norm(k + 2, u + 2)
                if ahead >= 1:
                    z_out(k + 1)
                if ahead >= 2:
                    scale_norm(k + 2, u + 2)
                finish(k, u)

            tiles(v, tile)

        @block.gpsimd
        def _(g):
            g.memset(neg_half, -0.5).then_inc(n_set := sem("neg_set"), 1)
            g.wait_ge(n_set, 1)
            with g.Fori(0, SLOTS) as k:
                g.wait_ge(var_done, k + 1)
                nc.gpsimd.tensor_tensor(rstd, var_eps, neg_half, ALU.pow).then_inc(rstd_done, 1)


PAIR = {"r": (0, 0), "k": (0, 64), "v": (1, 0), "g": (1, 64), "d": (2, 0)}
MIX_ORDER = "drkvg"
HEADS_PER_TILE = 2
HGROUP = 4
STEPS = NH * NT
UNITS = KD * HD
LAG = 3
PROBS = 3
PRODS = 6


class Outputs:

    def __init__(self, table, nbank):
        self.at = {name: n for n, (name, _) in enumerate(table)}
        self.reader = {name: who for name, who in table}
        self.n = len(table)
        self.names = [name for name, _ in table]
        self.order = {who: [x for x, w in table if w == who] for who in "avh"}
        self.nbank = nbank

    def bank(self, name):
        return self.at[name] % self.nbank

    def before(self, name):
        n = self.at[name] - self.nbank
        return self.names[n] if n >= 0 else None

    def made(self, b, name):
        return self.n * b + (self.at[name] + 1)

    def read(self, b, name):
        mine = self.order[self.reader[name]]
        return len(mine) * b + (mine.index(name) + 2)


PRE = ([("t0", "v"), ("t1", "a"), ("la_rk", "a"), ("la_vg", "a"), ("la_d", "a"),
        ("lb_d0", "v"), ("lb_d1", "v"), ("lb_r0", "v"), ("lb_r1", "v"), ("la_dd", "a"), ("lb_k0", "v"), ("lb_k1", "v"),
        ("pr_r0", "a"), ("pr_r1", "a"), ("lb_v0", "v"), ("lb_v1", "v"), ("pr_k0", "a"), ("pr_k1", "a"),
        ("lb_g0", "v"), ("lb_g1", "v"), ("pr_v0", "a"), ("pr_v1", "a"), ("lb_w0", "a"), ("lb_w1", "a"),
        ("pr_g0", "a"), ("pr_g1", "a"), ("xb0", "v"), ("xb1", "a"), ("ckv", "v")]
       + [(f"q{i}", "v") for i in range(NH // HEADS_PER_TILE)] + [("sp0", "v"), ("sp1", "v")]
       + [(f"k{i}", "a") for i in range(NH // HEADS_PER_TILE)] + [(f"v{i}", "a") for i in range(NT)])
def _experts():
    for e in range(ME + 2):
        if e <= ME:
            yield from ((f"g{e}", "a"), (f"u{e}", "h"))
        if e:
            yield from ((f"d{e - 1}a", "v"), (f"d{e - 1}b", "v"))


POST = ([("mean0", "v"), ("mean1", "v"), ("wo0", "v"), ("wo1", "v"), ("var0", "v"), ("var1", "v"),
         ("xc0", "v"), ("xc1", "a"), ("gate", "v")] + list(_experts()) + [("o0", "v"), ("o1", "v")])


def phase_c(nc, io, dram, mem, const, bank, pos_all, out):
    with ExitStack() as ctx:
        def sem(name):
            return ctx.enter_context(nc.semaphore("c_" + name))

        pre, post = Outputs(PRE, 8), Outputs(POST, 8)
        tail = mem.take(NCONST - NCONST_A)

        def table(name):
            at = CONST[name][0] - NCONST_A
            return tail[:, at:at + CONST[name][1]]

        sel, red = table("sel").rearrange("p (j c) -> p j c", j=HD), table("red").rearrange("p (g c) -> p g c", c=32)
        spread, mean_m, mask, cos, sin = (table(x) for x in ("spread", "mean", "mask", "cos", "sin"))
        rkvg_w = {x: mem.take(KD, D) for x in "rkvg"}
        o_w = mem.take(KD, D)
        la_w = mem.take(KD, 5 * LORA)
        lb_w = mem.take(3, D)
        vecs = mem.take(io["vecs"].shape[1])
        VEC = {}
        at = 0
        for name, n in (("ll_r", KD), ("ll_k", KD), ("ll_v", KD), ("ll_g", KD), ("ll_d", KD), ("xw", KD), ("u", KD),
                        ("init", KD * HD), ("ln_w", 1), ("ln_b", 1), ("w_ln1", KD), ("w_ln2", KD)):
            VEC[name] = vecs[:, at:at + n]
            at += n
        q_w = mem.take(KD, NH * 64)
        kva_w = mem.take(KD, ND + RD)
        kbuild = mem.take(NH // HEADS_PER_TILE, P)
        kvb_w = mem.take(NH * ND)
        wo_w = mem.take(NH // HGROUP, D)
        gate_w = mem.take(KD, ME)
        gate_b = mem.take(ME)
        eg_w = [mem.take(KD, MI) for _ in range(ME + 1)]
        eu_w = [mem.take(KD, MI) for _ in range(ME + 1)]
        ed_w = [mem.take(D) for _ in range(ME + 1)]
        mask_b = mem.take(P // 2).bitcast(BF16)
        ident_b = mem.take(P // 2).bitcast(BF16)
        x2, xn = mem.take(NT, D), mem.take(NT, D)
        proj = {x: mem.take(KD, T) for x in "rkvgw"}
        bonus = mem.take(KD, T)
        prods_at = mem.at
        prods = [mem.take(T) for _ in range(PRODS)]
        kv = mem.take(T)
        state_at = mem.at
        state = [mem.take(T + 1) for _ in range(2)]
        probs_at = mem.at
        probs = [mem.take(T) for _ in range(PROBS)]
        qT, kT = mem.take(NH // 2, T), mem.take(NH // 2, T)
        v_tok = mem.take(NT, NH * ND)
        turned_at = mem.at
        turned = [mem.take(NT, T) for _ in range(HGROUP)]
        neg_max, row_sum, row_inv = mem.take(STEPS), mem.take(STEPS), mem.take(STEPS)
        stats, mv = mem.take(NT, 6), mem.take(NT, 2)
        var_eps, rstd, ssq, rms = mem.take(NT), mem.take(NT), mem.take(NT), mem.take(NT)
        neg_half = mem.take(NT)
        idx = mem.take(NT).bitcast(U32)
        waste = mem.take(NT)
        logits = mem.take(NT, ME)
        route = [mem.take(NT, ME) for _ in range(4)]
        routs = [mem.take(NT) for _ in range(6)]
        early = Arena(mem.tensor, turned_at)
        x_in, s_in, g_in = early.take(NT, D), early.take(NT, D), early.take(NT, D)
        xnT, dxT, lerp = early.take(KD, T), early.take(KD, T), early.take(KD, T)
        mix = [early.take(KD, T) for _ in range(2)]
        early = Arena(mem.tensor, probs_at)
        th = [early.take(T) for _ in range(3)]
        silu_g = [th[0], th[1]]
        hid = [th[2], kv]
        early = Arena(mem.tensor, prods_at)
        xb = early.take(NT, D)
        xbT = early.take(KD, T)
        acc_at = early.at
        shuf = [early.take(T) for _ in range(2)]
        acc = Arena(mem.tensor, acc_at).take(NT, D)
        ckvT = Arena(mem.tensor, state_at).take(T)
        yT = [qT[:, 2 * i, :] for i in range(NH // HGROUP)]
        y = proj["r"]
        sq, inv = proj["v"], proj["k"]

        weights_in, ready_b = sem("weights_in"), sem("ready_b")
        kb_step = sem("kb_step")
        x_loaded, g_loaded, idx_set = sem("x_loaded"), sem("g_loaded"), sem("idx_set")
        stored = sem("stored")
        made = sem("made")
        made2 = sem("made2")
        a_read, v_read = sem("a_read"), sem("v_read")
        a_read2, v_read2 = sem("a_read2"), sem("v_read2")
        x2_step = sem("x2_step")
        var_done, rstd_done = sem("var_done"), sem("rstd_done")
        xn_done, ssq_done, ms_done, rms_done, xb_done = (sem(x) for x in ("xn_done", "ssq_done", "ms_done", "rms_done", "xb_done"))
        dx_step, lerp_done = sem("dx_step"), sem("lerp_done")
        mixed = sem("mixed")
        w_step = sem("w_step")
        turned_q = sem("turned_q")
        rope_step, rope_mul, init_set, pool_set = sem("rope_step"), sem("rope_mul"), sem("init_set"), sem("pool_set")
        ruk_done = sem("ruk_done")
        bonus_done = sem("bonus_done")
        (s_mm, s_max, s_exp, s_inv, s_norm, s_turn, s_keep, vrep, kv_done, scan_done, prod_done, red_mm, y_read, pv_mm,
         y_out) = (sem(x) for x in ("score_mm", "max", "exp", "rowinv", "norm", "turn", "keep", "vrep", "kv", "scan", "prod",
                                    "red", "y_read", "pv_mm", "y_out"))
        sq_done, inv_done, ln_step, o_done = (sem(x) for x in ("sq", "inv", "ln_step", "o_done"))
        gsilu = sem("gsilu")
        ssq2_done, ms2_done, rms2_done, xc_done = (sem(x) for x in ("ssq2", "ms2", "rms2", "xc"))
        top_step, comb_in, comb_out, comb_done = sem("top_step"), sem("comb_in"), sem("comb_out"), sem("comb_done")
        hid_done = sem("hid")
        f_done, out_ready = sem("f_done"), sem("out_ready")

        block = ctx.enter_context(nc.Block())
        NW = 17 + 3 * (ME + 1)

        @block.sync
        def _(sp):
            def load(dst, src):
                sp.dma_start(dst, src).then_inc(weights_in, 16)

            load(tail, io["const"][:, NCONST_A:NCONST])
            load(vecs, io["vecs"][:, :])
            load(la_w, io["laT"].rearrange("(k p) n -> p k n", p=P))
            load(lb_w, io["lbT"].rearrange("(g p) n -> p g n", p=P))
            for x in "rkvg":
                load(rkvg_w[x], io[x + "WT"].rearrange("(k p) n -> p k n", p=P))
            load(q_w, io["L1_ffn_Wq"].rearrange("(k p) n -> p k n", p=P))
            load(kva_w, io["L1_ffn_Wkva"].rearrange("(k p) n -> p k n", p=P))
            load(kvb_w[0:ND, :], io["L1_ffn_Wkvb"][:, :])
            sp.wait_ge(kb_step, 1)
            for h in range(HEADS_PER_TILE):
                load(kbuild[0:ND, :, 64 * h:64 * h + ND],
                     io["L1_ffn_Wkvb"].rearrange("p (t h n) -> p t h n", h=2, n=ND)[:, :, h, :])
            load(o_w, io["oWT"].rearrange("(k p) n -> p k n", p=P))
            load(wo_w, io["Wo"].rearrange("(g p) n -> p g n", p=P))
            load(gate_w, io["L1_ffn_Wgate"].rearrange("(k p) n -> p k n", p=P))
            load(gate_b, io["gate_b"][:, :].broadcast_to([P, ME]))
            for e in range(ME + 1):
                wg, wu, wd = ((io["L1_ffn_" + x][e] if e < ME else io["L1_ffn_s" + x][0]) for x in ("Wg", "Wu", "Wd"))
                load(eg_w[e], wg.rearrange("(k p) n -> p k n", p=P))
                load(eu_w[e], wu.rearrange("(k p) n -> p k n", p=P))
                load(ed_w[e], wd)
            x_rows = io["L0_attn_h"].rearrange("b t d -> (b t) d")
            out_rows = out.rearrange("b t d -> (b t) d")

            def load_sequence(b):
                sp.dma_start(x_in, x_rows[bass.ds(b * T, T), :].rearrange("(i p) d -> p i d", p=P)).then_inc(x_loaded, 16)
                sp.dma_start(s_in, dram["s"][bass.ds(b * T, T), :].rearrange("(i p) d -> p i d", p=P)).then_inc(x_loaded, 16)

            def store_sequence(b):
                sp.wait_ge(out_ready, b + 1)
                sp.dma_start(out_rows[bass.ds(b * T, T), :].rearrange("(i p) d -> p i d", p=P), x2).then_inc(stored, 16)

            load_sequence(0)
            with sp.Fori(0, B - 1) as b:
                sp.wait_ge(pv_mm, 4 * b + 4 + 4)
                load_sequence(b + 1)
                store_sequence(b)
            store_sequence(B - 1)
            sp.wait_ge(stored, 16 * B + 16)

        @block.tensor
        def _(pe):
            ident = const[:, 0:P]

            def begin(b, name, table, sems):
                old = table.before(name)
                if old is not None:
                    pe.wait_ge(sems[table.reader[old]], table.read(b, old))

            pre_read, post_read = {"a": a_read, "v": v_read}, {"a": a_read2, "v": v_read2, "h": hid_done}

            def product(b, name, pairs, width=T, rows=P):
                begin(b, name, pre, pre_read)
                dst = bank[pre.bank(name)]
                for n, (w, x) in enumerate(pairs):
                    last = nc.tensor.matmul(dst[0:rows, 0:width], w, x, start=(n == 0), stop=(n == len(pairs) - 1))
                last.then_inc(made, 1)

            def turn(dst, src, name, b, table, sems, signal):
                begin(b, name, table, sems)
                for i in range(NT):
                    last = nc.tensor.transpose(dst[:, i * P:(i + 1) * P], src(i), ident)
                last.then_inc(signal, 1)

            def lora_b(b, x, name, th_tile):
                g, r0 = PAIR[x]
                for m in range(KD):
                    product(b, f"lb_{name}{m}", [(lb_w[r0:r0 + LORA, g, m * P:(m + 1) * P], th_tile[r0:r0 + LORA, :])])

            def project(b, x):
                src = mix[MIX_ORDER.index(x) % 2]
                pe.wait_ge(mixed, 10 * b + 2 * MIX_ORDER.index(x) + 2)
                for m in range(KD):
                    product(b, f"pr_{x}{m}", [(rkvg_w[x][:, k, m * P:(m + 1) * P], src[:, k, :]) for k in range(KD)])

            def scores(b, s):
                h, qt = s // NT, s % NT
                dst, rows, n = bank[3 + s % 2], 64 * (h % 2), (qt + 1) * P
                if s >= 2:
                    pe.wait_ge(s_exp, STEPS * b + (s - 1))
                nc.tensor.matmul(dst[:, 0:n], qT[rows:rows + 64, h // 2, qt * P:(qt + 1) * P], kT[rows:rows + 64, h // 2, 0:n],
                                 start=True, stop=False)
                nc.tensor.matmul(dst[:, qt * P:n], ident_b, mask_b, start=False, stop=True).then_inc(s_mm, 1)

            def turn_probs(b, s):
                qt = s % NT
                pe.wait_ge(s_norm, STEPS * b + (s + 1))
                if s >= 2:
                    pe.wait_ge(s_keep, STEPS * b + (s - 1))
                for kt in range(qt + 1):
                    last = nc.tensor.transpose(bank[5 + s % 2][:, kt * P:(kt + 1) * P], probs[s % PROBS][:, kt * P:(kt + 1) * P], ident)
                last.then_inc(s_turn, 1)

            def replicate_v(b, n):
                if n >= 2:
                    pe.wait_ge(kv_done, UNITS * b + (n - 1))
                nc.tensor.matmul(bank[n % 2][:, :], sel[:, n % HD, :], proj["v"][:, n // HD, :], start=True, stop=True).then_inc(vrep, 1)

            def reduce_state(b, g):
                pe.wait_ge(prod_done, UNITS * b + (4 * g + 4))
                if g == 4:
                    pe.wait_ge(y_read, 2 * b + 1)
                for q in range(4):
                    last = nc.tensor.matmul(bank[2][32 * q:32 * q + 32, :], red[:, g % 4, :], prods[(4 * g + q) % PRODS],
                                            start=(g % 4 == 0), stop=(g % 4 == 3))
                last.then_inc(red_mm, 1)

            def weigh_values(b, g):
                pe.wait_ge(s_keep, STEPS * b + 4 * NT * (g + 1))
                if g:
                    pe.wait_ge(y_out, 4 * b + g)
                for kt in range(NT):
                    for i in range(HGROUP):
                        h = HGROUP * g + i
                        last = nc.tensor.matmul(bank[7][32 * i:32 * i + 32, kt * P:T], v_tok[:, kt, h * ND:(h + 1) * ND],
                                                turned[i][:, kt, kt * P:T], start=(kt == 0), stop=(kt == NT - 1))
                last.then_inc(pv_mm, 1)

            pe.wait_ge(weights_in, 16 * NW)
            pe.wait_ge(ready_b, 4)
            pe.sem_inc(pv_mm, NH // HGROUP)
            with pe.Fori(0, B) as b:
                pe.wait_ge(a_read2, len(post.order["a"]) * b + 1)
                pe.wait_ge(v_read2, len(post.order["v"]) * b + 1)
                pe.wait_ge(xn_done, b + 1)
                for k in range(KD):
                    turn(bank[pre.bank(f"t{k}")], lambda i: xn[:, i, k * P:(k + 1) * P], f"t{k}", b, pre, pre_read, made)
                pe.wait_ge(lerp_done, b + 1)
                for name, at, n in (("rk", 0, 2), ("vg", 2, 2), ("d", 4, 1)):
                    product(b, "la_" + name, [(la_w[:, k, at * LORA:(at + n) * LORA], lerp[:, k, :]) for k in range(KD)],
                            rows=n * LORA)
                pe.wait_ge(a_read, pre.read(b, "la_d"))
                lora_b(b, "d", "d", th[2])
                lora_b(b, "r", "r", th[0])
                pe.wait_ge(mixed, 10 * b + 2)
                product(b, "la_dd", [(la_w[:, k, 4 * LORA:5 * LORA], mix[0][:, k, :]) for k in range(KD)], rows=LORA)
                lora_b(b, "k", "k", th[0])
                project(b, "r")
                lora_b(b, "v", "v", th[1])
                project(b, "k")
                lora_b(b, "g", "g", th[1])
                project(b, "v")
                pe.wait_ge(a_read, pre.read(b, "la_dd"))
                lora_b(b, "d", "w", th[2])
                project(b, "g")
                pe.wait_ge(xb_done, b + 1)
                for k in range(KD):
                    turn(bank[pre.bank(f"xb{k}")], lambda i: xb[:, i, k * P:(k + 1) * P], f"xb{k}", b, pre, pre_read, made)
                pe.wait_ge(v_read, pre.read(b, "xb0"))
                pe.wait_ge(a_read, pre.read(b, "xb1"))
                product(b, "ckv", [(kva_w[:, k, :], xbT[:, k, :]) for k in range(KD)], rows=ND + RD)
                for i in range(NH // 2):
                    product(b, f"q{i}", [(q_w[:, k, i * P:(i + 1) * P], xbT[:, k, :]) for k in range(KD)])
                pe.wait_ge(ruk_done, 2 * b + 2)
                for m in range(KD):
                    product(b, f"sp{m}", [(spread, bonus[:, m, :])])
                pe.wait_ge(turned_q, 9 * b + 1)
                for i in range(NH // 2):
                    product(b, f"k{i}", [(kbuild[0:64, i, :], ckvT[0:64, :])])
                for i in range(NT):
                    product(b, f"v{i}", [(ckvT[0:ND, i * P:(i + 1) * P], kvb_w[0:ND, :])])
                pe.wait_ge(a_read, pre.read(b, f"v{NT - 1}"))
                pe.wait_ge(v_read, pre.read(b, "sp1"))
                pe.wait_ge(turned_q, 9 * b + 9)
                for s in range(STEPS + LAG + 2):
                    if s < STEPS:
                        scores(b, s)
                        if s % 2 == 0:
                            replicate_v(b, s // 2)
                    if s >= 16 + LAG and (s - LAG) % 16 == 0:
                        weigh_values(b, (s - LAG) // 16 - 1)
                    if LAG <= s < STEPS + LAG:
                        turn_probs(b, s - LAG)
                    if s >= 10 and (s - 10) % 8 == 0 and (s - 10) // 8 < 8:
                        reduce_state(b, (s - 10) // 8)
                def result(name, pairs, dst):
                    begin(b, name, post, post_read)
                    for n, (o, w, x, first, last_one) in enumerate(pairs):
                        last = nc.tensor.matmul(dst[o], w, x, start=first, stop=last_one)
                    last.then_inc(made2, 1)

                pe.wait_ge(y_out, 4 * b + 4)
                pe.wait_ge(y_read, 2 * b + 2)
                full = slice(None), slice(0, T)
                for m in range(KD):
                    result(f"mean{m}", [(full, mean_m, y[:, m, :], True, True)], bank[post.bank(f"mean{m}")])

                def by_tokens(name, tiles, lhs, rhs, n):
                    result(name, [((slice(None), slice((i % 2) * D, (i % 2 + 1) * D)), lhs(i, c), rhs(c), c == 0, c == n - 1)
                                  for i in tiles for c in range(n)], bank[post.bank(name)])

                for half in range(2):
                    by_tokens(f"wo{half}", (2 * half, 2 * half + 1), lambda i, c: yT[c][:, i * P:(i + 1) * P],
                              lambda c: wo_w[:, c, :], NH // HGROUP)
                pe.wait_ge(sq_done, 2 * b + 2)
                for m in range(KD):
                    result(f"var{m}", [(full, mean_m, sq[:, m, :], True, True)], bank[post.bank(f"var{m}")])
                pe.wait_ge(xc_done, b + 1)
                for k in range(KD):
                    turn(bank[post.bank(f"xc{k}")], lambda i: xb[:, i, k * P:(k + 1) * P], f"xc{k}", b, post, post_read, made2)
                pe.wait_ge(v_read2, post.read(b, "xc0"))
                pe.wait_ge(a_read2, post.read(b, "xc1"))
                result("gate", [((slice(None), slice(i * ME, (i + 1) * ME)), xbT[:, k, i * P:(i + 1) * P], gate_w[:, k, :],
                                 k == 0, k == KD - 1) for i in range(NT) for k in range(KD)], bank[post.bank("gate")])

                def up(e):
                    for x, w in (("g", eg_w[e]), ("u", eu_w[e])):
                        result(f"{x}{e}", [(full, w[:, k, :], xbT[:, k, :], k == 0, k == KD - 1) for k in range(KD)],
                               bank[post.bank(f"{x}{e}")])

                def down(e):
                    pe.wait_ge(hid_done, post.read(b, f"u{e}"))
                    for half, name in enumerate("ab"):
                        by_tokens(f"d{e}{name}", (2 * half, 2 * half + 1), lambda i, c: hid[e % 2][:, i * P:(i + 1) * P],
                                  lambda c: ed_w[e], 1)

                for e in range(ME + 2):
                    if e <= ME:
                        up(e)
                    if e:
                        down(e - 1)
                pe.wait_ge(o_done, 2 * b + 2)
                for half in range(2):
                    by_tokens(f"o{half}", (2 * half, 2 * half + 1), lambda i, c: y[:, c, i * P:(i + 1) * P],
                              lambda c: o_w[:, c, :], KD)

        @block.scalar
        def _(act):
            act.sem_inc(a_read, 1)
            act.sem_inc(a_read2, 1)
            act.sem_inc(stored, 16)
            act.wait_ge(weights_in, 16 * NW)
            with act.Fori(0, B) as b:
                def take(name, dst, func, **kw):
                    act.wait_ge(made, pre.made(b, name))
                    rows = dst.shape[0]
                    return nc.scalar.activation(dst, bank[pre.bank(name)][0:rows, :], func, **kw)

                act.wait_ge(xn_done, b + 1)
                for i in range(NT):
                    last = nc.scalar.activation(xb[:, i, :], xn[:, i, :], ACT.Square, accum_out=ssq[:, i:i + 1])
                last.then_inc(ssq_done, 1)
                take("t1", xnT[:, 1, :], ACT.Copy).then_inc(a_read, 1)
                for n, name in enumerate(("rk", "vg")):
                    take("la_" + name, th[n], ACT.Tanh).then_inc(a_read, 1)
                take("la_d", th[2][0:LORA, :], ACT.Tanh).then_inc(a_read, 1)
                act.wait_ge(made, pre.made(b, "lb_d1"))
                take("la_dd", th[2][0:LORA, :], ACT.Tanh).then_inc(a_read, 1)
                for x in "rkv":
                    for m in range(KD):
                        take(f"pr_{x}{m}", proj[x][:, m, :], ACT.Copy).then_inc(a_read, 1)
                    if x == "v":
                        for m in range(KD):
                            take(f"lb_w{m}", proj["w"][:, m, :], ACT.Exp, bias=VEC["ll_d"][:, m:m + 1]).then_inc(a_read, 1)
                            act.wait_ge(a_read, pre.read(b, f"lb_w{m}"))
                            nc.scalar.activation(proj["w"][:, m, :], proj["w"][:, m, :], ACT.Exp, scale=-1.0).then_inc(w_step, 1)
                for m in range(KD):
                    take(f"pr_g{m}", proj["g"][:, m, :], ACT.Copy).then_inc(a_read, 1)
                take("xb1", xbT[:, 1, :], ACT.Copy, scale=VEC["w_ln1"][:, 1:2]).then_inc(a_read, 1)
                for i in range(NH // 2):
                    take(f"k{i}", kT[:, i, :], ACT.Copy, scale=0.125).then_inc(a_read, 1)
                for i in range(NT):
                    take(f"v{i}", v_tok[:, i, :], ACT.Copy).then_inc(a_read, 1)

                def exp(s):
                    n = (s % NT + 1) * P
                    act.wait_ge(s_max, STEPS * b + (s + 1))
                    if s >= PROBS:
                        act.wait_ge(s_turn, STEPS * b + (s - PROBS + 1))
                    nc.scalar.activation(probs[s % PROBS][:, 0:n], bank[3 + s % 2][:, 0:n], ACT.Exp, bias=neg_max[:, s:s + 1],
                                         accum_out=row_sum[:, s:s + 1]).then_inc(s_exp, 1)

                def keep(s):
                    h, qt = s // NT, s % NT
                    act.wait_ge(s_turn, STEPS * b + (s + 1))
                    if h >= HGROUP and s % (HGROUP * NT) == 0:
                        act.wait_ge(pv_mm, 4 * b + h // HGROUP + 4)
                    nc.scalar.activation(turned[h % HGROUP][:, 0:qt + 1, qt * P:(qt + 1) * P],
                                         bank[5 + s % 2][:, 0:(qt + 1) * P].rearrange("p (k c) -> p k c", c=P),
                                         ACT.Copy).then_inc(s_keep, 1)

                for s in range(STEPS + LAG + 2):
                    if s >= 16 + LAG + 1 and (s - LAG - 1) % 16 == 0:
                        g = (s - LAG - 1) // 16 - 1
                        act.wait_ge(pv_mm, 4 * b + g + 5)
                        nc.scalar.activation(yT[g], bank[7][:, :], ACT.Copy).then_inc(y_out, 1)
                    if LAG < s <= STEPS + LAG:
                        keep(s - LAG - 1)
                    if s < STEPS:
                        exp(s)

                def take2(name, dst, func, **kw):
                    act.wait_ge(made2, post.made(b, name))
                    return nc.scalar.activation(dst, bank[post.bank(name)][:, :], func, **kw)

                for m in range(KD):
                    act.wait_ge(v_read2, post.read(b, f"var{m}"))
                    nc.scalar.activation(inv[:, m, :], inv[:, m, :], ACT.Sqrt).then_inc(inv_done, 1)
                for m in range(KD):
                    nc.scalar.activation(proj["g"][:, m, :], proj["g"][:, m, :], ACT.Silu).then_inc(gsilu, 1)
                act.wait_ge(v_read2, post.read(b, "wo1"))
                for i in range(NT):
                    last = nc.scalar.activation(xb[:, i, :], xn[:, i, :], ACT.Square, accum_out=ssq[:, i:i + 1])
                last.then_inc(ssq2_done, 1)
                take2("xc1", xbT[:, 1, :], ACT.Copy, scale=VEC["w_ln2"][:, 1:2]).then_inc(a_read2, 1)
                act.wait_ge(comb_in, 2 * b + 2)
                nc.scalar.activation(routs[4], routs[4], ACT.Tanh, scale=0.5).then_inc(comb_out, 1)
                take2("g0", silu_g[0], ACT.Silu).then_inc(a_read2, 1)
                take2("g1", silu_g[1], ACT.Silu).then_inc(a_read2, 1)
                for e in range(2, ME + 1):
                    act.wait_ge(hid_done, post.read(b, f"u{e - 2}"))
                    take2(f"g{e}", silu_g[e % 2], ACT.Silu).then_inc(a_read2, 1)
                act.wait_ge(v_read2, post.read(b, f"d{ME}b"))
                nc.scalar.activation(acc, acc, ACT.Silu).then_inc(f_done, 1)

        @block.vector
        def _(v):
            v.memset(kbuild[0:64, :, :], 0.0).then_inc(kb_step, 1)
            v.wait_ge(kb_step, 1)
            for h in range(HEADS_PER_TILE):
                v.tensor_copy(kbuild[ND:64, :, 64 * h + ND:64 * h + 64],
                              const[ND:64, ND:64].rearrange("p (o n) -> p o n", o=1).broadcast_to([RD, NH // 2, RD])).then_inc(ready_b, 1)
            v.sem_inc(v_read, 1)
            v.sem_inc(v_read2, 1)
            v.sem_inc(hid_done, 1)
            v.wait_ge(weights_in, 16 * NW)
            v.tensor_copy(mask_b, mask).then_inc(ready_b, 1)
            v.tensor_copy(ident_b, const[:, 0:P]).then_inc(ready_b, 1)
            with v.Fori(0, B) as b:
                step = Steps(4 * b)
                v.wait_ge(x_loaded, 32 * b + 32)
                v.wait_ge(g_loaded, 64 * b + 64)
                nc.vector.tensor_tensor(s_in, s_in, g_in, ALU.mult).then_inc(x2_step, 1)
                v.wait_ge(stored, 16 * b + 16)
                v.wait_ge(x2_step, step.next())
                nc.vector.tensor_tensor(x2, x_in, s_in, ALU.add).then_inc(x2_step, 1)
                v.wait_ge(x2_step, step.next())
                for i in range(NT):
                    last = nc.vector.bn_stats(stats[:, i, :], x2[:, i, :])
                last.then_inc(x2_step, 1)
                v.wait_ge(x2_step, step.next())
                nc.vector.memset(var_eps, EPS)
                for i in range(NT):
                    last = nc.vector.bn_aggr(mv[:, i, :], stats[:, i, :])
                last.then_inc(x2_step, 1)
                v.wait_ge(x2_step, step.next())
                nc.vector.tensor_scalar_add(var_eps, mv[:, :, 1], EPS).then_inc(var_done, 1)
                v.wait_ge(rstd_done, b + 1)
                for i in range(NT):
                    last = nc.vector.tensor_scalar(xn[:, i, :], x2[:, i, :], mv[:, i, 0:1], rstd[:, i:i + 1], ALU.subtract, ALU.mult)
                last.then_inc(xn_done, 1)
                v.wait_ge(made, pre.made(b, "t0"))
                nc.vector.tensor_copy(xnT[:, 0, :], bank[pre.bank("t0")][:, :]).then_inc(v_read, 1)
                v.wait_ge(v_read, pre.read(b, "t0"))
                v.wait_ge(a_read, pre.read(b, "t1"))
                nc.vector.tensor_scalar_mul(dxT[:, :, 0:1], xnT[:, :, 0:1], -1.0).then_inc(dx_step, 1)
                nc.vector.tensor_tensor(dxT[:, :, 1:T], xnT[:, :, 0:T - 1], xnT[:, :, 1:T], ALU.subtract).then_inc(dx_step, 1)
                v.wait_ge(dx_step, 2 * b + 2)
                for k in range(KD):
                    last = nc.vector.scalar_tensor_tensor(lerp[:, k, :], dxT[:, k, :], VEC["xw"][:, k:k + 1], xnT[:, k, :],
                                                          ALU.mult, ALU.add)
                last.then_inc(lerp_done, 1)
                v.wait_ge(ssq_done, b + 1)
                nc.vector.tensor_scalar(ssq, ssq, 1.0 / D, EPS, ALU.mult, ALU.add).then_inc(ms_done, 1)
                v.wait_ge(rms_done, b + 1)
                for i in range(NT):
                    last = nc.vector.tensor_scalar_mul(xb[:, i, :], xn[:, i, :], rms[:, i:i + 1])
                last.then_inc(xb_done, 1)
                for n, x in enumerate(MIX_ORDER):
                    if x == "k":
                        v.wait_ge(made, pre.made(b, "la_dd"))
                    elif n >= 2:
                        v.wait_ge(made, pre.made(b, f"pr_{MIX_ORDER[n - 2]}1"))
                    for m in range(KD):
                        name = f"lb_{x}{m}"
                        v.wait_ge(made, pre.made(b, name))
                        nc.vector.scalar_tensor_tensor(mix[n % 2][:, m, :], bank[pre.bank(name)][:, :], VEC["ll_" + x][:, m:m + 1],
                                                       dxT[:, m, :], ALU.add, ALU.mult).then_inc(v_read, 1)
                v.wait_ge(made, pre.made(b, "xb0"))
                nc.vector.tensor_scalar_mul(xbT[:, 0, :], bank[pre.bank("xb0")][:, :], VEC["w_ln1"][:, 0:1]).then_inc(v_read, 1)
                swap = [i ^ 1 for i in range(32)]
                for n in range(1 + NH // 2):
                    name, rows = ("ckv", 64) if n == 0 else (f"q{n - 1}", P)
                    dst = ckvT if n == 0 else qT[:, n - 1, :]
                    src = bank[pre.bank(name)]
                    v.wait_ge(made, pre.made(b, name))
                    if n >= 2:
                        v.wait_ge(turned_q, 9 * b + (n - 1))
                    nc.vector.tensor_tensor(dst[0:rows, :], src[0:rows, :], cos[0:rows, :], ALU.mult).then_inc(rope_step, 1)
                    nc.vector.stream_shuffle(shuf[n % 2][0:rows, :], src[0:rows, :], swap).then_inc(v_read, 1)
                v.wait_ge(a_read, pre.read(b, "pr_k1"))
                for m in range(KD):
                    nc.vector.scalar_tensor_tensor(bonus[:, m, :], proj["r"][:, m, :], VEC["u"][:, m:m + 1], proj["k"][:, m, :],
                                                   ALU.mult, ALU.mult).then_inc(ruk_done, 1)
                for m in range(KD):
                    v.wait_ge(made, pre.made(b, f"sp{m}"))
                    v.wait_ge(a_read, pre.read(b, f"pr_v{m}"))
                    nc.vector.tensor_tensor(bonus[:, m, :], bank[pre.bank(f"sp{m}")][:, :], proj["v"][:, m, :], ALU.mult).then_inc(v_read, 1)
                v.wait_ge(w_step, 2 * b + 2)

                def highest(s):
                    n = (s % NT + 1) * P
                    v.wait_ge(s_mm, STEPS * b + (s + 1))
                    nc.vector.tensor_reduce(neg_max[:, s:s + 1], bank[3 + s % 2][:, 0:n], X, ALU.max, negate=True).then_inc(s_max, 1)

                def invert(s):
                    v.wait_ge(s_exp, STEPS * b + (s + 1))
                    nc.vector.reciprocal(row_inv[:, s:s + 1], row_sum[:, s:s + 1]).then_inc(s_inv, 1)

                def outer(n):
                    v.wait_ge(vrep, UNITS * b + (n + 1))
                    if n:
                        v.wait_ge(scan_done, UNITS * b + n)
                    nc.vector.tensor_tensor(kv, bank[n % 2][:, :], proj["k"][:, n // HD, :], ALU.mult).then_inc(kv_done, 1)

                def scan(n):
                    m, j = n // HD, n % HD
                    v.wait_ge(kv_done, UNITS * b + (n + 1))
                    if n >= 2:
                        v.wait_ge(prod_done, UNITS * b + (n - 1))
                    nc.vector.tensor_tensor_scan(state[n % 2][:, 1:T + 1], proj["w"][:, m, :], kv,
                                                 VEC["init"][:, m * HD + j:m * HD + j + 1], ALU.mult, ALU.add).then_inc(scan_done, 1)

                def read_out(m):
                    v.wait_ge(red_mm, 8 * b + (4 * m + 4))
                    nc.vector.tensor_tensor(y[:, m, :], bank[2][:, :], bonus[:, m, :], ALU.add).then_inc(y_read, 1)

                for s in range(STEPS + LAG + 2):
                    if s < STEPS:
                        highest(s)
                    if 1 <= s <= STEPS:
                        invert(s - 1)
                    if s < STEPS:
                        outer(s // 2) if s % 2 == 0 else scan(s // 2)
                    if s in (35, 67):
                        read_out((s - 35) // 32)

                for m in range(KD):
                    v.wait_ge(made2, post.made(b, f"mean{m}"))
                    nc.vector.tensor_tensor(y[:, m, :], y[:, m, :], bank[post.bank(f"mean{m}")][:, :], ALU.subtract).then_inc(v_read2, 1)
                for half in range(2):
                    v.wait_ge(made2, post.made(b, f"wo{half}"))
                    nc.vector.tensor_tensor(xn[:, 2 * half:2 * half + 2, :], xn[:, 2 * half:2 * half + 2, :],
                                            bank[post.bank(f"wo{half}")][:, :].rearrange("p (i d) -> p i d", i=2), ALU.add).then_inc(v_read2, 1)
                for m in range(KD):
                    v.wait_ge(made2, post.made(b, f"var{m}"))
                    nc.vector.tensor_scalar_add(inv[:, m, :], bank[post.bank(f"var{m}")][:, :], EPS).then_inc(v_read2, 1)
                v.wait_ge(ssq2_done, b + 1)
                nc.vector.tensor_scalar(ssq, ssq, 1.0 / D, EPS, ALU.mult, ALU.add).then_inc(ms2_done, 1)
                v.wait_ge(rms2_done, b + 1)
                for i in range(NT):
                    last = nc.vector.tensor_scalar_mul(xb[:, i, :], xn[:, i, :], rms[:, i:i + 1])
                last.then_inc(xc_done, 1)
                v.wait_ge(made2, post.made(b, "xc0"))
                nc.vector.tensor_scalar_mul(xbT[:, 0, :], bank[post.bank("xc0")][:, :], VEC["w_ln2"][:, 0:1]).then_inc(v_read2, 1)
                iota = const[:, CONST["iota"][0]:CONST["iota"][0] + ME].rearrange("p (o e) -> p o e", o=1).broadcast_to([P, NT, ME])

                def wide(t):
                    return t.rearrange("p (t o) -> p t o", o=1).broadcast_to([P, NT, ME])

                v.wait_ge(made2, post.made(b, "gate"))
                bias = gate_b.rearrange("p (o e) -> p o e", o=1).broadcast_to([P, NT, ME])
                nc.vector.tensor_tensor(logits, bank[post.bank("gate")][:, 0:NT * ME].rearrange("p (t e) -> p t e", e=ME), bias,
                                        ALU.add).then_inc(v_read2, 1)
                v.wait_ge(v_read2, post.read(b, "gate"))
                tstep = Steps(10 * b)
                best, where = (routs[0], routs[1]), (routs[2], routs[3])
                for n in range(2):
                    hot = route[n]
                    nc.vector.tensor_reduce(best[n], logits, X, ALU.max).then_inc(top_step, 1)
                    v.wait_ge(top_step, tstep.next())
                    nc.vector.tensor_tensor(hot, logits, wide(best[n]), ALU.is_ge).then_inc(top_step, 1)
                    v.wait_ge(top_step, tstep.next())
                    nc.vector.scalar_tensor_tensor(hot, hot, -float(ME), iota, ALU.mult, ALU.add).then_inc(top_step, 1)
                    v.wait_ge(top_step, tstep.next())
                    nc.vector.tensor_reduce(where[n], hot, X, ALU.min).then_inc(top_step, 1)
                    v.wait_ge(top_step, tstep.next())
                    nc.vector.tensor_tensor(hot, hot, wide(where[n]), ALU.is_equal).then_inc(top_step, 1)
                    v.wait_ge(top_step, tstep.next())
                    if n == 0:
                        nc.vector.scalar_tensor_tensor(logits, hot, -3.0e38, logits, ALU.mult, ALU.add).then_inc(comb_in, 1)
                        v.wait_ge(comb_in, 2 * b + 1)
                nc.vector.tensor_tensor(routs[4], best[0], best[1], ALU.subtract).then_inc(comb_in, 1)
                v.wait_ge(comb_out, b + 1)
                nc.vector.tensor_scalar(routs[5], routs[4], -0.5, 0.5, ALU.mult, ALU.add).then_inc(comb_done, 1)
                nc.vector.tensor_scalar(routs[4], routs[4], 0.5, 0.5, ALU.mult, ALU.add).then_inc(comb_done, 1)
                v.wait_ge(comb_done, 5 * b + 2)
                nc.vector.tensor_tensor(route[0], route[0], wide(routs[4]), ALU.mult).then_inc(comb_done, 1)
                nc.vector.tensor_tensor(route[1], route[1], wide(routs[5]), ALU.mult).then_inc(comb_done, 1)
                v.wait_ge(comb_done, 5 * b + 4)
                nc.vector.tensor_tensor(route[2], route[0], route[1], ALU.add).then_inc(comb_done, 1)
                v.wait_ge(comb_done, 5 * b + 5)

                def hidden(e):
                    v.wait_ge(a_read2, post.read(b, f"g{e}"))
                    v.wait_ge(made2, post.made(b, f"u{e}"))
                    nc.vector.tensor_tensor(hid[e % 2], silu_g[e % 2], bank[post.bank(f"u{e}")][:, :], ALU.mult).then_inc(hid_done, 1)

                hidden(0)
                for e in range(ME + 1):
                    if e < ME:
                        hidden(e + 1)
                    for half, name in enumerate("ab"):
                        v.wait_ge(made2, post.made(b, f"d{e}{name}"))
                        if e:
                            v.wait_ge(v_read2, post.read(b, f"d{e - 1}{name}"))
                        for i in (2 * half, 2 * half + 1):
                            src = bank[post.bank(f"d{e}{name}")][:, (i % 2) * D:(i % 2 + 1) * D]
                            weight = route[2][:, i, e:e + 1] if e < ME else 1.0
                            base = xn[:, i, :] if e == 0 else acc[:, i, :]
                            last = nc.vector.scalar_tensor_tensor(acc[:, i, :], src, weight, base, ALU.mult, ALU.add)
                        last.then_inc(v_read2, 1)
                for m in range(KD):
                    v.wait_ge(inv_done, 2 * b + m + 1)
                    lstep = Steps(6 * b + 3 * m)
                    nc.vector.reciprocal(inv[:, m, :], inv[:, m, :]).then_inc(ln_step, 1)
                    v.wait_ge(ln_step, lstep.next())
                    nc.vector.tensor_tensor(y[:, m, :], y[:, m, :], inv[:, m, :], ALU.mult).then_inc(ln_step, 1)
                    v.wait_ge(ln_step, lstep.next())
                    nc.vector.tensor_scalar(y[:, m, :], y[:, m, :], VEC["ln_w"], VEC["ln_b"], ALU.mult, ALU.add).then_inc(ln_step, 1)
                    v.wait_ge(ln_step, lstep.next())
                    v.wait_ge(gsilu, 2 * b + m + 1)
                    nc.vector.tensor_tensor(y[:, m, :], y[:, m, :], proj["g"][:, m, :], ALU.mult).then_inc(o_done, 1)
                v.wait_ge(f_done, b + 1)
                for half in range(2):
                    v.wait_ge(made2, post.made(b, f"o{half}"))
                    nc.vector.tensor_tensor(acc[:, 2 * half:2 * half + 2, :], acc[:, 2 * half:2 * half + 2, :],
                                            bank[post.bank(f"o{half}")][:, :].rearrange("p (i d) -> p i d", i=2), ALU.mult).then_inc(v_read2, 1)
                v.wait_ge(v_read2, post.read(b, "o1"))
                nc.vector.tensor_tensor(x2, x2, acc, ALU.add).then_inc(out_ready, 1)

        @block.gpsimd
        def _(g):
            g.memset(neg_half, -0.5).then_inc(pool_set, 1)
            g.wait_ge(pool_set, 1)
            g.wait_ge(weights_in, 16 * NW)

            def gather(b):
                nc.gpsimd.tensor_copy(idx, pos_all[:, bass.ds(b * NT, NT)]).then_inc(idx_set, 1)
                g.wait_ge(idx_set, b + 1)
                nc.gpsimd.tensor_tensor(waste, neg_half, neg_half, ALU.mult)
                for i in range(NT):
                    g.indirect_dma_start(out=g_in[:, i, :], out_offset=None, in_=dram["g"][:, :],
                                         in_offset=bass.IndirectOffsetOnAxis(ap=idx[:, i:i + 1], axis=0)).then_inc(g_loaded, 16)

            gather(0)
            with g.Fori(0, B) as b:
                g.wait_ge(var_done, b + 1)
                nc.gpsimd.tensor_tensor(rstd, var_eps, neg_half, ALU.pow).then_inc(rstd_done, 1)
                g.wait_ge(ms_done, b + 1)
                nc.gpsimd.tensor_tensor(rms, ssq, neg_half, ALU.pow).then_inc(rms_done, 1)
                for n, x in enumerate(MIX_ORDER):
                    for m in range(KD):
                        g.wait_ge(v_read, pre.read(b, f"lb_{x}{m}"))
                        nc.gpsimd.tensor_tensor(mix[n % 2][:, m, :], mix[n % 2][:, m, :], xnT[:, m, :], ALU.add).then_inc(mixed, 1)
                for n in range(1 + NH // 2):
                    name, rows = ("ckv", 64) if n == 0 else (f"q{n - 1}", P)
                    dst = ckvT if n == 0 else qT[:, n - 1, :]
                    g.wait_ge(v_read, pre.read(b, name))
                    nc.gpsimd.tensor_tensor(shuf[n % 2][0:rows, :], shuf[n % 2][0:rows, :], sin[0:rows, :], ALU.mult).then_inc(rope_mul, 1)
                    g.wait_ge(rope_mul, 9 * b + (n + 1))
                    nc.gpsimd.tensor_tensor(dst[0:rows, :], dst[0:rows, :], shuf[n % 2][0:rows, :], ALU.add).then_inc(turned_q, 1)

                def norm(s):
                    n = (s % NT + 1) * P
                    g.wait_ge(s_inv, STEPS * b + (s + 1))
                    nc.gpsimd.tensor_tensor(probs[s % PROBS][:, 0:n], probs[s % PROBS][:, 0:n],
                                            row_inv[:, s:s + 1].broadcast_to([P, n]), ALU.mult).then_inc(s_norm, 1)

                def product(n):
                    m, j = n // HD, n % HD
                    nc.gpsimd.tensor_copy(state[n % 2][:, 0:1], VEC["init"][:, m * HD + j:m * HD + j + 1]).then_inc(init_set, 1)
                    g.wait_ge(init_set, UNITS * b + (n + 1))
                    g.wait_ge(scan_done, UNITS * b + (n + 1))
                    if n >= PRODS:
                        g.wait_ge(red_mm, 8 * b + (n - PRODS) // 4 + 1)
                    nc.gpsimd.tensor_tensor(prods[n % PRODS], state[n % 2][:, 0:T], proj["r"][:, m, :], ALU.mult).then_inc(prod_done, 1)

                for s in range(1, STEPS + 2):
                    if s <= STEPS:
                        norm(s - 1)
                    if s >= 2 and s % 2 == 0:
                        product(s // 2 - 1)
                g.wait_ge(pv_mm, 4 * b + 4 + 4)
                gather(b + 1)
                for m in range(KD):
                    g.wait_ge(v_read2, post.read(b, f"mean{m}"))
                    nc.gpsimd.tensor_tensor(sq[:, m, :], y[:, m, :], y[:, m, :], ALU.mult).then_inc(sq_done, 1)
                g.wait_ge(ms2_done, b + 1)
                nc.gpsimd.tensor_tensor(rms, ssq, neg_half, ALU.pow).then_inc(rms2_done, 1)
            g.wait_ge(g_loaded, 64 * (B + 1))


IN_NAMES = ["L0_attn_h", "L0_attn_W0", "L0_attn_W1", "centT", "W1T", "W2T", "const",
            "gammaT", "betaT", "b1T", "b2row", "vecs", "laT", "lbT", "rWT", "kWT", "vWT", "gWT", "oWT", "Wo", "gate_b",
            "L1_ffn_Wq", "L1_ffn_Wkva", "L1_ffn_Wkvb", "L1_ffn_Wgate", "L1_ffn_Wg", "L1_ffn_Wu", "L1_ffn_Wd",
            "L1_ffn_sWg", "L1_ffn_sWu", "L1_ffn_sWd"]


def build(nc, io, out):
    with ExitStack() as ctx:
        def scratch(name, shape):
            return nc.dram_tensor(name, shape, F32, kind="Internal").ap()

        dram = {"sorted": scratch("sorted_rows", (6 * (B - 1) * P, ROW)),
                "g": scratch("gate_rows", (SLOTS * P, D)),
                "s": scratch("s_rows", (B * T, D))}
        arena = ctx.enter_context(nc.sbuf_tensor("arena", [P, 53200], F32))
        bank = [ctx.enter_context(nc.psum_tensor(f"bank{i}", [P, 512], F32)) for i in range(8)]
        ffn_loaded = ctx.enter_context(nc.semaphore("ffn_loaded"))
        mem = Arena(arena)
        const = mem.take(NCONST_A)
        pos_all = mem.take(TILES + NT).bitcast(U32)
        after_pos = mem.at
        tile_expert = mem.take(SLOTS).bitcast(I32)
        w_at = mem.at
        w1s = mem.take(E * KD * F)
        w2s = mem.take(E * FC * D)
        assert 6 * (B - 1) >= SLOTS + 1
        spare = Arena(arena, w_at + (E - 1) * KD * F)
        phase_a(nc, io, dram, Arena(arena, mem.at), spare, const, bank, w1s, w2s, pos_all, tile_expert, ffn_loaded)
        phase_b(nc, io, dram, Arena(arena, mem.at), const, bank, w1s, w2s, tile_expert, ffn_loaded)
        phase_c(nc, io, dram, Arena(arena, after_pos), const, bank, pos_all, out)


def kernel(**inputs):
    import concourse.bacc as bacc
    from concourse.bass_utils import run_bass_kernel_spmd

    a = {k: np.asarray(x) for k, x in inputs.items()}
    a["centT"] = a["L0_ffn_centroids"].T
    a["W1T"] = a["L0_ffn_W1"].transpose(0, 2, 1).reshape(E * D, F)
    a["W2T"] = a["L0_ffn_W2"].transpose(0, 2, 1).reshape(E * F, D)
    for name, key in (("gammaT", "L0_ffn_gamma"), ("betaT", "L0_ffn_beta"), ("b1T", "L0_ffn_b1")):
        a[name] = a[key].reshape(-1, P).T
    a["b2row"] = a["L0_ffn_b2"].reshape(1, -1)
    order = np.zeros(P, np.int64)
    for h in range(HG):
        for j in range(HD):
            order[rho(h, j)] = h * HD + j
    both = np.concatenate([order, P + order])
    for x in "rkvg":
        w = a[f"L1_attn_{x}W"].T
        a[x + "WT"] = w[:, both] if x in "vg" else w
    a["oWT"] = a["L1_attn_oW"].T[both]
    a["laT"] = np.concatenate([a[f"L1_attn_{x}_la"].T for x in "rkvgd"], axis=1)
    a["lbT"] = np.concatenate([a[f"L1_attn_{x}_lb"].T for x in "rkvgd"] + [np.zeros((LORA, D), np.float32)])

    def columns(x):
        return x.reshape(KD, P, -1).transpose(1, 0, 2).reshape(P, -1)

    a["vecs"] = np.concatenate(
        [columns(a[f"L1_attn_{x}_ll"]) for x in "rkvgd"] + [columns(a["L1_attn_xw"]), columns(a["L1_attn_u"]),
         columns(a["L1_attn_init_state"].reshape(D, HD)), a["L1_attn_ln_w"][order % HD][:, None],
         a["L1_attn_ln_b"][order % HD][:, None], columns(a["L1_ffn_w_ln1"]), columns(a["L1_ffn_w_ln2"])], axis=1)
    a["Wo"] = a["L1_ffn_Wo"].reshape(NH, 64, D)[:, :ND].reshape(NH * ND, D)
    a["gate_b"] = a["L1_ffn_expert_bias"].reshape(1, ME)
    a["const"] = constants()
    nc = bacc.Bacc("TRN2", target_bir_lowering=False, num_devices=1)
    arrays, io = {}, {}
    for name in IN_NAMES:
        arrays["in_" + name] = np.ascontiguousarray(a[name])
        io[name] = nc.dram_tensor("in_" + name, arrays["in_" + name].shape, F32, kind="ExternalInput").ap()
    out = nc.dram_tensor("out_0", (B, T, D), F32, kind="ExternalOutput").ap()
    build(nc, io, out)
    r = run_bass_kernel_spmd(nc, [arrays], core_ids=[0])
    return r.results[0]["out_0"]
```

```python
from contextlib import ExitStack

import concourse.bass as bass
import numpy as np
from concourse import mybir

F32 = mybir.dt.float32
BF16 = mybir.dt.bfloat16
I32 = mybir.dt.int32
U32 = mybir.dt.uint32
ALU = mybir.AluOpType
ACT = mybir.ActivationFunctionType
X = mybir.AxisListType.X

P = 128
B, T, D = 8, 512, 256
NT = T // P
KD = D // P
TILES = B * NT
E, F = 8, 1024
FC = F // P
ROW = D + 1
SLOTS = TILES + E - 1
EPS = 1e-5
ROUTE_STEPS = 17
HD = 16
RING = 4
HG = P // HD
NH, ND, RD = 16, 32, 32
LORA = 64
ME, MI = 8, 128

CONST = {}
_at = 0
for _name, _n in (("ident", P), ("before", P), ("ones", P), ("iota", E), ("slot", SLOTS),
                  ("sel", HD * P // 2), ("red", HD // 4 * 32), ("spread", P), ("mean", P), ("mask", P),
                  ("cos", T), ("sin", T)):
    if _name == "sel":
        NCONST_A = _at
    CONST[_name] = (_at, _n)
    _at += _n
NCONST = _at


def rho(h, j):
    return 32 * (j % 4) + HG * (j // 4) + h


def constants():
    c = np.zeros((P, NCONST), np.float32)

    def put(name, a):
        at, n = CONST[name]
        c[:, at:at + n] = a

    p = np.arange(P)
    put("ident", np.eye(P))
    put("before", p[:, None] < p[None, :])
    put("ones", 1.0)
    put("iota", np.arange(E)[None, :])
    put("slot", np.arange(SLOTS)[None, :] * P)
    sel = np.zeros((P, HD, P), np.float32)
    red = np.zeros((P, HD // 4, 32), np.float32)
    spread = np.zeros((P, P), np.float32)
    mean = np.zeros((P, P), np.float32)
    for h in range(HG):
        for j in range(HD):
            sel[rho(h, j), j, h * HD:(h + 1) * HD] = 1.0
            spread[h * HD:(h + 1) * HD, rho(h, j)] = 1.0
            for i in range(HD):
                mean[rho(h, j), rho(h, i)] = 1.0 / HD
        for g in range(HD // 4):
            red[h * HD:(h + 1) * HD, g, HG * g + h] = 1.0
    put("sel", (sel.reshape(P, -1).astype(np.uint16) * 0x3F80).view(np.float32))
    put("red", red.reshape(P, -1))
    put("spread", spread)
    put("mean", mean)
    put("mask", np.where(p[None, :] > p[:, None], -1e30, 0.0))
    freqs = np.float32(1.0) / np.float32(100000.0) ** (np.arange(0, RD, 2, dtype=np.float32) / np.float32(RD))
    ang = np.outer(np.arange(T, dtype=np.float32), freqs)
    cos, sin = np.ones((P, T), np.float32), np.zeros((P, T), np.float32)
    for base in (ND, ND + 64):
        for r in range(RD):
            cos[base + r] = np.cos(ang[:, r // 2])
            sin[base + r] = np.sin(ang[:, r // 2]) * (1.0 if r % 2 else -1.0)
    put("cos", cos)
    put("sin", sin)
    return c


class Arena:

    def __init__(self, tensor, at=0):
        self.tensor, self.at = tensor, at

    def take(self, *shape):
        n = 1
        for s in shape:
            n *= s
        view = self.tensor[:, self.at:self.at + n]
        self.at += n
        assert self.at <= self.tensor.shape[1], self.at
        if len(shape) == 2:
            return view.rearrange("p (a b) -> p a b", a=shape[0])
        if len(shape) == 3:
            return view.rearrange("p (a b c) -> p a b c", a=shape[0], b=shape[1])
        return view


class Steps:

    def __init__(self, base):
        self.base, self.n = base, 0

    def next(self):
        self.n += 1
        return self.base + self.n


def phase_a(nc, io, dram, mem, spare, const, bank, w1s, w2s, pos_all, tile_expert, ffn_loaded):
    with ExitStack() as ctx:
        def sem(name):
            return ctx.enter_context(nc.semaphore("a_" + name))

        x_sb = mem.take(NT, D)
        xn = x_sb
        xn_all = mem.take(TILES, ROW)
        zeros = mem.take(ROW)
        stats = mem.take(NT, 6)
        mv = mem.take(NT, 2)
        var_eps = mem.take(NT)
        rstd = mem.take(NT)
        neg_half = mem.take(NT)
        h0 = mem.take(KD, T)
        h1 = mem.take(KD, T)
        h2 = spare.take(KD, T)
        gru_w = [mem.take(KD, 3 * D) for _ in range(2)]
        cent = mem.take(KD, E)
        sig_hidden, sig_gate = mem.take(T), mem.take(T)
        sig = [[sig_hidden, sig_gate, mem.take(T), mem.take(T), spare.take(T)] for _ in range(2)]
        scanned = mem.take(T)
        s_tok = mem.take(NT, D)
        scores = mem.take(TILES, E)
        top = mem.take(TILES)
        cand, onehot, incl, excl = (spare.take(TILES, E) for _ in range(4))
        slot_ge = spare.take(SLOTS, E)
        first, posf = spare.take(TILES), spare.take(TILES)
        pad_i = spare.take(E).bitcast(I32)
        padded, ends, starts = spare.take(E), spare.take(E), spare.take(E)
        slot_e = spare.take(SLOTS)

        const_in = sem("const_in")
        weights_in = sem("weights_in")
        x_in = sem("x_in")
        zeroed = sem("zeroed")
        zeros_set = sem("zeros_set")
        half_set = sem("half_set")
        xn_done = sem("xn_done")
        dve_step = sem("dve_step")
        rstd_done = sem("rstd_done")
        xn_kept = sem("xn_kept")
        xn_turned = sem("xn_turned")
        h0_left = sem("h0_left")
        h0_right = sem("h0_right")
        score_mm = sem("score_mm")
        scores_read = sem("scores_read")
        gru_mm = sem("gru_mm")
        gru_sig = sem("gru_sig")
        gru_read = sem("gru_read")
        gru_step = sem("gru_step")
        gru_scan = sem("gru_scan")
        kept_h = sem("kept_h")
        h_ready = sem("h_ready")
        s_turned = sem("s_turned")
        s_out = sem("s_out")
        s_stored = sem("s_stored")
        chain = sem("chain")
        route_mm = sem("route_mm")
        route_read = sem("route_read")
        pos_done = sem("pos_done")
        alpha_done = sem("alpha_done")
        top_done = sem("top_done")
        scattered = sem("scattered")

        NPER = 2 * NT + 1
        block = ctx.enter_context(nc.Block())
        h_rows = io["L0_attn_h"].rearrange("b t d -> (b t) d")

        @block.sync
        def _(sp):
            sp.dma_start(x_sb, h_rows[0:T, :].rearrange("(i p) d -> p i d", p=P)).then_inc(x_in, 16)
            sp.dma_start(const, io["const"][:, 0:NCONST_A]).then_inc(const_in, 16)
            for layer in range(2):
                sp.dma_start(gru_w[layer], io[f"L0_attn_W{layer}"].rearrange("(k p) n -> p k n", p=P)).then_inc(weights_in, 16)
            sp.dma_start(cent, io["centT"].rearrange("(k p) n -> p k n", p=P)).then_inc(weights_in, 16)
            sp.wait_ge(zeros_set, 1)

            def expert_weights(e):
                sp.dma_start(w1s[:, bass.ds(e * KD * F, KD * F)].rearrange("p (k f) -> p k f", k=KD),
                             io["W1T"][bass.ds(e * D, D), :].rearrange("(k p) f -> p k f", p=P)).then_inc(ffn_loaded, 16)
                sp.dma_start(w2s[:, bass.ds((E - 1) * FC * D - e * (FC * D), FC * D)].rearrange("p (k f) -> p k f", k=FC),
                             io["W2T"][bass.ds(e * F, F), :].rearrange("(k p) f -> p k f", p=P)).then_inc(ffn_loaded, 16)

            with sp.Fori(0, B - 1) as b:
                sp.wait_ge(xn_kept, b + 1)
                sp.wait_ge(xn_turned, 2 * b + 2)
                sp.dma_start(x_sb, h_rows[bass.ds(b * T + T, T), :].rearrange("(i p) d -> p i d", p=P)).then_inc(x_in, 16)
                expert_weights(b)
                for z in range(6):
                    sp.dma_start(dram["sorted"][bass.ds((6 * b + z) * P, P), :], zeros).then_inc(zeroed, 16)
            sp.wait_ge(h_ready, 4 * B + 2)
            sp.wait_ge(s_turned, 2 * B)
            sp.wait_ge(chain, ROUTE_STEPS)
            sp.wait_ge(pos_done, 1)
            expert_weights(B - 1)

        def sequences(engine, body):
            body(0)
            with engine.Fori(1, B - 1) as b:
                body(b)
            body(B - 1)

        def is_(b, n):
            return isinstance(b, int) and b == n

        @block.tensor
        def _(pe):
            ident = const[:, 0:P]

            def turn_in(b):
                pe.wait_ge(xn_done, NT * b + NT)
                for k in range(KD):
                    for i in range(NT):
                        last = nc.tensor.transpose(bank[6 + k][:, i * P:(i + 1) * P], xn[:, i, k * P:(k + 1) * P], ident)
                    last.then_inc(xn_turned, 1)

            def score(b):
                pe.wait_ge(h0_left, b + 1)
                pe.wait_ge(h0_right, b + 1)
                for i in range(NT):
                    for k in range(KD):
                        last = nc.tensor.matmul(bank[6][:, i * E:(i + 1) * E], h0[:, k, i * P:(i + 1) * P], cent[:, k, :],
                                                start=(k == 0), stop=(k == KD - 1))
                last.then_inc(score_mm, 1)

            def banks_free(b, u):
                pe.wait_ge(gru_sig, 20 * b + 5 * u + 5)
                pe.wait_ge(gru_read, 4 * b + u + 1)

            def gru_half(b, u, k):
                layer, m, s = u // 2, u % 2, 3 * (u % 2)
                src = h0 if layer == 0 else h1
                for q in range(3):
                    last = nc.tensor.matmul(bank[s + q][:, :], gru_w[layer][:, k, q * D + m * P:q * D + (m + 1) * P],
                                            src[:, k, :], start=(k == 0), stop=(k == KD - 1))
                if k == KD - 1:
                    last.then_inc(gru_mm, 1)

            def turn_out(b):
                pe.wait_ge(h_ready, 4 * b + 4 + 2)
                pe.wait_ge(scores_read, b + 1)
                for half in range(2):
                    for i in (2 * half, 2 * half + 1):
                        for m in range(KD):
                            last = nc.tensor.transpose(bank[6 + half][:, (i % 2) * D + m * P:(i % 2) * D + (m + 1) * P],
                                                       h2[:, m, i * P:(i + 1) * P], ident)
                    last.then_inc(s_turned, 1)

            def ranks():
                pe.wait_ge(chain, 4)
                oh = onehot.rearrange("p t e -> p (t e)")
                for n, name in enumerate(("before", "ones")):
                    at = CONST[name][0]
                    last = nc.tensor.matmul(bank[6 + n][:, 0:TILES * E], const[:, at:at + P], oh, start=True, stop=True)
                last.then_inc(route_mm, 1)

            def sequence(b):
                banks_free(b, 0)
                if is_(b, B - 1):
                    ranks()
                gru_half(b, 0, 0)
                gru_half(b, 0, 1)
                banks_free(b, 1)
                gru_half(b, 1, 0)
                gru_half(b, 1, 1)
                if not is_(b, 0):
                    if is_(b, B - 1):
                        pe.wait_ge(route_read, 1)
                    else:
                        pe.wait_ge(scores_read, b + 1)
                    turn_out(b - 1)
                for k in range(KD):
                    pe.wait_ge(h_ready, 4 * b + k + 1 + 2)
                    for u in (2, 3):
                        if k == 0:
                            banks_free(b, u)
                        gru_half(b, u, k)
                    if k == 0 and not is_(b, B - 1):
                        pe.wait_ge(s_out, 2 * b + 2)
                        turn_in(b + 1)
                if not is_(b, B - 1):
                    score(b + 1)

            pe.wait_ge(const_in, 16)
            pe.wait_ge(weights_in, 48)
            turn_in(0)
            score(0)
            sequences(pe, sequence)
            pe.wait_ge(s_out, 2 * B)
            turn_out(B - 1)

        @block.scalar
        def _(act):
            act.sem_inc(gru_sig, 10)
            act.sem_inc(s_out, 2)
            act.sem_inc(s_stored, 16)

            def right(b):
                act.wait_ge(xn_turned, 2 * b + 2)
                if not is_(b, 0):
                    act.wait_ge(kept_h, 4 * b - 2)
                nc.scalar.activation(h0[:, 1, :], bank[7][:, :], ACT.Copy).then_inc(h0_right, 1)

            def unit(b, u):
                s = 3 * (u % 2)
                act.wait_ge(gru_mm, 4 * b + u + 1)
                act.wait_ge(gru_scan, 4 * b + u + 2)
                act.wait_ge(h_ready, 4 * b + u + 1)
                for n, (q, scale) in enumerate(((0, 1.0), (1, 1.0), (1, -1.0), (2, 1.0), (2, -1.0))):
                    nc.scalar.activation(sig[u % 2][n], bank[s + q][:, :], ACT.Sigmoid, scale=scale).then_inc(gru_sig, 1)

            def store(b):
                act.wait_ge(s_stored, 16 * b + 16)
                for half in range(2):
                    act.wait_ge(s_turned, 2 * b + half + 1)
                    nc.scalar.activation(s_tok[:, 2 * half:2 * half + 2, :],
                                         bank[6 + half][:, :].rearrange("p (i d) -> p i d", i=2), ACT.Copy).then_inc(s_out, 1)
                act.wait_ge(s_out, 2 * b + 4)
                act.dma_start(dram["s"][bass.ds(b * T, T), :].rearrange("(i p) d -> p i d", p=P), s_tok).then_inc(s_stored, 16)

            def sequence(b):
                if is_(b, B - 1):
                    act.wait_ge(top_done, 1)
                    nc.scalar.activation(xn_all[:, :, D], top, ACT.Sigmoid).then_inc(alpha_done, 1)
                unit(b, 0)
                unit(b, 1)
                if not is_(b, 0):
                    store(b - 1)
                if not is_(b, B - 1):
                    right(b + 1)
                unit(b, 2)
                unit(b, 3)

            right(0)
            sequences(act, sequence)
            store(B - 1)
            act.wait_ge(s_stored, 16 * B + 16)

        @block.vector
        def _(v):
            v.memset(zeros, 0.0).then_inc(zeros_set, 1)
            v.sem_inc(gru_read, 2)
            v.sem_inc(gru_scan, 2)
            v.sem_inc(h_ready, 2)

            def norm(b):
                step = Steps(NPER * b)
                v.wait_ge(x_in, 16 * b + 16)
                for i in range(NT):
                    nc.vector.bn_stats(stats[:, i, :], x_sb[:, i, :]).then_inc(dve_step, 1)
                for i in range(NT):
                    got = step.next()
                v.wait_ge(dve_step, got)
                nc.vector.memset(var_eps, EPS)
                for i in range(NT):
                    nc.vector.bn_aggr(mv[:, i, :], stats[:, i, :]).then_inc(dve_step, 1)
                for i in range(NT):
                    got = step.next()
                v.wait_ge(dve_step, got)
                nc.vector.tensor_scalar_add(var_eps, mv[:, :, 1], EPS).then_inc(dve_step, 1)
                v.wait_ge(rstd_done, b + 1)
                for i in range(NT):
                    nc.vector.tensor_scalar(xn[:, i, :], x_sb[:, i, :], mv[:, i, 0:1], rstd[:, i:i + 1],
                                            ALU.subtract, ALU.mult).then_inc(xn_done, 1)

            def left(b):
                v.wait_ge(xn_turned, 2 * b + 1)
                if not is_(b, 0):
                    v.wait_ge(kept_h, 4 * b - 2)
                nc.vector.tensor_copy(h0[:, 0, :], bank[6][:, :]).then_inc(h0_left, 1)

            def read_scores(b):
                v.wait_ge(score_mm, b + 1)
                nc.vector.tensor_copy(scores.rearrange("p t e -> p (t e)")[:, bass.ds(b * NT * E, NT * E)],
                                      bank[6][:, 0:NT * E]).then_inc(scores_read, 1)

            def unit(b, u):
                hidden = bank[3 * (u % 2)]
                s_hid, s_gate, s_rest, s_proj, kept = sig[u % 2]
                at, n = 20 * b + 5 * u + 10, 4 * b + u
                link = Steps(12 * b + 3 * u)
                v.wait_ge(gru_sig, at + 1)
                nc.vector.tensor_scalar_min(s_hid, s_hid, 0.5).then_inc(gru_step, 1)
                v.wait_ge(gru_step, link.next())
                nc.vector.scalar_tensor_tensor(s_hid, hidden[:, :], 0.0, s_hid, ALU.max, ALU.add).then_inc(gru_read, 1)
                v.wait_ge(gru_read, n + 1 + 2)
                v.wait_ge(gru_sig, at + 2)
                nc.vector.tensor_tensor(s_gate, s_hid, s_gate, ALU.mult).then_inc(gru_step, 1)
                v.wait_ge(gru_step, link.next())
                v.wait_ge(gru_sig, at + 3)
                v.wait_ge(h_ready, n + 2)
                nc.vector.tensor_tensor_scan(scanned, s_rest, s_gate, 0.0, ALU.mult, ALU.add).then_inc(gru_scan, 1)
                v.wait_ge(gru_scan, n + 1 + 2)
                v.wait_ge(gru_sig, at + 4)
                nc.vector.tensor_tensor(scanned, scanned, s_proj, ALU.mult).then_inc(gru_step, 1)
                v.wait_ge(gru_step, link.next())
                if is_(b, B - 1):
                    v.wait_ge(gru_sig, at + 5)
                    if u == 1:
                        v.wait_ge(h0_right, b + 1)
                    src = h0 if u < 2 else h1
                    nc.vector.tensor_tensor(kept, kept, src[:, u % 2, :], ALU.mult).then_inc(kept_h, 1)
                v.wait_ge(kept_h, n + 1)
                dst = h1 if u < 2 else h2
                nc.vector.tensor_tensor(dst[:, u % 2, :], scanned, kept, ALU.add).then_inc(h_ready, 1)

            link = Steps(0)

            def hottest():
                v.wait_ge(scores_read, B)
                nc.vector.tensor_reduce(top, scores, X, ALU.max).then_inc(top_done, 1)
                v.wait_ge(top_done, 1)
                nc.vector.tensor_tensor(cand, scores, top.rearrange("p (t o) -> p t o", o=1).broadcast_to([P, TILES, E]),
                                        ALU.is_ge).then_inc(chain, 1)
                v.wait_ge(chain, link.next())
                iota = const[:, CONST["iota"][0]:CONST["iota"][0] + E].rearrange("p (o e) -> p o e", o=1).broadcast_to([P, TILES, E])
                nc.vector.scalar_tensor_tensor(cand, cand, -float(E), iota, ALU.mult, ALU.add).then_inc(chain, 1)
                v.wait_ge(chain, link.next())
                nc.vector.tensor_reduce(first, cand, X, ALU.min).then_inc(chain, 1)
                v.wait_ge(chain, link.next())
                nc.vector.tensor_tensor(onehot, cand, first.rearrange("p (t o) -> p t o", o=1).broadcast_to([P, TILES, E]),
                                        ALU.is_equal).then_inc(chain, 1)
                link.next()

            def positions():
                v.wait_ge(route_mm, 1)
                rank = bank[6][:, 0:TILES * E].rearrange("p (t e) -> p t e", e=E)
                counts = bank[7][:, 0:TILES * E].rearrange("p (t e) -> p t e", e=E)
                one = const[:, CONST["ones"][0]:CONST["ones"][0] + TILES]
                for e in range(E):
                    last = nc.vector.tensor_tensor_scan(incl[:, :, e], one, counts[:, :, e], 0.0, ALU.mult, ALU.add)
                last.then_inc(chain, 1)
                v.wait_ge(chain, link.next())
                nc.vector.tensor_tensor(excl, incl, counts, ALU.subtract).then_inc(chain, 1)
                nc.vector.tensor_scalar_add(pad_i, incl[:, TILES - 1, :], float(P - 1)).then_inc(chain, 1)
                link.next()
                v.wait_ge(chain, link.next())
                nc.vector.tensor_tensor(excl, excl, rank, ALU.add).then_inc(route_read, 1)
                nc.vector.tensor_single_scalar(pad_i, pad_i, 7, ALU.arith_shift_right).then_inc(chain, 1)
                v.wait_ge(chain, link.next())
                nc.vector.tensor_scalar_mul(padded, pad_i, float(P)).then_inc(chain, 1)
                v.wait_ge(chain, link.next())
                nc.vector.tensor_tensor_scan(ends, one[:, 0:E], padded, 0.0, ALU.mult, ALU.add).then_inc(chain, 1)
                v.wait_ge(chain, link.next())
                nc.vector.tensor_tensor(starts, ends, padded, ALU.subtract).then_inc(chain, 1)
                v.wait_ge(chain, link.next())
                v.wait_ge(route_read, 1)
                nc.vector.tensor_tensor(excl, excl, starts.rearrange("p (o e) -> p o e", o=1).broadcast_to([P, TILES, E]),
                                        ALU.add).then_inc(chain, 1)
                v.wait_ge(chain, link.next())
                nc.vector.tensor_tensor(excl, excl, onehot, ALU.mult).then_inc(chain, 1)
                v.wait_ge(chain, link.next())
                nc.vector.tensor_reduce(posf, excl, X, ALU.add).then_inc(chain, 1)
                v.wait_ge(chain, link.next())
                nc.vector.memset(pos_all[:, TILES:TILES + NT], 0)
                nc.vector.tensor_copy(pos_all[:, 0:TILES], posf).then_inc(pos_done, 1)
                slot = const[:, CONST["slot"][0]:CONST["slot"][0] + SLOTS].rearrange("p (t o) -> p t o", o=1).broadcast_to([P, SLOTS, E])
                nc.vector.tensor_tensor(slot_ge, slot, ends.rearrange("p (o e) -> p o e", o=1).broadcast_to([P, SLOTS, E]),
                                        ALU.is_ge).then_inc(chain, 1)
                v.wait_ge(chain, link.next())
                nc.vector.tensor_reduce(slot_e, slot_ge, X, ALU.add).then_inc(chain, 1)
                v.wait_ge(chain, link.next())
                nc.vector.tensor_scalar_min(tile_expert, slot_e, float(E - 1)).then_inc(chain, 1)
                v.wait_ge(chain, link.next())
                assert link.n == ROUTE_STEPS

            def sequence(b):
                if is_(b, B - 1):
                    hottest()
                    positions()
                unit(b, 0)
                if not is_(b, B - 1):
                    norm(b + 1)
                unit(b, 1)
                if not is_(b, B - 1):
                    left(b + 1)
                unit(b, 2)
                unit(b, 3)
                if not is_(b, B - 1):
                    read_scores(b + 1)

            norm(0)
            left(0)
            read_scores(0)
            sequences(v, sequence)

        @block.gpsimd
        def _(g):
            g.memset(neg_half, -0.5).then_inc(half_set, 1)
            g.wait_ge(half_set, 1)

            def norm(b):
                g.wait_ge(dve_step, NPER * b + NPER)
                nc.gpsimd.tensor_tensor(rstd, var_eps, neg_half, ALU.pow).then_inc(rstd_done, 1)

            def keep(b):
                g.wait_ge(xn_done, NT * b + NT)
                nc.gpsimd.tensor_copy(xn_all[:, bass.ds(b * NT, NT), 0:D], xn).then_inc(xn_kept, 1)

            def unit(b, u):
                src = h0 if u < 2 else h1
                if u >= 2:
                    g.wait_ge(h_ready, 4 * b + u - 1 + 2)
                else:
                    g.wait_ge(h0_left if u == 0 else h0_right, b + 1)
                g.wait_ge(gru_sig, 20 * b + 5 * u + 5 + 10)
                nc.gpsimd.tensor_tensor(sig[u % 2][4], sig[u % 2][4], src[:, u % 2, :], ALU.mult).then_inc(kept_h, 1)

            def scatter(t0, t1):
                for t in range(t0, t1):
                    g.indirect_dma_start(out=dram["sorted"][:, :],
                                         out_offset=bass.IndirectOffsetOnAxis(ap=pos_all[:, t:t + 1], axis=0),
                                         in_=xn_all[:, t, :], in_offset=None).then_inc(scattered, 16)

            def sequence(b):
                if is_(b, B - 1):
                    g.wait_ge(zeroed, 16 * 6 * (B - 1))
                    g.wait_ge(alpha_done, 1)
                    g.wait_ge(pos_done, 1)
                    scatter(0, TILES)
                else:
                    unit(b, 0)
                    norm(b + 1)
                    unit(b, 1)
                    keep(b + 1)
                    unit(b, 2)
                    unit(b, 3)

            norm(0)
            keep(0)
            sequences(g, sequence)
            g.wait_ge(scattered, 16 * TILES)


def phase_b(nc, io, dram, mem, const, bank, w1s, w2s, tile_expert, ffn_loaded, loads, weights_in):
    with ExitStack() as ctx:
        def sem(name):
            return ctx.enter_context(nc.semaphore("b_" + name))

        xs = [mem.take(ROW) for _ in range(RING)]
        n_tok = mem.take(D)
        stats, mv = mem.take(6), mem.take(2)
        var_eps, rstd, neg_half = mem.take(1), mem.take(1), mem.take(1)
        nT = [mem.take(KD, P) for _ in range(2)]
        z_sb = mem.take(F)
        hT = mem.take(FC, P)
        f_sb = [mem.take(D) for _ in range(2)]
        g_sb = [mem.take(D) for _ in range(RING)]
        gamma, beta = mem.take(E * KD), mem.take(E * KD)
        b1 = mem.take(E * FC)
        b2 = mem.take(E * D)
        turn_bank, z_bank, zT_bank, out_bank = bank[0], bank[1:3], bank[3:5], bank[5:7]

        small_in = sem("small_in")
        xs_in = [sem(f"xs_in{u}") for u in range(RING)]
        var_done = sem("var_done")
        stat_step = sem("stat_step")
        rstd_done = sem("rstd_done")
        n_done = sem("n_done")
        n_turned = sem("n_turned")
        nT_done = sem("nT_done")
        z_mm = sem("z_mm")
        z_left = sem("z_left")
        z_right = sem("z_right")
        z_turned = sem("z_turned")
        h_left = sem("h_left")
        h_right = sem("h_right")
        out_mm = sem("out_mm")
        f_done = sem("f_done")
        g_done = sem("g_done")
        g_stored = [sem(f"g_stored{u}") for u in range(RING)]

        ROUNDS = (SLOTS - 2) // RING
        REST = SLOTS - RING * ROUNDS
        assert 2 <= REST < RING
        block = ctx.enter_context(nc.Block())

        def tiles(engine, tile):
            with engine.Fori(0, ROUNDS) as j:
                for u in range(RING):
                    tile(RING * j + u, u)
            for u in range(REST):
                tile(RING * ROUNDS + u, u, min(2, REST - 1 - u))

        def expert_of(engine, k):
            return engine.value_load(tile_expert[0:1, bass.ds(k, 1)], min_val=0, max_val=E - 1)

        @block.sync
        def _(sp):
            for dst, name in ((gamma, "gammaT"), (beta, "betaT"), (b1, "b1T")):
                sp.dma_start(dst, io[name][:, :]).then_inc(small_in, 16)
            sp.dma_start(b2[0:1, :], io["b2row"][:, :]).then_inc(small_in, 16)
            for k in range(RING):
                sp.dma_start(xs[k], dram["sorted"][k * P:(k + 1) * P, :]).then_inc(xs_in[k], 16)

            for dst, src in loads:
                sp.dma_start(dst, src).then_inc(weights_in, 16)

            def store(k, u):
                sp.wait_ge(g_done, k + 1 + 2)
                sp.dma_start(dram["g"][bass.ds(k * P, P), :], g_sb[u]).then_inc(g_stored[u], 16)

            with sp.Fori(0, ROUNDS) as j:
                for u in range(RING):
                    k = RING * j + u
                    store(k, u)
                    sp.dma_start(xs[u], dram["sorted"][bass.ds((k + RING) * P, P), :]).then_inc(xs_in[u], 16)
            for u in range(REST):
                store(RING * ROUNDS + u, u)
            for u in range(RING):
                sp.wait_ge(xs_in[u], 16 * (ROUNDS + 1))
                sp.wait_ge(g_stored[u], 16 * (ROUNDS + (u < REST)) + 16)

        @block.tensor
        def _(pe):
            ident = const[:, 0:P]
            ones_row = const[0:1, CONST["ones"][0]:CONST["ones"][0] + P]

            def turn_norm(k):
                pe.wait_ge(n_done, k + 1)
                if not (isinstance(k, int) and k == 0):
                    pe.wait_ge(nT_done, k)
                for c in range(KD):
                    last = nc.tensor.transpose(turn_bank[:, c * P:(c + 1) * P], n_tok[:, c * P:(c + 1) * P], ident)
                last.then_inc(n_turned, 1)

            def expand(k, u):
                e = expert_of(pe, k)
                pe.wait_ge(nT_done, k + 1)
                for half in range(2):
                    for c in range(KD):
                        last = nc.tensor.matmul(z_bank[half][:, :], nT[u % 2][:, c, :],
                                                w1s[:, bass.ds(e * (KD * F) + (c * F + half * 512), 512)],
                                                start=(c == 0), stop=(c == KD - 1))
                last.then_inc(z_mm, 1)

            def turn_z(k):
                for half in range(2):
                    pe.wait_ge(z_left if half == 0 else z_right, k + 1)
                    for c in range(4):
                        last = nc.tensor.transpose(zT_bank[half][:, c * P:(c + 1) * P],
                                                   z_sb[:, half * 512 + c * P:half * 512 + (c + 1) * P], ident)
                    last.then_inc(z_turned, 1)

            def back(k, u):
                e = expert_of(pe, k)
                pe.wait_ge(f_done, k + 1)
                nc.tensor.matmul(out_bank[u % 2][:, 0:D], ones_row, b2[0:1, bass.ds(e * D, D)], start=True, stop=False)
                pe.wait_ge(h_left, k + 1)
                pe.wait_ge(h_right, k + 1)
                for c in range(FC):
                    last = nc.tensor.matmul(out_bank[u % 2][:, 0:D], hT[:, c, :],
                                            w2s[:, bass.ds((E - 1) * FC * D + c * D - e * (FC * D), D)], start=False, stop=(c == FC - 1))
                last.then_inc(out_mm, 1)

            pe.wait_ge(ffn_loaded, 16 * 2 * E)
            pe.wait_ge(small_in, 64)
            turn_norm(0)
            expand(0, 0)
            turn_norm(1)

            def tile(k, u, ahead=2):
                turn_z(k)
                if ahead >= 1:
                    expand(k + 1, u + 1)
                if ahead >= 2:
                    turn_norm(k + 2)
                back(k, u)

            tiles(pe, tile)

        @block.scalar
        def _(act):
            act.sem_inc(g_done, 2)
            for u in range(RING):
                act.sem_inc(g_stored[u], 16)

            def z_out(k):
                act.wait_ge(z_mm, k + 1)
                nc.scalar.activation(z_sb[:, 0:512], z_bank[0][:, :], ACT.Copy).then_inc(z_left, 1)

            def relu(k):
                e = expert_of(act, k)
                act.wait_ge(z_turned, 2 * k + 1)
                for c in range(4):
                    last = nc.scalar.activation(hT[:, c, :], zT_bank[0][:, c * P:(c + 1) * P], ACT.Relu,
                                                bias=b1[:, bass.ds(e * FC + c, 1)])
                last.then_inc(h_left, 1)

            def silu(k, u):
                act.wait_ge(g_stored[u], 4 * k - (4 * u - 16))
                act.wait_ge(f_done, k + 1 + 2)
                nc.scalar.activation(g_sb[u], f_sb[u % 2], ACT.Silu).then_inc(g_done, 1)

            act.wait_ge(small_in, 64)
            z_out(0)

            def tile(k, u, ahead=2):
                relu(k)
                if ahead >= 1:
                    z_out(k + 1)
                silu(k, u)

            tiles(act, tile)

        @block.vector
        def _(v):
            v.sem_inc(f_done, 2)
            v.wait_ge(small_in, 64)

            def norm(k, u):
                step = Steps(2 * k)
                v.wait_ge(xs_in[u % RING], 4 * k - (4 * (u % RING) - 16))
                nc.vector.bn_stats(stats, xs[u % RING][:, 0:D]).then_inc(stat_step, 1)
                v.wait_ge(stat_step, step.next())
                nc.vector.memset(var_eps, EPS)
                nc.vector.bn_aggr(mv, stats).then_inc(stat_step, 1)
                v.wait_ge(stat_step, step.next())
                nc.vector.tensor_scalar_add(var_eps, mv[:, 1:2], EPS).then_inc(var_done, 1)
                v.wait_ge(rstd_done, k + 1)
                nc.vector.tensor_scalar(n_tok, xs[u % RING][:, 0:D], mv[:, 0:1], rstd, ALU.subtract, ALU.mult).then_inc(n_done, 1)

            def scale_norm(k, u):
                e = expert_of(v, k)
                v.wait_ge(n_turned, k + 1)
                for c in range(KD):
                    last = nc.vector.tensor_scalar(nT[u % 2][:, c, :], turn_bank[:, c * P:(c + 1) * P], gamma[:, bass.ds(e * KD + c, 1)],
                                                   beta[:, bass.ds(e * KD + c, 1)], ALU.mult, ALU.add)
                last.then_inc(nT_done, 1)

            def z_out(k):
                v.wait_ge(z_mm, k + 1)
                nc.vector.tensor_copy(z_sb[:, 512:1024], z_bank[1][:, :]).then_inc(z_right, 1)

            def relu(k):
                e = expert_of(v, k)
                v.wait_ge(z_turned, 2 * k + 2)
                for c in range(4):
                    last = nc.vector.tensor_scalar(hT[:, 4 + c, :], zT_bank[1][:, c * P:(c + 1) * P],
                                                   b1[:, bass.ds(e * FC + (4 + c), 1)], 0.0, ALU.add, ALU.max)
                last.then_inc(h_right, 1)

            def finish(k, u):
                v.wait_ge(out_mm, k + 1)
                v.wait_ge(g_done, k + 1)
                nc.vector.scalar_tensor_tensor(f_sb[u % 2], out_bank[u % 2][:, 0:D], xs[u][:, D:D + 1], xs[u][:, 0:D],
                                               ALU.mult, ALU.add).then_inc(f_done, 1)

            norm(0, 0)
            scale_norm(0, 0)
            norm(1, 1)
            z_out(0)
            scale_norm(1, 1)

            def tile(k, u, ahead=2):
                relu(k)
                if ahead >= 2:
                    norm(k + 2, u + 2)
                if ahead >= 1:
                    z_out(k + 1)
                if ahead >= 2:
                    scale_norm(k + 2, u + 2)
                finish(k, u)

            tiles(v, tile)

        @block.gpsimd
        def _(g):
            g.memset(neg_half, -0.5).then_inc(n_set := sem("neg_set"), 1)
            g.wait_ge(n_set, 1)
            with g.Fori(0, SLOTS) as k:
                g.wait_ge(var_done, k + 1)
                nc.gpsimd.tensor_tensor(rstd, var_eps, neg_half, ALU.pow).then_inc(rstd_done, 1)


PAIR = {"r": (0, 0), "k": (0, 64), "v": (1, 0), "g": (1, 64), "d": (2, 0)}
MIX_ORDER = "drkvg"
HEADS_PER_TILE = 2
HGROUP = 4
STEPS = NH * NT
UNITS = KD * HD
LAG = 3
PROBS = 3
PRODS = 6


class Outputs:

    def __init__(self, table, nbank, first=0, credit=1):
        self.at = {name: n for n, (name, _) in enumerate(table)}
        self.reader = {name: who for name, who in table}
        self.n = len(table)
        self.names = [name for name, _ in table]
        self.order = {who: [x for x, w in table if w == who] for who in "avh"}
        self.nbank, self.first, self.credit = nbank, first, credit

    def bank(self, name):
        return (self.at[name] + self.first) % self.nbank

    def before(self, name):
        n = self.at[name] - self.nbank
        return self.names[n] if n >= 0 else None

    def made(self, b, name):
        return self.n * b + (self.at[name] + 1)

    def read(self, b, name):
        mine = self.order[self.reader[name]]
        return len(mine) * b + (mine.index(name) + 1 + self.credit)


SECOND = 10320
QKV = "q0 q1 sp0 sp1 q2 k0 k1 q3 k2 v0 q4 k3 v1 q5 k4 v2 q6 k5 v3 q7 k6 k7".split()
PRE = ([("la_rk", "a"), ("la_vg", "a"), ("la_d", "a"),
        ("lb_d0", "v"), ("lb_d1", "v"), ("lb_r0", "v"), ("lb_r1", "v"), ("la_dd", "a"), ("lb_k0", "v"), ("lb_k1", "v"),
        ("pr_r0", "a"), ("pr_r1", "a"), ("lb_v0", "v"), ("lb_v1", "v"), ("pr_k0", "a"), ("pr_k1", "a"),
        ("lb_g0", "v"), ("lb_g1", "v"), ("pr_v0", "a"), ("pr_v1", "a"), ("lb_w0", "a"), ("lb_w1", "a"),
        ("pr_g0", "a"), ("pr_g1", "a"), ("xb0", "v"), ("xb1", "a"), ("ckv", "v")]
       + [(x, "v" if x[0] in "qs" else "a") for x in QKV])
def _experts():
    for e in range(ME + 2):
        if e <= ME:
            yield from ((f"g{e}", "a"), (f"u{e}", "h"))
        if e:
            yield from ((f"d{e - 1}a", "v"), (f"d{e - 1}b", "v"))


POST = ([("mean0", "v"), ("wo0", "v"), ("wo1", "v"), ("mean1", "v"), ("var0", "v"),
         ("xc0", "v"), ("xc1", "a"), ("var1", "v"), ("gate", "v")] + list(_experts()) + [("o0", "v"), ("o1", "v")])


def second_weights(top, io):
    w = {"tail": top.take(NCONST - NCONST_A), "vecs": top.take(io["vecs"].shape[1]), "la_w": top.take(KD, 5 * LORA),
         "lb_w": top.take(3, D), "rkvg_w": {x: top.take(KD, D) for x in "rkvg"}, "kva_w": top.take(KD, ND + RD),
         "q_w": top.take(KD, NH * 64), "kvb_w": top.take(NH * ND), "o_w": top.take(KD, D),
         "wo_w": top.take(NH // HGROUP, D), "gate_w": top.take(KD, ME), "gate_b": top.take(ME)}
    loads = [(w["tail"], io["const"][:, NCONST_A:NCONST]), (w["vecs"], io["vecs"][:, :]),
             (w["lb_w"], io["lbT"].rearrange("(g p) n -> p g n", p=P)), (w["kvb_w"][0:ND, :], io["L1_ffn_Wkvb"][:, :]),
             (w["wo_w"], io["Wo"].rearrange("(g p) n -> p g n", p=P)), (w["gate_b"], io["gate_b"][:, :].broadcast_to([P, ME]))]
    for dst, name in ([(w["la_w"], "laT"), (w["kva_w"], "L1_ffn_Wkva"), (w["q_w"], "L1_ffn_Wq"), (w["o_w"], "oWT"),
                       (w["gate_w"], "L1_ffn_Wgate")] + [(w["rkvg_w"][x], x + "WT") for x in "rkvg"]):
        loads.append((dst, io[name].rearrange("(k p) n -> p k n", p=P)))
    return w, loads


def phase_c(nc, io, dram, mem, const, bank, pos_all, second, second_loads, weights_in, out):
    with ExitStack() as ctx:
        def sem(name):
            return ctx.enter_context(nc.semaphore("c_" + name))

        pre = Outputs(PRE, 8)
        post = Outputs(POST, 8, first=(8 - len(POST)) % 8, credit=3)
        last_g, last_u = f"g{ME}", f"u{ME}"
        tail, vecs, la_w, lb_w, rkvg_w, q_w, kva_w, kvb_w, o_w, wo_w, gate_w, gate_b = (
            second[x] for x in "tail vecs la_w lb_w rkvg_w q_w kva_w kvb_w o_w wo_w gate_w gate_b".split())

        def table(name):
            at = CONST[name][0] - NCONST_A
            return tail[:, at:at + CONST[name][1]]

        sel, red = table("sel").bitcast(BF16).rearrange("p (j c) -> p j c", j=HD), table("red").rearrange("p (g c) -> p g c", c=32)
        spread, mean_m, mask, cos, sin = (table(x) for x in ("spread", "mean", "mask", "cos", "sin"))
        VEC = {}
        at = 0
        for name, n in (("ll_r", KD), ("ll_k", KD), ("ll_v", KD), ("ll_g", KD), ("ll_d", KD), ("xw", KD), ("u", KD),
                        ("init", KD * HD), ("ln_w", 1), ("ln_b", 1), ("w_ln1", KD), ("w_ln2", KD)):
            VEC[name] = vecs[:, at:at + n]
            at += n
        kbuild = mem.take(NH // HEADS_PER_TILE, P)
        eg_w = [mem.take(KD, MI) for _ in range(ME + 1)]
        eu_w = [mem.take(KD, MI) for _ in range(ME + 1)]
        ed_w = [mem.take(D) for _ in range(ME + 1)]
        mask_b = mem.take(P // 2).bitcast(BF16)
        ident_b = mem.take(P // 2).bitcast(BF16)
        x2, xn = mem.take(NT, D), mem.take(NT, D)
        proj = {x: mem.take(KD, T) for x in "rkvgw"}
        bonus = mem.take(KD, T)
        v_hi = [mem.take(T // 2).bitcast(BF16) for _ in range(KD)]
        left_over = [mem.take(T // 2), mem.take(T // 2), proj["v"][:, 0, 0:T // 2], proj["v"][:, 0, T // 2:T]]
        v_mid = [left_over[0].bitcast(BF16), left_over[2].bitcast(BF16)]
        v_lo = [left_over[1].bitcast(BF16), left_over[3].bitcast(BF16)]
        prods_at = mem.at
        prods = [mem.take(T) for _ in range(PRODS)]
        kv = mem.take(T)
        state_at = mem.at
        state = [mem.take(T + 1) for _ in range(2)]
        probs_at = mem.at
        probs = [mem.take(T) for _ in range(PROBS)]
        qT, kT = mem.take(NH // 2, T), mem.take(NH // 2, T)
        v_tok = mem.take(NT, NH * ND)
        turned_at = mem.at
        turned = [mem.take(NT, T) for _ in range(HGROUP)]
        neg_max, row_sum, row_inv = mem.take(STEPS), mem.take(STEPS), mem.take(STEPS)
        stats, mv = mem.take(NT, 6), mem.take(NT, 2)
        var_eps, rstd, ssq, rms = mem.take(NT), mem.take(NT), mem.take(NT), mem.take(NT)
        neg_half = mem.take(NT)
        idx = mem.take(NT).bitcast(U32)
        waste = mem.take(NT)
        logits = mem.take(NT, ME)
        route = [mem.take(NT, ME) for _ in range(4)]
        routs = [mem.take(NT) for _ in range(6)]
        early = Arena(mem.tensor, turned_at)
        x_in, s_in, g_in = early.take(NT, D), early.take(NT, D), early.take(NT, D)
        xnT, dxT, lerp = early.take(KD, T), early.take(KD, T), early.take(KD, T)
        mix = [early.take(KD, T) for _ in range(2)]
        early = Arena(mem.tensor, probs_at)
        th = [early.take(T) for _ in range(3)]
        silu_g = [th[0], th[1]]
        hid = [th[2], kv]
        early = Arena(mem.tensor, prods_at)
        xb = early.take(NT, D)
        xbT = early.take(KD, T)
        acc_at = early.at
        shuf = [early.take(T) for _ in range(2)]
        acc = Arena(mem.tensor, acc_at).take(NT, D)
        ckvT = Arena(mem.tensor, state_at).take(T)
        yT = [qT[:, 2 * i, :] for i in range(NH // HGROUP)]
        y = proj["r"]
        sq, inv = proj["v"], proj["k"]

        ready_b = sem("ready_b")
        kb_step = sem("kb_step")
        x_loaded, g_loaded, idx_set = sem("x_loaded"), sem("g_loaded"), sem("idx_set")
        xn_turned, xnT_left, xnT_right = sem("xn_turned"), sem("xnT_left"), sem("xnT_right")
        x2_kept = sem("x2_kept")
        v_hi_done, v_res_done, v_mid_done, v_lo_done = (sem(x) for x in ("v_hi", "v_res", "v_mid", "v_lo"))
        moe_in = sem("moe_in")
        stored = sem("stored")
        made = sem("made")
        made2 = sem("made2")
        a_read, v_read = sem("a_read"), sem("v_read")
        a_read2, v_read2 = sem("a_read2"), sem("v_read2")
        x2_step = sem("x2_step")
        var_done, rstd_done = sem("var_done"), sem("rstd_done")
        xn_done, ssq_done, ms_done, rms_done, xb_done = (sem(x) for x in ("xn_done", "ssq_done", "ms_done", "rms_done", "xb_done"))
        dx_step, lerp_done = sem("dx_step"), sem("lerp_done")
        mixed = sem("mixed")
        w_step = sem("w_step")
        turned_q = sem("turned_q")
        rope_step, rope_mul, init_set, pool_set = sem("rope_step"), sem("rope_mul"), sem("init_set"), sem("pool_set")
        ruk_done = sem("ruk_done")
        bonus_done = sem("bonus_done")
        (s_mm, s_max, s_exp, s_inv, s_norm, s_turn, s_keep, vrep, kv_done, scan_done, prod_done, red_mm, y_read, pv_mm,
         y_out) = (sem(x) for x in ("score_mm", "max", "exp", "rowinv", "norm", "turn", "keep", "vrep", "kv", "scan", "prod",
                                    "red", "y_read", "pv_mm", "y_out"))
        s_norm_long = sem("norm_long")
        sq_done, inv_done, ln_step, o_done = (sem(x) for x in ("sq", "inv", "ln_step", "o_done"))
        gsilu = sem("gsilu")
        ssq2_done, ms2_done, rms2_done, xc_done = (sem(x) for x in ("ssq2", "ms2", "rms2", "xc"))
        top_step, comb_in, comb_out, comb_done = sem("top_step"), sem("comb_in"), sem("comb_out"), sem("comb_done")
        hid_done = sem("hid")
        f_done, out_ready = sem("f_done"), sem("out_ready")

        block = ctx.enter_context(nc.Block())
        NW = second_loads + HEADS_PER_TILE

        @block.sync
        def _(sp):
            def load(dst, src):
                sp.dma_start(dst, src).then_inc(weights_in, 16)

            sp.dma_start(x_in, io["L0_attn_h"][0].rearrange("(i p) d -> p i d", p=P)).then_inc(x_loaded, 16)
            sp.dma_start(s_in, dram["s"][0:T, :].rearrange("(i p) d -> p i d", p=P)).then_inc(x_loaded, 16)
            sp.wait_ge(kb_step, 1)
            for h in range(HEADS_PER_TILE):
                load(kbuild[0:ND, :, 64 * h:64 * h + ND],
                     io["L1_ffn_Wkvb"].rearrange("p (t h n) -> p t h n", h=2, n=ND)[:, :, h, :])
            x_rows = io["L0_attn_h"].rearrange("b t d -> (b t) d")
            out_rows = out.rearrange("b t d -> (b t) d")

            def load_sequence(b):
                sp.dma_start(x_in, x_rows[bass.ds(b * T, T), :].rearrange("(i p) d -> p i d", p=P)).then_inc(x_loaded, 16)
                sp.dma_start(s_in, dram["s"][bass.ds(b * T, T), :].rearrange("(i p) d -> p i d", p=P)).then_inc(x_loaded, 16)

            def store_sequence(b):
                sp.wait_ge(out_ready, b + 1 + 1)
                sp.dma_start(out_rows[bass.ds(b * T, T), :].rearrange("(i p) d -> p i d", p=P), acc).then_inc(stored, 16)

            for e in range(ME + 1):
                wg, wu, wd = ((io["L1_ffn_" + x][e] if e < ME else io["L1_ffn_s" + x][0]) for x in ("Wg", "Wu", "Wd"))
                sp.dma_start(eg_w[e], wg.rearrange("(k p) n -> p k n", p=P)).then_inc(moe_in, 16)
                sp.dma_start(eu_w[e], wu.rearrange("(k p) n -> p k n", p=P)).then_inc(moe_in, 16)
                sp.dma_start(ed_w[e], wd).then_inc(moe_in, 16)
            with sp.Fori(0, B - 1) as b:
                sp.wait_ge(pv_mm, 4 * b + 4 + 4)
                load_sequence(b + 1)
                store_sequence(b)
            sp.wait_ge(pv_mm, 4 * (B - 1) + 4 + 4)
            load_sequence(B - 1)
            store_sequence(B - 1)
            sp.wait_ge(x_loaded, 32 * (B + 1))
            sp.wait_ge(stored, 16 * B + 16)

        @block.tensor
        def _(pe):
            ident = const[:, 0:P]

            def begin(b, name, table, sems):
                old = table.before(name)
                if old is not None:
                    pe.wait_ge(sems[table.reader[old]], table.read(b, old))

            pre_read, post_read = {"a": a_read, "v": v_read}, {"a": a_read2, "v": v_read2, "h": hid_done}

            def product(b, name, pairs, width=T, rows=P):
                begin(b, name, pre, pre_read)
                dst = bank[pre.bank(name)]
                for n, (w, x) in enumerate(pairs):
                    last = nc.tensor.matmul(dst[0:rows, 0:width], w, x, start=(n == 0), stop=(n == len(pairs) - 1))
                last.then_inc(made, 1)

            def turn(dst, src, name, b, table, sems, signal):
                begin(b, name, table, sems)
                for i in range(NT):
                    last = nc.tensor.transpose(dst[:, i * P:(i + 1) * P], src(i), ident)
                last.then_inc(signal, 1)

            def lora_b(b, x, name, th_tile):
                g, r0 = PAIR[x]
                for m in range(KD):
                    product(b, f"lb_{name}{m}", [(lb_w[r0:r0 + LORA, g, m * P:(m + 1) * P], th_tile[r0:r0 + LORA, :])])

            def project(b, x):
                src = mix[MIX_ORDER.index(x) % 2]
                pe.wait_ge(mixed, 10 * b + 2 * MIX_ORDER.index(x) + 2)
                for m in range(KD):
                    product(b, f"pr_{x}{m}", [(rkvg_w[x][:, k, m * P:(m + 1) * P], src[:, k, :]) for k in range(KD)])

            def scores(b, s):
                h, qt = s // NT, s % NT
                dst, rows, n = bank[3 + s % 2], 64 * (h % 2), (qt + 1) * P
                if s % (HEADS_PER_TILE * NT) == 0:
                    pe.wait_ge(turned_q, 9 * b + (h // HEADS_PER_TILE + 2))
                if s >= 2:
                    pe.wait_ge(s_exp, STEPS * b + (s - 1))
                nc.tensor.matmul(dst[:, 0:n], qT[rows:rows + 64, h // 2, qt * P:(qt + 1) * P], kT[rows:rows + 64, h // 2, 0:n],
                                 start=True, stop=False)
                nc.tensor.matmul(dst[:, qt * P:n], ident_b, mask_b, start=False, stop=True).then_inc(s_mm, 1)

            def turn_probs(b, s):
                qt = s % NT
                if qt == NT - 1:
                    pe.wait_ge(s_norm_long, NH * b + (s // NT + 1))
                else:
                    pe.wait_ge(s_norm, (STEPS - NH) * b + (s - s // NT + 1))
                if s >= 2:
                    pe.wait_ge(s_keep, STEPS * b + (s - 1))
                for kt in range(qt + 1):
                    last = nc.tensor.transpose(bank[5 + s % 2][:, kt * P:(kt + 1) * P], probs[s % PROBS][:, kt * P:(kt + 1) * P], ident)
                last.then_inc(s_turn, 1)

            def replicate_v(b, n):
                if n >= 2:
                    pe.wait_ge(kv_done, UNITS * b + (n - 1))
                for i, part in enumerate((v_hi, v_mid, v_lo)):
                    last = nc.tensor.matmul(bank[n % 2][:, :], sel[:, n % HD, :], part[n // HD], start=(i == 0), stop=(i == 2))
                last.then_inc(vrep, 1)

            def reduce_state(b, g):
                pe.wait_ge(prod_done, UNITS * b + (4 * g + 4))
                if g == 4:
                    pe.wait_ge(y_read, 2 * b + 1)
                for q in range(4):
                    last = nc.tensor.matmul(bank[2][32 * q:32 * q + 32, :], red[:, g % 4, :], prods[(4 * g + q) % PRODS],
                                            start=(g % 4 == 0), stop=(g % 4 == 3))
                last.then_inc(red_mm, 1)

            def weigh_values(b, g):
                pe.wait_ge(s_keep, STEPS * b + 4 * NT * (g + 1))
                if g:
                    pe.wait_ge(y_out, 4 * b + g)
                for kt in range(NT):
                    for i in range(HGROUP):
                        h = HGROUP * g + i
                        last = nc.tensor.matmul(bank[7][32 * i:32 * i + 32, kt * P:T], v_tok[:, kt, h * ND:(h + 1) * ND],
                                                turned[i][:, kt, kt * P:T], start=(kt == 0), stop=(kt == NT - 1))
                last.then_inc(pv_mm, 1)

            def turn_head(b):
                pe.wait_ge(xn_done, b + 1)
                for k, name in enumerate((last_g, last_u)):
                    for i in range(NT):
                        last = nc.tensor.transpose(bank[post.bank(name)][:, i * P:(i + 1) * P], xn[:, i, k * P:(k + 1) * P], ident)
                    last.then_inc(xn_turned, 1)

            turn_head(0)
            pe.wait_ge(weights_in, 16 * NW)
            pe.wait_ge(ready_b, 4)
            pe.sem_inc(pv_mm, NH // HGROUP)
            with pe.Fori(0, B) as b:
                pe.wait_ge(a_read2, len(post.order["a"]) * b + 3)
                pe.wait_ge(v_read2, len(post.order["v"]) * b + 1)
                pe.wait_ge(lerp_done, b + 1)
                for name, at, n in (("rk", 0, 2), ("vg", 2, 2), ("d", 4, 1)):
                    product(b, "la_" + name, [(la_w[:, k, at * LORA:(at + n) * LORA], lerp[:, k, :]) for k in range(KD)],
                            rows=n * LORA)
                pe.wait_ge(a_read, pre.read(b, "la_d"))
                lora_b(b, "d", "d", th[2])
                pe.wait_ge(v_read2, len(post.order["v"]) * b + 3)
                lora_b(b, "r", "r", th[0])
                pe.wait_ge(mixed, 10 * b + 2)
                product(b, "la_dd", [(la_w[:, k, 4 * LORA:5 * LORA], mix[0][:, k, :]) for k in range(KD)], rows=LORA)
                lora_b(b, "k", "k", th[0])
                project(b, "r")
                lora_b(b, "v", "v", th[1])
                project(b, "k")
                lora_b(b, "g", "g", th[1])
                project(b, "v")
                pe.wait_ge(a_read, pre.read(b, "la_dd"))
                lora_b(b, "d", "w", th[2])
                project(b, "g")
                pe.wait_ge(xb_done, b + 1)
                for k in range(KD):
                    turn(bank[pre.bank(f"xb{k}")], lambda i: xb[:, i, k * P:(k + 1) * P], f"xb{k}", b, pre, pre_read, made)
                pe.wait_ge(v_read, pre.read(b, "xb0"))
                pe.wait_ge(a_read, pre.read(b, "xb1"))
                product(b, "ckv", [(kva_w[:, k, :], xbT[:, k, :]) for k in range(KD)], rows=ND + RD)
                for name in QKV:
                    i = int(name[-1])
                    if name == "k0":
                        pe.wait_ge(turned_q, 9 * b + 1)
                    if name[0] == "q":
                        product(b, name, [(q_w[:, k, i * P:(i + 1) * P], xbT[:, k, :]) for k in range(KD)])
                    elif name[0] == "k":
                        product(b, name, [(kbuild[0:64, i, :], ckvT[0:64, :])])
                    elif name[0] == "v":
                        product(b, name, [(ckvT[0:ND, i * P:(i + 1) * P], kvb_w[0:ND, :])])
                    else:
                        pe.wait_ge(ruk_done, 2 * b + 2)
                        product(b, name, [(spread, bonus[:, i, :])])
                pe.wait_ge(a_read, pre.read(b, pre.order["a"][-1]))
                pe.wait_ge(v_lo_done, 2 * b + 2)
                for s in range(STEPS + LAG + 2):
                    if s < STEPS:
                        scores(b, s)
                        if s % 2 == 0:
                            replicate_v(b, s // 2)
                    if s >= 16 + LAG and (s - LAG) % 16 == 0:
                        weigh_values(b, (s - LAG) // 16 - 1)
                    if LAG <= s < STEPS + LAG:
                        turn_probs(b, s - LAG)
                    if s >= 10 and (s - 10) % 8 == 0 and (s - 10) // 8 < 8:
                        reduce_state(b, (s - 10) // 8)
                def result(name, pairs, dst):
                    begin(b, name, post, post_read)
                    for n, (o, w, x, first, last_one) in enumerate(pairs):
                        last = nc.tensor.matmul(dst[o], w, x, start=first, stop=last_one)
                    last.then_inc(made2, 1)

                pe.wait_ge(y_out, 4 * b + 4)
                pe.wait_ge(y_read, 2 * b + 2)
                full = slice(None), slice(0, T)

                def head_means(m):
                    result(f"mean{m}", [(full, mean_m, y[:, m, :], True, True)], bank[post.bank(f"mean{m}")])

                head_means(0)

                def by_tokens(name, tiles, lhs, rhs, n):
                    result(name, [((slice(None), slice((i % 2) * D, (i % 2 + 1) * D)), lhs(i, c), rhs(c), c == 0, c == n - 1)
                                  for i in tiles for c in range(n)], bank[post.bank(name)])

                for half in range(2):
                    by_tokens(f"wo{half}", (2 * half, 2 * half + 1), lambda i, c: yT[c][:, i * P:(i + 1) * P],
                              lambda c: wo_w[:, c, :], NH // HGROUP)
                head_means(1)

                def head_vars(m):
                    pe.wait_ge(sq_done, 2 * b + (m + 1))
                    result(f"var{m}", [(full, mean_m, sq[:, m, :], True, True)], bank[post.bank(f"var{m}")])

                head_vars(0)
                pe.wait_ge(xc_done, b + 1)
                for k in range(KD):
                    turn(bank[post.bank(f"xc{k}")], lambda i: xb[:, i, k * P:(k + 1) * P], f"xc{k}", b, post, post_read, made2)
                head_vars(1)
                pe.wait_ge(v_read2, post.read(b, "xc0"))
                pe.wait_ge(a_read2, post.read(b, "xc1"))
                result("gate", [((slice(None), slice(i * ME, (i + 1) * ME)), xbT[:, k, i * P:(i + 1) * P], gate_w[:, k, :],
                                 k == 0, k == KD - 1) for i in range(NT) for k in range(KD)], bank[post.bank("gate")])

                def up(e):
                    for x, w in (("g", eg_w[e]), ("u", eu_w[e])):
                        result(f"{x}{e}", [(full, w[:, k, :], xbT[:, k, :], k == 0, k == KD - 1) for k in range(KD)],
                               bank[post.bank(f"{x}{e}")])

                def down(e):
                    pe.wait_ge(hid_done, post.read(b, f"u{e}"))
                    for half, name in enumerate("ab"):
                        by_tokens(f"d{e}{name}", (2 * half, 2 * half + 1), lambda i, c: hid[e % 2][:, i * P:(i + 1) * P],
                                  lambda c: ed_w[e], 1)

                pe.wait_ge(moe_in, 16 * 3 * (ME + 1))
                for e in range(ME + 2):
                    if e <= ME:
                        up(e)
                    else:
                        pe.wait_ge(a_read2, post.read(b, last_g))
                        pe.wait_ge(hid_done, post.read(b, last_u))
                        turn_head(b + 1)
                    if e:
                        down(e - 1)
                pe.wait_ge(o_done, 2 * b + 2)
                for half in range(2):
                    by_tokens(f"o{half}", (2 * half, 2 * half + 1), lambda i, c: y[:, c, i * P:(i + 1) * P],
                              lambda c: o_w[:, c, :], KD)

        @block.scalar
        def _(act):
            def square_head(b):
                act.wait_ge(xn_done, b + 1)
                for i in range(NT):
                    last = nc.scalar.activation(xb[:, i, :], xn[:, i, :], ACT.Square, accum_out=ssq[:, i:i + 1])
                last.then_inc(ssq_done, 1)

            def right_head(b):
                act.wait_ge(xn_turned, 2 * b + 2)
                nc.scalar.activation(xnT[:, 1, :], bank[post.bank(last_u)][:, :], ACT.Copy).then_inc(xnT_right, 1)

            square_head(0)
            right_head(0)
            act.sem_inc(a_read, 1)
            act.sem_inc(a_read2, 3)
            act.sem_inc(stored, 16)
            act.wait_ge(weights_in, 16 * NW)
            with act.Fori(0, B) as b:
                def take(name, dst, func, **kw):
                    act.wait_ge(made, pre.made(b, name))
                    rows = dst.shape[0]
                    return nc.scalar.activation(dst, bank[pre.bank(name)][0:rows, :], func, **kw)

                for n, name in enumerate(("rk", "vg")):
                    take("la_" + name, th[n], ACT.Tanh).then_inc(a_read, 1)
                take("la_d", th[2][0:LORA, :], ACT.Tanh).then_inc(a_read, 1)
                act.wait_ge(made, pre.made(b, "lb_d1"))
                take("la_dd", th[2][0:LORA, :], ACT.Tanh).then_inc(a_read, 1)
                act.wait_ge(out_ready, b + 1)
                nc.scalar.activation(x2, s_in, ACT.Copy).then_inc(x2_kept, 1)
                for x in "rkv":
                    for m in range(KD):
                        take(f"pr_{x}{m}", proj[x][:, m, :], ACT.Copy).then_inc(a_read, 1)
                    if x == "v":
                        for m in range(KD):
                            take(f"lb_w{m}", proj["w"][:, m, :], ACT.Exp, bias=VEC["ll_d"][:, m:m + 1]).then_inc(a_read, 1)
                            act.wait_ge(a_read, pre.read(b, f"lb_w{m}"))
                            nc.scalar.activation(proj["w"][:, m, :], proj["w"][:, m, :], ACT.Exp, scale=-1.0).then_inc(w_step, 1)
                for m in range(KD):
                    take(f"pr_g{m}", proj["g"][:, m, :], ACT.Copy).then_inc(a_read, 1)
                take("xb1", xbT[:, 1, :], ACT.Copy, scale=VEC["w_ln1"][:, 1:2]).then_inc(a_read, 1)
                for name in QKV:
                    i = int(name[-1])
                    if name[0] == "k":
                        take(name, kT[:, i, :], ACT.Copy, scale=0.125).then_inc(a_read, 1)
                    elif name[0] == "v":
                        take(name, v_tok[:, i, :], ACT.Copy).then_inc(a_read, 1)
                    if name in ("k0", "k1"):
                        act.wait_ge(a_read, pre.read(b, f"pr_v{i}"))
                        nc.scalar.activation(v_hi[i], proj["v"][:, i, :], ACT.Copy).then_inc(v_hi_done, 1)
                    if name in ("v0", "v2"):
                        m = i // 2
                        act.wait_ge(v_res_done, 2 * b + m + 1)
                        if m:
                            act.wait_ge(v_lo_done, 2 * b + 1)
                        nc.scalar.activation(v_mid[m], proj["v"][:, m, :], ACT.Copy).then_inc(v_mid_done, 1)

                def exp(s):
                    n = (s % NT + 1) * P
                    act.wait_ge(s_max, STEPS * b + (s + 1))
                    if s >= PROBS:
                        act.wait_ge(s_turn, STEPS * b + (s - PROBS + 1))
                    nc.scalar.activation(probs[s % PROBS][:, 0:n], bank[3 + s % 2][:, 0:n], ACT.Exp, bias=neg_max[:, s:s + 1],
                                         accum_out=row_sum[:, s:s + 1]).then_inc(s_exp, 1)

                def keep(s):
                    h, qt = s // NT, s % NT
                    act.wait_ge(s_turn, STEPS * b + (s + 1))
                    if h >= HGROUP and s % (HGROUP * NT) == 0:
                        act.wait_ge(pv_mm, 4 * b + h // HGROUP + 4)
                    nc.scalar.activation(turned[h % HGROUP][:, 0:qt + 1, qt * P:(qt + 1) * P],
                                         bank[5 + s % 2][:, 0:(qt + 1) * P].rearrange("p (k c) -> p k c", c=P),
                                         ACT.Copy).then_inc(s_keep, 1)

                act.wait_ge(x2_kept, b + 1)
                for s in range(STEPS + LAG + 2):
                    if s >= 16 + LAG + 1 and (s - LAG - 1) % 16 == 0:
                        g = (s - LAG - 1) // 16 - 1
                        act.wait_ge(pv_mm, 4 * b + g + 5)
                        nc.scalar.activation(yT[g], bank[7][:, :], ACT.Copy).then_inc(y_out, 1)
                    if LAG < s <= STEPS + LAG:
                        keep(s - LAG - 1)
                    if s < STEPS:
                        exp(s)
                    if s % NT == 0 and 0 < s <= STEPS:
                        act.wait_ge(s_inv, STEPS * b + s)
                        nc.scalar.activation(probs[(s - 1) % PROBS], probs[(s - 1) % PROBS], ACT.Copy,
                                             scale=row_inv[:, s - 1:s]).then_inc(s_norm_long, 1)

                def take2(name, dst, func, **kw):
                    act.wait_ge(made2, post.made(b, name))
                    return nc.scalar.activation(dst, bank[post.bank(name)][:, :], func, **kw)

                for half in range(2):
                    act.wait_ge(v_read2, post.read(b, f"wo{half}"))
                    for i in (2 * half, 2 * half + 1):
                        last = nc.scalar.activation(xb[:, i, :], xn[:, i, :], ACT.Square, accum_out=ssq[:, i:i + 1])
                last.then_inc(ssq2_done, 1)
                take2("xc1", xbT[:, 1, :], ACT.Copy, scale=VEC["w_ln2"][:, 1:2]).then_inc(a_read2, 1)
                for m in range(KD):
                    act.wait_ge(v_read2, post.read(b, f"var{m}"))
                    nc.scalar.activation(inv[:, m, :], inv[:, m, :], ACT.Sqrt).then_inc(inv_done, 1)
                for m in range(KD):
                    nc.scalar.activation(proj["g"][:, m, :], proj["g"][:, m, :], ACT.Silu).then_inc(gsilu, 1)
                act.wait_ge(comb_in, 2 * b + 2)
                nc.scalar.activation(routs[4], routs[4], ACT.Tanh, scale=0.5).then_inc(comb_out, 1)
                take2("g0", silu_g[0], ACT.Silu).then_inc(a_read2, 1)
                take2("g1", silu_g[1], ACT.Silu).then_inc(a_read2, 1)
                for e in range(2, ME + 1):
                    act.wait_ge(hid_done, post.read(b, f"u{e - 2}"))
                    take2(f"g{e}", silu_g[e % 2], ACT.Silu).then_inc(a_read2, 1)
                    if e == ME - 2:
                        square_head(b + 1)
                right_head(b + 1)
                act.wait_ge(v_read2, post.read(b, f"d{ME}b"))
                nc.scalar.activation(acc, acc, ACT.Silu).then_inc(f_done, 1)

        @block.vector
        def _(v):
            v.memset(kbuild[0:64, :, :], 0.0).then_inc(kb_step, 1)
            v.wait_ge(kb_step, 1)
            for h in range(HEADS_PER_TILE):
                v.tensor_copy(kbuild[ND:64, :, 64 * h + ND:64 * h + 64],
                              const[ND:64, ND:64].rearrange("p (o n) -> p o n", o=1).broadcast_to([RD, NH // 2, RD])).then_inc(ready_b, 1)
            v.sem_inc(v_read, 1)
            v.sem_inc(v_read2, 3)
            v.sem_inc(hid_done, 3)
            v.sem_inc(out_ready, 1)

            def head_gate(b):
                v.wait_ge(x_loaded, 32 * b + 32)
                v.wait_ge(g_loaded, 64 * b + 64)
                nc.vector.tensor_tensor(s_in, s_in, g_in, ALU.mult).then_inc(x2_step, 1)

            def head_sum(b):
                v.wait_ge(x2_step, 4 * b + 1)
                nc.vector.tensor_tensor(s_in, x_in, s_in, ALU.add).then_inc(x2_step, 1)

            def head_stats(b):
                v.wait_ge(x2_step, 4 * b + 2)
                for i in range(NT):
                    last = nc.vector.bn_stats(stats[:, i, :], s_in[:, i, :])
                last.then_inc(x2_step, 1)
                v.wait_ge(x2_step, 4 * b + 3)
                nc.vector.memset(var_eps, EPS)
                for i in range(NT):
                    last = nc.vector.bn_aggr(mv[:, i, :], stats[:, i, :])
                last.then_inc(x2_step, 1)
                v.wait_ge(x2_step, 4 * b + 4)
                nc.vector.tensor_scalar_add(var_eps, mv[:, :, 1], EPS).then_inc(var_done, 1)

            def head_norm(b):
                v.wait_ge(rstd_done, b + 1)
                for i in range(NT):
                    last = nc.vector.tensor_scalar(xn[:, i, :], s_in[:, i, :], mv[:, i, 0:1], rstd[:, i:i + 1], ALU.subtract, ALU.mult)
                last.then_inc(xn_done, 1)

            def head_rms(b):
                v.wait_ge(ssq_done, b + 1)
                nc.vector.tensor_scalar(ssq, ssq, 1.0 / D, EPS, ALU.mult, ALU.add).then_inc(ms_done, 1)
                v.wait_ge(rms_done, b + 1)
                for i in range(NT):
                    last = nc.vector.tensor_scalar_mul(xb[:, i, :], xn[:, i, :], rms[:, i:i + 1])
                last.then_inc(xb_done, 1)

            def head_lerp(b):
                v.wait_ge(xn_turned, 2 * b + 1)
                nc.vector.tensor_copy(xnT[:, 0, :], bank[post.bank(last_g)][:, :]).then_inc(xnT_left, 1)
                v.wait_ge(xnT_left, b + 1)
                v.wait_ge(xnT_right, b + 1)
                nc.vector.tensor_scalar_mul(dxT[:, :, 0:1], xnT[:, :, 0:1], -1.0).then_inc(dx_step, 1)
                nc.vector.tensor_tensor(dxT[:, :, 1:T], xnT[:, :, 0:T - 1], xnT[:, :, 1:T], ALU.subtract).then_inc(dx_step, 1)
                v.wait_ge(dx_step, 2 * b + 2)
                for k in range(KD):
                    last = nc.vector.scalar_tensor_tensor(lerp[:, k, :], dxT[:, k, :], VEC["xw"][:, k:k + 1], xnT[:, k, :],
                                                          ALU.mult, ALU.add)
                last.then_inc(lerp_done, 1)

            head_gate(0)
            head_sum(0)
            head_stats(0)
            head_norm(0)
            head_rms(0)
            v.wait_ge(weights_in, 16 * NW)
            v.tensor_copy(mask_b, mask).then_inc(ready_b, 1)
            v.tensor_copy(ident_b, const[:, 0:P]).then_inc(ready_b, 1)
            head_lerp(0)
            with v.Fori(0, B) as b:
                for n, x in enumerate(MIX_ORDER):
                    if x == "k":
                        v.wait_ge(made, pre.made(b, "la_dd"))
                    elif n >= 2:
                        v.wait_ge(made, pre.made(b, f"pr_{MIX_ORDER[n - 2]}1"))
                    for m in range(KD):
                        name = f"lb_{x}{m}"
                        v.wait_ge(made, pre.made(b, name))
                        nc.vector.scalar_tensor_tensor(mix[n % 2][:, m, :], bank[pre.bank(name)][:, :], VEC["ll_" + x][:, m:m + 1],
                                                       dxT[:, m, :], ALU.add, ALU.mult).then_inc(v_read, 1)
                v.wait_ge(made, pre.made(b, "xb0"))
                nc.vector.tensor_scalar_mul(xbT[:, 0, :], bank[pre.bank("xb0")][:, :], VEC["w_ln1"][:, 0:1]).then_inc(v_read, 1)
                swap = [i ^ 1 for i in range(32)]
                v.wait_ge(stored, 16 * b + 16)

                def rotate(n):
                    name, rows = ("ckv", 64) if n == 0 else (f"q{n - 1}", P)
                    dst = ckvT if n == 0 else qT[:, n - 1, :]
                    src = bank[pre.bank(name)]
                    v.wait_ge(made, pre.made(b, name))
                    if n >= 2:
                        v.wait_ge(turned_q, 9 * b + (n - 1))
                    nc.vector.tensor_tensor(dst[0:rows, :], src[0:rows, :], cos[0:rows, :], ALU.mult).then_inc(rope_step, 1)
                    nc.vector.stream_shuffle(shuf[n % 2][0:rows, :], src[0:rows, :], swap).then_inc(v_read, 1)

                def without_hi(m):
                    v.wait_ge(v_hi_done, 2 * b + m + 1)
                    v.wait_ge(v_read, pre.read(b, f"sp{m}"))
                    nc.vector.tensor_tensor(proj["v"][:, m, :], proj["v"][:, m, :], v_hi[m], ALU.subtract).then_inc(v_res_done, 1)

                def without_mid(m):
                    v.wait_ge(v_mid_done, 2 * b + m + 1)
                    nc.vector.tensor_tensor(v_lo[m], proj["v"][:, m, :], v_mid[m], ALU.subtract).then_inc(v_lo_done, 1)

                rotate(0)
                v.wait_ge(a_read, pre.read(b, "pr_k1"))
                for m in range(KD):
                    nc.vector.scalar_tensor_tensor(bonus[:, m, :], proj["r"][:, m, :], VEC["u"][:, m:m + 1], proj["k"][:, m, :],
                                                   ALU.mult, ALU.mult).then_inc(ruk_done, 1)
                for name in QKV:
                    m = int(name[-1])
                    if name[0] == "s":
                        v.wait_ge(made, pre.made(b, name))
                        v.wait_ge(a_read, pre.read(b, f"pr_v{m}"))
                        nc.vector.tensor_tensor(bonus[:, m, :], bank[pre.bank(name)][:, :], proj["v"][:, m, :], ALU.mult).then_inc(v_read, 1)
                    elif name[0] == "q":
                        rotate(m + 1)
                    if name in ("q3", "q5"):
                        without_hi(m // 2 - 1)
                    if name in ("q4", "q7"):
                        without_mid(m // 3 - 1)
                v.wait_ge(w_step, 2 * b + 2)

                def highest(s):
                    n = (s % NT + 1) * P
                    v.wait_ge(s_mm, STEPS * b + (s + 1))
                    nc.vector.tensor_reduce(neg_max[:, s:s + 1], bank[3 + s % 2][:, 0:n], X, ALU.max, negate=True).then_inc(s_max, 1)

                def invert(s):
                    v.wait_ge(s_exp, STEPS * b + (s + 1))
                    nc.vector.reciprocal(row_inv[:, s:s + 1], row_sum[:, s:s + 1]).then_inc(s_inv, 1)

                def outer(n):
                    v.wait_ge(vrep, UNITS * b + (n + 1))
                    if n:
                        v.wait_ge(scan_done, UNITS * b + n)
                    nc.vector.tensor_tensor(kv, bank[n % 2][:, :], proj["k"][:, n // HD, :], ALU.mult).then_inc(kv_done, 1)

                def scan(n):
                    m, j = n // HD, n % HD
                    v.wait_ge(kv_done, UNITS * b + (n + 1))
                    if n >= 2:
                        v.wait_ge(prod_done, UNITS * b + (n - 1))
                    nc.vector.tensor_tensor_scan(state[n % 2][:, 1:T + 1], proj["w"][:, m, :], kv,
                                                 VEC["init"][:, m * HD + j:m * HD + j + 1], ALU.mult, ALU.add).then_inc(scan_done, 1)

                def read_out(m):
                    v.wait_ge(red_mm, 8 * b + (4 * m + 4))
                    nc.vector.tensor_tensor(y[:, m, :], bank[2][:, :], bonus[:, m, :], ALU.add).then_inc(y_read, 1)

                for s in range(STEPS + LAG + 2):
                    if s < STEPS:
                        highest(s)
                    if 1 <= s <= STEPS:
                        invert(s - 1)
                    if s < STEPS:
                        outer(s // 2) if s % 2 == 0 else scan(s // 2)
                    if s in (35, 67):
                        read_out((s - 35) // 32)

                def center(m):
                    v.wait_ge(made2, post.made(b, f"mean{m}"))
                    nc.vector.tensor_tensor(y[:, m, :], y[:, m, :], bank[post.bank(f"mean{m}")][:, :], ALU.subtract).then_inc(v_read2, 1)

                center(0)
                for half in range(2):
                    v.wait_ge(made2, post.made(b, f"wo{half}"))
                    nc.vector.tensor_tensor(xn[:, 2 * half:2 * half + 2, :], xn[:, 2 * half:2 * half + 2, :],
                                            bank[post.bank(f"wo{half}")][:, :].rearrange("p (i d) -> p i d", i=2), ALU.add).then_inc(v_read2, 1)
                center(1)
                v.wait_ge(ssq2_done, b + 1)
                nc.vector.tensor_scalar(ssq, ssq, 1.0 / D, EPS, ALU.mult, ALU.add).then_inc(ms2_done, 1)
                v.wait_ge(rms2_done, b + 1)
                for i in range(NT):
                    last = nc.vector.tensor_scalar_mul(xb[:, i, :], xn[:, i, :], rms[:, i:i + 1])
                last.then_inc(xc_done, 1)

                def head_var(m):
                    v.wait_ge(made2, post.made(b, f"var{m}"))
                    nc.vector.tensor_scalar_add(inv[:, m, :], bank[post.bank(f"var{m}")][:, :], EPS).then_inc(v_read2, 1)

                head_var(0)
                v.wait_ge(made2, post.made(b, "xc0"))
                nc.vector.tensor_scalar_mul(xbT[:, 0, :], bank[post.bank("xc0")][:, :], VEC["w_ln2"][:, 0:1]).then_inc(v_read2, 1)
                head_var(1)
                iota = const[:, CONST["iota"][0]:CONST["iota"][0] + ME].rearrange("p (o e) -> p o e", o=1).broadcast_to([P, NT, ME])

                def wide(t):
                    return t.rearrange("p (t o) -> p t o", o=1).broadcast_to([P, NT, ME])

                v.wait_ge(made2, post.made(b, "gate"))
                bias = gate_b.rearrange("p (o e) -> p o e", o=1).broadcast_to([P, NT, ME])
                nc.vector.tensor_tensor(logits, bank[post.bank("gate")][:, 0:NT * ME].rearrange("p (t e) -> p t e", e=ME), bias,
                                        ALU.add).then_inc(v_read2, 1)
                v.wait_ge(v_read2, post.read(b, "gate"))
                tstep = Steps(10 * b)
                best, where = (routs[0], routs[1]), (routs[2], routs[3])
                for n in range(2):
                    hot = route[n]
                    nc.vector.tensor_reduce(best[n], logits, X, ALU.max).then_inc(top_step, 1)
                    v.wait_ge(top_step, tstep.next())
                    nc.vector.tensor_tensor(hot, logits, wide(best[n]), ALU.is_ge).then_inc(top_step, 1)
                    v.wait_ge(top_step, tstep.next())
                    nc.vector.scalar_tensor_tensor(hot, hot, -float(ME), iota, ALU.mult, ALU.add).then_inc(top_step, 1)
                    v.wait_ge(top_step, tstep.next())
                    nc.vector.tensor_reduce(where[n], hot, X, ALU.min).then_inc(top_step, 1)
                    v.wait_ge(top_step, tstep.next())
                    nc.vector.tensor_tensor(hot, hot, wide(where[n]), ALU.is_equal).then_inc(top_step, 1)
                    v.wait_ge(top_step, tstep.next())
                    if n == 0:
                        nc.vector.scalar_tensor_tensor(logits, hot, -3.0e38, logits, ALU.mult, ALU.add).then_inc(comb_in, 1)
                        v.wait_ge(comb_in, 2 * b + 1)
                nc.vector.tensor_tensor(routs[4], best[0], best[1], ALU.subtract).then_inc(comb_in, 1)
                v.wait_ge(comb_out, b + 1)
                nc.vector.tensor_scalar(routs[5], routs[4], -0.5, 0.5, ALU.mult, ALU.add).then_inc(comb_done, 1)
                nc.vector.tensor_scalar(routs[4], routs[4], 0.5, 0.5, ALU.mult, ALU.add).then_inc(comb_done, 1)
                v.wait_ge(comb_done, 5 * b + 2)
                nc.vector.tensor_tensor(route[0], route[0], wide(routs[4]), ALU.mult).then_inc(comb_done, 1)
                nc.vector.tensor_tensor(route[1], route[1], wide(routs[5]), ALU.mult).then_inc(comb_done, 1)
                v.wait_ge(comb_done, 5 * b + 4)
                nc.vector.tensor_tensor(route[2], route[0], route[1], ALU.add).then_inc(comb_done, 1)
                v.wait_ge(comb_done, 5 * b + 5)

                def hidden(e):
                    v.wait_ge(a_read2, post.read(b, f"g{e}"))
                    v.wait_ge(made2, post.made(b, f"u{e}"))
                    nc.vector.tensor_tensor(hid[e % 2], silu_g[e % 2], bank[post.bank(f"u{e}")][:, :], ALU.mult).then_inc(hid_done, 1)

                def ln_inv(m):
                    v.wait_ge(inv_done, 2 * b + m + 1)
                    nc.vector.reciprocal(inv[:, m, :], inv[:, m, :]).then_inc(ln_step, 1)

                def ln_scale(m):
                    v.wait_ge(ln_step, 6 * b + 3 * m + 1)
                    nc.vector.tensor_tensor(y[:, m, :], y[:, m, :], inv[:, m, :], ALU.mult).then_inc(ln_step, 1)

                def ln_affine(m):
                    v.wait_ge(ln_step, 6 * b + 3 * m + 2)
                    nc.vector.tensor_scalar(y[:, m, :], y[:, m, :], VEC["ln_w"], VEC["ln_b"], ALU.mult, ALU.add).then_inc(ln_step, 1)

                def ln_gate(m):
                    v.wait_ge(ln_step, 6 * b + 3 * m + 3)
                    v.wait_ge(gsilu, 2 * b + m + 1)
                    nc.vector.tensor_tensor(y[:, m, :], y[:, m, :], proj["g"][:, m, :], ALU.mult).then_inc(o_done, 1)

                def between(e):
                    for n, part in enumerate((ln_inv, ln_scale, ln_affine, ln_gate)):
                        if e == n:
                            part(0)
                        if e == 4 + n:
                            part(1)
                    for at, part in ((1, head_gate), (2, head_sum), (3, head_stats), (5, head_norm), (6, head_rms), (7, head_lerp)):
                        if e == at:
                            part(b + 1)

                hidden(0)
                for e in range(ME + 1):
                    if e < ME:
                        hidden(e + 1)
                    for half, name in enumerate("ab"):
                        v.wait_ge(made2, post.made(b, f"d{e}{name}"))
                        if e:
                            v.wait_ge(v_read2, post.read(b, f"d{e - 1}{name}"))
                        for i in (2 * half, 2 * half + 1):
                            src = bank[post.bank(f"d{e}{name}")][:, (i % 2) * D:(i % 2 + 1) * D]
                            weight = route[2][:, i, e:e + 1] if e < ME else 1.0
                            base = xn[:, i, :] if e == 0 else acc[:, i, :]
                            last = nc.vector.scalar_tensor_tensor(acc[:, i, :], src, weight, base, ALU.mult, ALU.add)
                        last.then_inc(v_read2, 1)
                    between(e)
                v.wait_ge(f_done, b + 1)
                for half in range(2):
                    v.wait_ge(made2, post.made(b, f"o{half}"))
                    nc.vector.tensor_tensor(acc[:, 2 * half:2 * half + 2, :], acc[:, 2 * half:2 * half + 2, :],
                                            bank[post.bank(f"o{half}")][:, :].rearrange("p (i d) -> p i d", i=2), ALU.mult).then_inc(v_read2, 1)
                v.wait_ge(v_read2, post.read(b, "o1"))
                v.wait_ge(x2_kept, b + 1)
                nc.vector.tensor_tensor(acc, x2, acc, ALU.add).then_inc(out_ready, 1)

        @block.gpsimd
        def _(g):
            g.memset(neg_half, -0.5).then_inc(pool_set, 1)
            g.wait_ge(pool_set, 1)

            def gather(b):
                nc.gpsimd.tensor_copy(idx, pos_all[:, bass.ds(b * NT, NT)]).then_inc(idx_set, 1)
                g.wait_ge(idx_set, b + 1)
                nc.gpsimd.tensor_tensor(waste, neg_half, neg_half, ALU.mult)
                for i in range(NT):
                    g.indirect_dma_start(out=g_in[:, i, :], out_offset=None, in_=dram["g"][:, :],
                                         in_offset=bass.IndirectOffsetOnAxis(ap=idx[:, i:i + 1], axis=0)).then_inc(g_loaded, 16)

            def head(b):
                g.wait_ge(var_done, b + 1)
                nc.gpsimd.tensor_tensor(rstd, var_eps, neg_half, ALU.pow).then_inc(rstd_done, 1)
                g.wait_ge(ms_done, b + 1)
                nc.gpsimd.tensor_tensor(rms, ssq, neg_half, ALU.pow).then_inc(rms_done, 1)

            gather(0)
            head(0)
            g.wait_ge(weights_in, 16 * NW)
            with g.Fori(0, B) as b:
                for n, x in enumerate(MIX_ORDER):
                    for m in range(KD):
                        g.wait_ge(v_read, pre.read(b, f"lb_{x}{m}"))
                        nc.gpsimd.tensor_tensor(mix[n % 2][:, m, :], mix[n % 2][:, m, :], xnT[:, m, :], ALU.add).then_inc(mixed, 1)
                for n in range(1 + NH // 2):
                    name, rows = ("ckv", 64) if n == 0 else (f"q{n - 1}", P)
                    dst = ckvT if n == 0 else qT[:, n - 1, :]
                    g.wait_ge(v_read, pre.read(b, name))
                    nc.gpsimd.tensor_tensor(shuf[n % 2][0:rows, :], shuf[n % 2][0:rows, :], sin[0:rows, :], ALU.mult).then_inc(rope_mul, 1)
                    g.wait_ge(rope_mul, 9 * b + (n + 1))
                    nc.gpsimd.tensor_tensor(dst[0:rows, :], dst[0:rows, :], shuf[n % 2][0:rows, :], ALU.add).then_inc(turned_q, 1)

                def norm(s):
                    n = (s % NT + 1) * P
                    g.wait_ge(s_inv, STEPS * b + (s + 1))
                    nc.gpsimd.tensor_tensor(probs[s % PROBS][:, 0:n], probs[s % PROBS][:, 0:n],
                                            row_inv[:, s:s + 1].broadcast_to([P, n]), ALU.mult).then_inc(s_norm, 1)

                def product(n):
                    m, j = n // HD, n % HD
                    nc.gpsimd.tensor_copy(state[n % 2][:, 0:1], VEC["init"][:, m * HD + j:m * HD + j + 1]).then_inc(init_set, 1)
                    g.wait_ge(init_set, UNITS * b + (n + 1))
                    g.wait_ge(scan_done, UNITS * b + (n + 1))
                    if n >= PRODS:
                        g.wait_ge(red_mm, 8 * b + (n - PRODS) // 4 + 1)
                    nc.gpsimd.tensor_tensor(prods[n % PRODS], state[n % 2][:, 0:T], proj["r"][:, m, :], ALU.mult).then_inc(prod_done, 1)

                for s in range(1, STEPS + 2):
                    if s <= STEPS and s % NT:
                        norm(s - 1)
                    if s >= 2 and s % 2 == 0:
                        product(s // 2 - 1)
                for m in range(KD):
                    g.wait_ge(v_read2, post.read(b, f"mean{m}"))
                    nc.gpsimd.tensor_tensor(sq[:, m, :], y[:, m, :], y[:, m, :], ALU.mult).then_inc(sq_done, 1)
                g.wait_ge(ms2_done, b + 1)
                nc.gpsimd.tensor_tensor(rms, ssq, neg_half, ALU.pow).then_inc(rms2_done, 1)
                g.wait_ge(pv_mm, 4 * b + 4 + 4)
                gather(b + 1)
                head(b + 1)
            g.wait_ge(g_loaded, 64 * (B + 1))


IN_NAMES = ["L0_attn_h", "L0_attn_W0", "L0_attn_W1", "centT", "W1T", "W2T", "const",
            "gammaT", "betaT", "b1T", "b2row", "vecs", "laT", "lbT", "rWT", "kWT", "vWT", "gWT", "oWT", "Wo", "gate_b",
            "L1_ffn_Wq", "L1_ffn_Wkva", "L1_ffn_Wkvb", "L1_ffn_Wgate", "L1_ffn_Wg", "L1_ffn_Wu", "L1_ffn_Wd",
            "L1_ffn_sWg", "L1_ffn_sWu", "L1_ffn_sWd"]


def build(nc, io, out):
    with ExitStack() as ctx:
        def scratch(name, shape):
            return nc.dram_tensor(name, shape, F32, kind="Internal").ap()

        dram = {"sorted": scratch("sorted_rows", (6 * (B - 1) * P, ROW)),
                "g": scratch("gate_rows", (SLOTS * P, D)),
                "s": scratch("s_rows", (B * T, D))}
        arena = ctx.enter_context(nc.sbuf_tensor("arena", [P, 53200], F32))
        bank = [ctx.enter_context(nc.psum_tensor(f"bank{i}", [P, 512], F32)) for i in range(8)]
        ffn_loaded = ctx.enter_context(nc.semaphore("ffn_loaded"))
        mem = Arena(arena)
        const = mem.take(NCONST_A)
        pos_all = mem.take(TILES + NT).bitcast(U32)
        after_pos = mem.at
        tile_expert = mem.take(SLOTS).bitcast(I32)
        w_at = mem.at
        w1s = mem.take(E * KD * F)
        w2s = mem.take(E * FC * D)
        assert 6 * (B - 1) >= SLOTS + 1
        spare = Arena(arena, w_at + (E - 1) * KD * F)
        phase_a(nc, io, dram, Arena(arena, mem.at), spare, const, bank, w1s, w2s, pos_all, tile_expert, ffn_loaded)
        free = Arena(arena, mem.at)
        top_at = arena.shape[1] - SECOND
        top = Arena(arena, top_at)
        second, loads = second_weights(top, io)
        weights_in = ctx.enter_context(nc.semaphore("weights_in"))
        phase_b(nc, io, dram, free, const, bank, w1s, w2s, tile_expert, ffn_loaded, loads, weights_in)
        assert free.at <= top_at
        low = Arena(arena, after_pos)
        phase_c(nc, io, dram, low, const, bank, pos_all, second, len(loads), weights_in, out)
        assert low.at <= top_at


def kernel(**inputs):
    import concourse.bacc as bacc
    from concourse.bass_utils import run_bass_kernel_spmd

    a = {k: np.asarray(x) for k, x in inputs.items()}
    a["centT"] = a["L0_ffn_centroids"].T
    a["W1T"] = a["L0_ffn_W1"].transpose(0, 2, 1).reshape(E * D, F)
    a["W2T"] = a["L0_ffn_W2"].transpose(0, 2, 1).reshape(E * F, D)
    for name, key in (("gammaT", "L0_ffn_gamma"), ("betaT", "L0_ffn_beta"), ("b1T", "L0_ffn_b1")):
        a[name] = a[key].reshape(-1, P).T
    a["b2row"] = a["L0_ffn_b2"].reshape(1, -1)
    order = np.zeros(P, np.int64)
    for h in range(HG):
        for j in range(HD):
            order[rho(h, j)] = h * HD + j
    both = np.concatenate([order, P + order])
    for x in "rkvg":
        w = a[f"L1_attn_{x}W"].T
        a[x + "WT"] = w[:, both] if x in "vg" else w
    a["oWT"] = a["L1_attn_oW"].T[both]
    a["laT"] = np.concatenate([a[f"L1_attn_{x}_la"].T for x in "rkvgd"], axis=1)
    a["lbT"] = np.concatenate([a[f"L1_attn_{x}_lb"].T for x in "rkvgd"] + [np.zeros((LORA, D), np.float32)])

    def columns(x):
        return x.reshape(KD, P, -1).transpose(1, 0, 2).reshape(P, -1)

    a["vecs"] = np.concatenate(
        [columns(a[f"L1_attn_{x}_ll"]) for x in "rkvgd"] + [columns(a["L1_attn_xw"]), columns(a["L1_attn_u"]),
         columns(a["L1_attn_init_state"].reshape(D, HD)), a["L1_attn_ln_w"][order % HD][:, None],
         a["L1_attn_ln_b"][order % HD][:, None], columns(a["L1_ffn_w_ln1"]), columns(a["L1_ffn_w_ln2"])], axis=1)
    a["Wo"] = a["L1_ffn_Wo"].reshape(NH, 64, D)[:, :ND].reshape(NH * ND, D)
    a["gate_b"] = a["L1_ffn_expert_bias"].reshape(1, ME)
    a["const"] = constants()
    nc = bacc.Bacc("TRN2", target_bir_lowering=False, num_devices=1)
    arrays, io = {}, {}
    for name in IN_NAMES:
        arrays["in_" + name] = np.ascontiguousarray(a[name])
        io[name] = nc.dram_tensor("in_" + name, arrays["in_" + name].shape, F32, kind="ExternalInput").ap()
    out = nc.dram_tensor("out_0", (B, T, D), F32, kind="ExternalOutput").ap()
    build(nc, io, out)
    r = run_bass_kernel_spmd(nc, [arrays], core_ids=[0])
    return r.results[0]["out_0"]
```
